# Optimizing a Trainium2 kernel written in Bass

```python
import numpy as np
import jax
import jax.numpy as jnp

def _softmax(x, axis=-1):
    return jax.nn.softmax(x, axis=axis)

def _gelu(x):
    return jax.nn.gelu(x, approximate=True)

def _silu(x):
    return jax.nn.silu(x)

def _sigmoid(x):
    return jax.nn.sigmoid(x)

def _layernorm(x, axis=-1, eps=1e-05):
    m = jnp.mean(x, axis=axis, keepdims=True)
    v = jnp.var(x, axis=axis, keepdims=True)
    return (x - m) / jnp.sqrt(v + eps)

def _scatter_add(tgt, idx, src, axis=0):
    return tgt.at[idx].add(src)

def _segment_sum(src, seg, n):
    return jax.ops.segment_sum(src, seg, n)
kernel_name = 'mk_hybrid_d1_jaxref_r8_33b194'

def setup_inputs(seed: int=0):
    np.random.seed(seed)
    _w = jnp.asarray

    def _L0_attn_a_setup():
        import jax, jax.numpy as jnp
        import numpy as np
        B, N, D = (4, 256, 128)
        H, HD = (8, 64)
        FF = 512
        ETA = 0.1
        DT = 0.01
        GAMMA_FLOOR = 0.1
        EPS = 1e-05

        def layernorm(x, g, b):
            m = jnp.mean(x, -1, keepdims=True)
            v = jnp.var(x, -1, keepdims=True)
            return (x - m) * jax.lax.rsqrt(v + EPS) * g + b

        def _cf_scan(d):
            dT = jnp.swapaxes(d, 0, 1)

            def step(c, di):
                a = di - 1.0 / c
                return (a, a)
            _, rest = jax.lax.scan(step, dT[0], dT[1:])
            return jnp.swapaxes(jnp.concatenate([dT[:1], rest], 0), 0, 1)

        def bk_core_diag(V, gamma):
            d = jax.lax.complex(V + 2.0, -gamma)
            a = _cf_scan(d)
            b = _cf_scan(d[:, ::-1])[:, ::-1]
            G = 1.0 / (a + b - d)
            return jnp.stack([G.real, G.imag], axis=-1)

        def hebbian_scan(q, k, v, gamma):
            qT = jnp.transpose(q, (1, 0, 2, 3))
            kT = jnp.transpose(k, (1, 0, 2, 3))
            vT = jnp.transpose(v, (1, 0, 2, 3))
            gT = jnp.swapaxes(gamma, 0, 1)
            W0 = jnp.zeros((q.shape[0], H, HD, HD), dtype=q.dtype)

            def step(W, inp):
                q_t, k_t, v_t, g_t = inp
                decay = jnp.exp(-g_t * DT)[:, None, None, None]
                W = decay * W + ETA * (k_t[..., :, None] * v_t[..., None, :])
                o = jnp.einsum('bhd,bhde->bhe', q_t, W)
                return (W, o)
            _, outs = jax.lax.scan(step, W0, (qT, kT, vT, gT))
            return jnp.transpose(outs, (1, 0, 2, 3)).reshape(q.shape[0], q.shape[1], H * HD)
        key = jax.random.key(seed)
        ks = jax.random.split(key, 12)
        s = lambda fan: 1.0 / np.sqrt(fan)
        return {'x': jax.random.normal(ks[0], (B, N, D), jnp.float32), 'ln1_g': jnp.ones((D,), jnp.float32), 'ln1_b': jnp.zeros((D,), jnp.float32), 'ln2_g': jnp.ones((D,), jnp.float32), 'ln2_b': jnp.zeros((D,), jnp.float32), 'ln3_g': jnp.ones((D,), jnp.float32), 'ln3_b': jnp.zeros((D,), jnp.float32), 'w_pot': jax.random.normal(ks[1], (D, 2), jnp.float32) * s(D), 'b_pot': jnp.zeros((2,), jnp.float32), 'w_bk': jax.random.normal(ks[2], (2, D), jnp.float32) * s(2), 'b_bk': jnp.zeros((D,), jnp.float32), 'w_qkv': jax.random.normal(ks[3], (D, 3 * H * HD), jnp.float32) * s(D), 'b_qkv': jnp.zeros((3 * H * HD,), jnp.float32), 'w_out': jax.random.normal(ks[4], (H * HD, D), jnp.float32) * s(H * HD), 'b_out': jnp.zeros((D,), jnp.float32), 'w_ff1': jax.random.normal(ks[5], (D, FF), jnp.float32) * s(D), 'b_ff1': jnp.zeros((FF,), jnp.float32), 'w_ff2': jax.random.normal(ks[6], (FF, D), jnp.float32) * s(FF), 'b_ff2': jnp.zeros((D,), jnp.float32)}
    _L0_attn_a_in = _L0_attn_a_setup()

    def _L0_attn_b_setup():
        import jax, jax.numpy as jnp
        import numpy as np
        EPS = 1e-08

        def _gated_scan(dt, ut):
            a = 1.0 - dt
            b = dt * ut

            def combine(c1, c2):
                a1, b1 = c1
                a2, b2 = c2
                return (a2 * a1, a2 * b1 + b2)
            _, h = jax.lax.associative_scan(combine, (a, b), axis=1)
            return h
        key = jax.random.key(seed)
        ks = jax.random.split(key, 6)
        B, L, D, S = (4, 1024, 128, 64)
        sc = lambda fan_in: 1.0 / np.sqrt(fan_in)
        return {'x': jax.random.normal(ks[0], (B, L, D), dtype=jnp.float32), 'norm_w': jnp.ones((D,), dtype=jnp.float32), 'W_in': jax.random.normal(ks[1], (D, 3 * S), dtype=jnp.float32) * sc(D), 'b_in': jnp.zeros((3 * S,), dtype=jnp.float32), 'W_x': jax.random.normal(ks[2], (S, S), dtype=jnp.float32) * sc(S), 'b_x': jnp.zeros((S,), dtype=jnp.float32), 'W_dt': jax.random.normal(ks[3], (S, S), dtype=jnp.float32) * sc(S), 'b_dt': jnp.zeros((S,), dtype=jnp.float32), 'W_out': jax.random.normal(ks[4], (S, D), dtype=jnp.float32) * sc(S), 'b_out': jnp.zeros((D,), dtype=jnp.float32)}
    _L0_attn_b_in = _L0_attn_b_setup()

    def _L0_ffn_setup():
        import jax, jax.numpy as jnp
        import numpy as np
        E = 8
        K = 2
        D = 128
        P = 512
        key = jax.random.key(seed)
        ks = jax.random.split(key, 8)
        s = lambda fan_in: 1.0 / np.sqrt(fan_in)
        x = jax.random.normal(ks[0], (2, 256, D), dtype=jnp.float32)
        W1 = jax.random.normal(ks[1], (E, D, P), dtype=jnp.float32) * s(D)
        b1 = jax.random.normal(ks[2], (E, P), dtype=jnp.float32) * 0.01
        W2 = jax.random.normal(ks[3], (E, P, D), dtype=jnp.float32) * s(P)
        b2 = jax.random.normal(ks[4], (E, D), dtype=jnp.float32) * 0.01
        Wr = jax.random.normal(ks[5], (D, E), dtype=jnp.float32) * s(D)
        br = jax.random.normal(ks[6], (E,), dtype=jnp.float32) * 0.01
        return {'x': x, 'W1': W1, 'b1': b1, 'W2': W2, 'b2': b2, 'Wr': Wr, 'br': br}
    _L0_ffn_in = _L0_ffn_setup()
    _d = {'L0_attn_a_x': _L0_attn_a_in['x'], 'L0_attn_a_ln1_g': _L0_attn_a_in['ln1_g'], 'L0_attn_a_ln1_b': _L0_attn_a_in['ln1_b'], 'L0_attn_a_ln2_g': _L0_attn_a_in['ln2_g'], 'L0_attn_a_ln2_b': _L0_attn_a_in['ln2_b'], 'L0_attn_a_ln3_g': _L0_attn_a_in['ln3_g'], 'L0_attn_a_ln3_b': _L0_attn_a_in['ln3_b'], 'L0_attn_a_w_pot': _L0_attn_a_in['w_pot'], 'L0_attn_a_b_pot': _L0_attn_a_in['b_pot'], 'L0_attn_a_w_bk': _L0_attn_a_in['w_bk'], 'L0_attn_a_b_bk': _L0_attn_a_in['b_bk'], 'L0_attn_a_w_qkv': _L0_attn_a_in['w_qkv'], 'L0_attn_a_b_qkv': _L0_attn_a_in['b_qkv'], 'L0_attn_a_w_out': _L0_attn_a_in['w_out'], 'L0_attn_a_b_out': _L0_attn_a_in['b_out'], 'L0_attn_a_w_ff1': _L0_attn_a_in['w_ff1'], 'L0_attn_a_b_ff1': _L0_attn_a_in['b_ff1'], 'L0_attn_a_w_ff2': _L0_attn_a_in['w_ff2'], 'L0_attn_a_b_ff2': _L0_attn_a_in['b_ff2'], 'L0_attn_b_norm_w': _L0_attn_b_in['norm_w'], 'L0_attn_b_W_in': _L0_attn_b_in['W_in'], 'L0_attn_b_b_in': _L0_attn_b_in['b_in'], 'L0_attn_b_W_x': _L0_attn_b_in['W_x'], 'L0_attn_b_b_x': _L0_attn_b_in['b_x'], 'L0_attn_b_W_dt': _L0_attn_b_in['W_dt'], 'L0_attn_b_b_dt': _L0_attn_b_in['b_dt'], 'L0_attn_b_W_out': _L0_attn_b_in['W_out'], 'L0_attn_b_b_out': _L0_attn_b_in['b_out'], 'L0_ffn_W1': _L0_ffn_in['W1'], 'L0_ffn_b1': _L0_ffn_in['b1'], 'L0_ffn_W2': _L0_ffn_in['W2'], 'L0_ffn_b2': _L0_ffn_in['b2'], 'L0_ffn_Wr': _L0_ffn_in['Wr'], 'L0_ffn_br': _L0_ffn_in['br']}
    _x0 = _d['L0_attn_a_x']
    _d['L0_attn_a_x'] = jax.random.normal(jax.random.fold_in(jax.random.key(seed), 1), (8, 512, 128), dtype=_x0.dtype)
    del _x0
    return _d

def reference(L0_attn_a_x, L0_attn_a_ln1_g, L0_attn_a_ln1_b, L0_attn_a_ln2_g, L0_attn_a_ln2_b, L0_attn_a_ln3_g, L0_attn_a_ln3_b, L0_attn_a_w_pot, L0_attn_a_b_pot, L0_attn_a_w_bk, L0_attn_a_b_bk, L0_attn_a_w_qkv, L0_attn_a_b_qkv, L0_attn_a_w_out, L0_attn_a_b_out, L0_attn_a_w_ff1, L0_attn_a_b_ff1, L0_attn_a_w_ff2, L0_attn_a_b_ff2, L0_attn_b_norm_w, L0_attn_b_W_in, L0_attn_b_b_in, L0_attn_b_W_x, L0_attn_b_b_x, L0_attn_b_W_dt, L0_attn_b_b_dt, L0_attn_b_W_out, L0_attn_b_b_out, L0_ffn_W1, L0_ffn_b1, L0_ffn_W2, L0_ffn_b2, L0_ffn_Wr, L0_ffn_br):

    def _L0_attn_a_ref(x, ln1_g, ln1_b, ln2_g, ln2_b, ln3_g, ln3_b, w_pot, b_pot, w_bk, b_bk, w_qkv, b_qkv, w_out, b_out, w_ff1, b_ff1, w_ff2, b_ff2):
        import jax, jax.numpy as jnp
        import numpy as np
        B, N, D = (4, 256, 128)
        H, HD = (8, 64)
        FF = 512
        ETA = 0.1
        DT = 0.01
        GAMMA_FLOOR = 0.1
        EPS = 1e-05

        def layernorm(x, g, b):
            m = jnp.mean(x, -1, keepdims=True)
            v = jnp.var(x, -1, keepdims=True)
            return (x - m) * jax.lax.rsqrt(v + EPS) * g + b

        def _cf_scan(d):
            dT = jnp.swapaxes(d, 0, 1)

            def step(c, di):
                a = di - 1.0 / c
                return (a, a)
            _, rest = jax.lax.scan(step, dT[0], dT[1:])
            return jnp.swapaxes(jnp.concatenate([dT[:1], rest], 0), 0, 1)

        def bk_core_diag(V, gamma):
            d = jax.lax.complex(V + 2.0, -gamma)
            a = _cf_scan(d)
            b = _cf_scan(d[:, ::-1])[:, ::-1]
            G = 1.0 / (a + b - d)
            return jnp.stack([G.real, G.imag], axis=-1)

        def hebbian_scan(q, k, v, gamma):
            qT = jnp.transpose(q, (1, 0, 2, 3))
            kT = jnp.transpose(k, (1, 0, 2, 3))
            vT = jnp.transpose(v, (1, 0, 2, 3))
            gT = jnp.swapaxes(gamma, 0, 1)
            W0 = jnp.zeros((q.shape[0], H, HD, HD), dtype=q.dtype)

            def step(W, inp):
                q_t, k_t, v_t, g_t = inp
                decay = jnp.exp(-g_t * DT)[:, None, None, None]
                W = decay * W + ETA * (k_t[..., :, None] * v_t[..., None, :])
                o = jnp.einsum('bhd,bhde->bhe', q_t, W)
                return (W, o)
            _, outs = jax.lax.scan(step, W0, (qT, kT, vT, gT))
            return jnp.transpose(outs, (1, 0, 2, 3)).reshape(q.shape[0], q.shape[1], H * HD)
        b, n, d = x.shape
        xn1 = layernorm(x, ln1_g, ln1_b)
        pot = xn1 @ w_pot + b_pot
        V = pot[..., 0]
        gamma = jax.nn.softplus(pot[..., 1]) + GAMMA_FLOOR
        bk_features = bk_core_diag(V, gamma)
        x = x + bk_features @ w_bk + b_bk
        xn2 = layernorm(x, ln2_g, ln2_b)
        qkv = (xn2 @ w_qkv + b_qkv).reshape(b, n, 3, H, HD)
        q, k, v = (qkv[:, :, 0], qkv[:, :, 1], qkv[:, :, 2])
        heb = hebbian_scan(q, k, v, gamma)
        x = x + heb @ w_out + b_out
        xn3 = layernorm(x, ln3_g, ln3_b)
        x = x + jax.nn.gelu(xn3 @ w_ff1 + b_ff1) @ w_ff2 + b_ff2
        return x

    def _L0_attn_b_ref(x, norm_w, W_in, b_in, W_x, b_x, W_dt, b_dt, W_out, b_out):
        import jax, jax.numpy as jnp
        import numpy as np
        EPS = 1e-08

        def _gated_scan(dt, ut):
            a = 1.0 - dt
            b = dt * ut

            def combine(c1, c2):
                a1, b1 = c1
                a2, b2 = c2
                return (a2 * a1, a2 * b1 + b2)
            _, h = jax.lax.associative_scan(combine, (a, b), axis=1)
            return h
        residual = x
        xn = x * jax.lax.rsqrt(jnp.mean(x * x, axis=-1, keepdims=True) + EPS) * norm_w
        p = jnp.einsum('bld,df->blf', xn, W_in) + b_in
        u, z, g = jnp.split(p, 3, axis=-1)
        ut = jnp.tanh(jnp.einsum('bls,st->blt', u, W_x) + b_x)
        dt = jax.nn.sigmoid(jnp.einsum('bls,st->blt', z, W_dt) + b_dt)
        h = _gated_scan(dt, ut)
        y = h * jax.nn.sigmoid(g)
        out = jnp.einsum('bls,sd->bld', y, W_out) + b_out
        return residual + out

    def _L0_ffn_ref(x, W1, b1, W2, b2, Wr, br):
        import jax, jax.numpy as jnp
        import numpy as np
        E = 8
        K = 2
        D = 128
        P = 512
        B, S, _ = x.shape
        xf = x.reshape(B * S, D)
        scores = xf @ Wr + br
        _, top_idx = jax.lax.top_k(scores, K)
        mask = jax.nn.one_hot(top_idx, E, dtype=scores.dtype).sum(-2) > 0
        router_weights = jax.nn.softmax(jnp.where(mask, scores, -jnp.inf), axis=-1)
        h = jax.nn.gelu(jnp.einsum('td,edp->etp', xf, W1) + b1[:, None, :])
        y = jnp.einsum('etp,epd->etd', h, W2) + b2[:, None, :]
        out = jnp.einsum('te,etd->td', router_weights, y)
        return out.reshape(B, S, D)
    x = L0_attn_a_x
    x = x + _L0_attn_a_ref(_layernorm(x, axis=-1), L0_attn_a_ln1_g, L0_attn_a_ln1_b, L0_attn_a_ln2_g, L0_attn_a_ln2_b, L0_attn_a_ln3_g, L0_attn_a_ln3_b, L0_attn_a_w_pot, L0_attn_a_b_pot, L0_attn_a_w_bk, L0_attn_a_b_bk, L0_attn_a_w_qkv, L0_attn_a_b_qkv, L0_attn_a_w_out, L0_attn_a_b_out, L0_attn_a_w_ff1, L0_attn_a_b_ff1, L0_attn_a_w_ff2, L0_attn_a_b_ff2)
    x = x + _L0_ffn_ref(_layernorm(x, axis=-1), L0_ffn_W1, L0_ffn_b1, L0_ffn_W2, L0_ffn_b2, L0_ffn_Wr, L0_ffn_br)
    x = x + _L0_attn_b_ref(_layernorm(x, axis=-1), L0_attn_b_norm_w, L0_attn_b_W_in, L0_attn_b_b_in, L0_attn_b_W_x, L0_attn_b_b_x, L0_attn_b_W_dt, L0_attn_b_b_dt, L0_attn_b_W_out, L0_attn_b_b_out)
    x = x + _L0_ffn_ref(_layernorm(x, axis=-1), L0_ffn_W1, L0_ffn_b1, L0_ffn_W2, L0_ffn_b2, L0_ffn_Wr, L0_ffn_br)
    return x

_drawn_inputs = setup_inputs


def setup_inputs(seed=0):
    import zlib

    import numpy as np

    out = dict(_drawn_inputs(seed))
    spreads = {'L0_attn_a_ln1_g': (1.0, 0.2),
     'L0_attn_a_ln1_b': (0.0, 0.1),
     'L0_attn_a_ln2_g': (1.0, 0.2),
     'L0_attn_a_ln2_b': (0.0, 0.1),
     'L0_attn_a_ln3_g': (1.0, 0.6),
     'L0_attn_a_ln3_b': (0.0, 0.8),
     'L0_attn_a_b_pot': (0.0, 0.672),
     'L0_attn_a_b_bk': (0.0, 0.1),
     'L0_attn_a_b_qkv': (0.0, 0.1),
     'L0_attn_a_b_out': (0.0, 0.8),
     'L0_attn_a_b_ff1': (0.0, 0.8),
     'L0_attn_a_b_ff2': (0.0, 0.8),
     'L0_attn_b_norm_w': (1.0, 0.6),
     'L0_attn_b_b_in': (0.0, 0.8),
     'L0_attn_b_b_x': (0.0, 2.0),
     'L0_attn_b_b_dt': (0.0, 2.0),
     'L0_attn_b_b_out': (0.0, 0.8)}
    factors = {'L0_attn_b_W_in': 3.578,
     'L0_attn_b_W_x': 3.624,
     'L0_attn_b_W_dt': 8.0,
     'L0_attn_b_W_out': 3.702,
     'L0_ffn_b1': 64.0,
     'L0_ffn_b2': 53.377,
     'L0_ffn_br': 35.311}
    for name, (base, spread) in spreads.items():
        noise = np.random.default_rng([zlib.crc32(name.encode()), seed]).standard_normal(out[name].shape)
        drawn = base * np.exp(spread * noise) if base else spread * noise
        out[name] = jnp.asarray(drawn.astype(out[name].dtype))
    for name, factor in factors.items():
        out[name] = (out[name] * factor).astype(out[name].dtype)
    return out
```

```python
from contextlib import ExitStack

import concourse.bass as bass
from concourse import mybir

F32 = mybir.dt.float32
I32 = mybir.dt.int32
ALU = mybir.AluOpType
ACT = mybir.ActivationFunctionType
X_AXIS = mybir.AxisListType.X

B, N, D = 8, 512, 128
P = 128
TPS = N // P
NT = B * TPS
H, HD = 8, 64
PAIRS = H // 2
FF = 512
FC = FF // P
ETA, DT, GAMMA_FLOOR, EPS = 0.1, 0.01, 0.1, 1e-5
RMS_EPS = 1e-8
S = 64
E_N = 8
CH = 32
NC = N // CH
SEG = CH // 2
TT = 256
TH = TT // P
CAP = B * N + TT
MAX_TILES = 2 * B * N // TT + E_N - 1
MIN_TILES = 2 * B * N // TT
ROW = 132
ROWS_X = E_N * CAP + (MAX_TILES - MIN_TILES) * TT
NOWHERE = 1 << 20
NEG_BIG = -3e38

CONST_W = dict(ident=P, ones=P, before=P, mask=P, rev=E_N, ebase=E_N, kthr=16, jj=MAX_TILES)
COLS_W = dict(w_pot=2, g1=1, b1=1, g2=1, b2=1, g3=1, b3=1, bq=PAIRS, bk=PAIRS, bff1=FC, norm_w=1,
              b_uz=1, b_g=1, b_x=1, b_dt=1, b_pot=1)
ROWS_W = dict(bk=H * HD, bv=H * HD, b_out=D, b_ff2=D, b_outb=D, br=E_N)
WTS_W = dict(q=H * HD, k=H * HD, v=H * HD, w_out=PAIRS * D, ff1=FF, ff2=FC * D, w_in=3 * S, w_xdt=S, w_outb=D, wr=E_N)
EXP_W = dict(w1=FF, w2=FC * D, b1=FC)


def offsets(widths):
    at, out = 0, {}
    for name, w in widths.items():
        out[name] = (at, at + w)
        at += w
    return out, at


CONST_AT, CONST_N = offsets(CONST_W)
COLS_AT, COLS_N = offsets(COLS_W)
ROWS_AT, ROWS_N = offsets(ROWS_W)
WTS_AT, WTS_N = offsets(WTS_W)
EXP_AT, EXP_N = offsets(EXP_W)


WORK = 22000
PARAM_LOADS = 6
PER_A, PER_R, PER_G = 2 * 31, 2 * 38, 35
AHEAD = 4
TILES_OF = [len(range(q, MAX_TILES, AHEAD)) for q in range(AHEAD)]
RETURNS = [len(range(q, MAX_TILES, 2)) * TH * 16 for q in range(2)]


class Turn:

    def __init__(self, k, n=None, unroll=2):
        self.k, self.n, self.unroll = k, n, unroll

    def at(self, d):
        return Turn(self.k + d, self.n, self.unroll)

    @property
    def par(self):
        return self.k % 2

    @property
    def quad(self):
        return self.k % AHEAD

    def count(self, each=1, more=0):
        if self.n is None:
            return each * self.k + more
        return self.n * (self.unroll * each) + (each * self.k + more)

    def part(self, of, each=1, more=0):
        if self.n is None:
            return each * (self.k // of) + more
        return self.n * (self.unroll // of * each) + (each * (self.k // of) + more)

    def half(self, each=1, more=0):
        return self.part(2, each, more)


class Link:

    def __init__(self, eng, sem):
        self.eng, self.sem, self.base, self.k = eng, sem, 0, 0

    def mark(self, ins):
        ins.then_inc(self.sem, 1)
        self.k += 1

    def sync(self):
        self.eng.wait_ge(self.sem, self.base + self.k)

    def __call__(self, ins):
        self.mark(ins)
        self.sync()

    def enter(self, n, per, first):
        self.start, self.per = self.base + self.k, per
        self.base, self.k = n * per + (self.start - first * per), 0

    def leave(self, passes):
        assert self.k == self.per, f"a pass adds {self.k}, not {self.per}"
        self.base, self.k = self.start + passes * self.per, 0


def hybrid_kernel(nc, x_in, consts, ids_in, tail_in, cols_in, rows_in, wts_in, wbk_in, experts_in, eb2_in, out):
    def dram(name, shape, dt=F32):
        return nc.dram_tensor(name, shape, dt, kind="Internal").ap()

    pot_d = dram("pot_d", (2, B * N))
    gamma_d = dram("gamma_d", (B * N,))
    csum_d = dram("csum_d", (B * N,))
    maps_d = dram("maps_d", (2, B, NC, 16))
    states_d = dram("states_d", (2, B, NC, 4))
    green_d = dram("green_d", (2, B * N))
    routed_d = dram("routed_d", (ROWS_X, ROW))
    back_d = dram("back_d", (2 * B * N, D))

    with ExitStack() as ctx:
        def sb(name, shape, dt=F32):
            return ctx.enter_context(nc.sbuf_tensor(name, shape, dt))

        def sem(name):
            return ctx.enter_context(nc.semaphore(name))

        cst = sb("cst", [P, CONST_N])
        ids = sb("ids", [P, NT, 2], I32)
        tail = sb("tail", [P, TH, ROW], I32)
        cols = sb("cols", [P, COLS_N])
        rows = sb("rows", [P, ROWS_N])
        wts = sb("wts", [P, WTS_N])
        wbk = sb("wbk", [3, D])

        def C(name):
            a, b = CONST_AT[name]
            return cst[:, a:b]

        def col(name, i=0):
            a, _ = COLS_AT[name]
            return cols[:, a + i:a + i + 1]

        def row(name):
            a, b = ROWS_AT[name]
            return rows[:, a:b]

        def W(name, a=0, b=None):
            lo, hi = WTS_AT[name]
            return wts[:, lo + a:hi if b is None else lo + b]

        ident = C("ident")

        X = sb("X", [P, NT, D])
        decays = sb("decays", [P, B * N])
        dmat = sb("dmat", [P, B * N])
        decC = sb("decC", [P, NT])
        sm = sb("sm", [P, 10, NT])
        powc = sb("powc", [P, NT])
        gt = [sb(f"gt{q}", [3, N]) for q in range(2)]
        x2 = [sb(f"x2{q}", [P, TPS, D]) for q in range(2)]
        x2b = [sb(f"x2b{q}", [P, TPS, D]) for q in range(2)]
        xh = [sb(f"xh{q}", [P, TPS, D]) for q in range(2)]
        xnT = [sb(f"xnT{q}", [P, N]) for q in range(2)]
        xres, x3, x3h = (sb(n, [P, TPS, D]) for n in ("xres", "x3", "x3h"))
        x3T = sb("x3T", [P, N])
        stat, stat3 = sb("stat", [P, TPS, 6]), sb("stat3", [P, TPS, 6])
        mv, mv3 = sb("mv", [P, TPS, 2]), sb("mv3", [P, TPS, 2])
        ve, ve3 = sb("ve", [P, TPS]), sb("ve3", [P, TPS])
        rs, rs3 = sb("rs", [P, TPS]), sb("rs3", [P, TPS])
        rms = sb("rms", [P, 3, TPS])
        pay = [sb(f"pay{q}", [P, TPS, 2, ROW]) for q in range(2)]
        wtok = sb("wtok", [P, 2, NT])
        cnt = sb("cnt", [P, TPS + 1, E_N])

        pool = sb("work", [P, WORK])
        used = [0]

        def carve(*shape, dt=F32):
            n = 1
            for s in shape:
                n *= s
            a = used[0]
            used[0] = a + n
            assert used[0] <= WORK, used[0]
            v = pool[:, a:a + n]
            if dt is not F32:
                v = v.bitcast(dt)
            names = " ".join("abcde"[:len(shape)])
            return v.rearrange(f"p ({names}) -> p {names}", **dict(zip("abcde", shape))) if len(shape) > 1 else v

        st1 = carve(NT, 6)
        cf = carve(6, CH)
        dre, dim2 = carve(CH, 2), carve(CH, 2, 2)
        pseq = carve(2, SEG + 2, 8)
        cstep, cnrm = carve(2, 8), carve(2, 2)
        cmap, cstate, cneg = carve(2, 16), carve(2, 4), carve(2, 4)
        cmap16, cst16, cprod16, cnrm16 = carve(NC, 16), carve(NC + 1, 4), carve(16), carve(2, NC)
        pval = carve(4, 2 * (SEG + 2))
        cw = carve(10, 2, CH)
        green = carve(2, CH)
        gw, potT, potb = carve(2), carve(B * N), carve(1)
        csr, csr2, csT = carve(P), carve(P), carve(NT)
        used[0] = 0
        qT, kT, qd = carve(PAIRS, N), carve(PAIRS, N), carve(PAIRS, N)
        ktok, vtok, vdec = carve(TPS, H * HD), carve(TPS, H * HD), carve(TPS, H * HD)
        pT = [[carve(PAIRS, P) for _ in range(2)] for _ in range(2)]
        wst = [carve(PAIRS, P) for _ in range(TPS - 1)]
        hebT, hff = carve(PAIRS, N), carve(FC, N)
        used[0] = 0
        rt, rv = carve(12, TPS, E_N), carve(6, TPS)
        rsl = carve(2, TPS)
        slots = [carve(2, TPS, dt=I32) for _ in range(2)]
        tl, tlk, tlj, tlr = carve(4, E_N), carve(E_N, 16), carve(MAX_TILES, E_N), carve(4, MAX_TILES)
        tile_e, tile_row, tail_row = carve(MAX_TILES, dt=I32), carve(MAX_TILES, dt=I32), carve(E_N, dt=I32)
        ewt = [carve(EXP_N) for _ in range(4)]
        eb2 = [carve(D) for _ in range(4)]
        ex = [carve(TH, ROW) for _ in range(4)]
        exT = [carve(TT) for _ in range(2)]
        ehT = [carve(FC, TT) for _ in range(2)]
        ey = [carve(TH, D) for _ in range(2)]
        yb = [[carve(TPS, D) for _ in range(2)] for _ in range(2)]
        gstat, gmv, gr = carve(2, TPS, 6), carve(2, TPS, 2), carve(4, 2, TPS)
        uz = [carve(N) for _ in range(2)]
        sg, ut, dtm, am, bm, hm, ym = (carve(N) for _ in range(7))

        psb = [ctx.enter_context(nc.psum_tensor(f"ps{i}", [P, 512], F32)) for i in range(8)]
        ps_t, ps_p, ps_s, ps_h, ps_u, ps_o = psb[0], psb[1:3], psb[3:5], psb[5], psb[6], psb[7]

        class Sems(dict):
            def __missing__(self, name):
                self[name] = sem(name)
                return self[name]

        s = Sems()

        def started(value):
            return not isinstance(value, int) or value > 0

        def apart(eng):
            eng.sem_inc(s["passed"], 1)

        def pairs_of(eng, body, items, first=2, link=None, per=0, shift=0):
            for k in range(first):
                body(Turn(k), Turn(k + shift))
            with eng.Fori(first // 2, items // 2) as n:
                if link:
                    link.enter(n, per, first // 2)
                for u in range(2):
                    body(Turn(u, n), Turn(u + shift, n))
            if link:
                link.leave(items // 2 - first // 2)

        def route_loop(eng, item, ts, link=None, per=0):
            for k in range(2):
                item(Turn(k), Turn(ts + k))
            with eng.Fori(1, B // 2 - 1) as n:
                if link:
                    link.enter(n, per, 1)
                for u in range(2):
                    item(Turn(u, n), Turn(ts + u, n))
            if link:
                link.leave(B // 2 - 2)
            item(Turn(B - 2), Turn(ts + B - 2))
            item(Turn(B - 1), Turn(ts + B - 1), last=True)

        def tile_loop(eng, body, layer, ahead=None, behind=None, peel=2):
            def step(k, n=None, first=False, last=False):
                j = Turn(k, n, AHEAD)
                js = j.at(layer * MAX_TILES)
                body(j, js)
                if behind and not first:
                    behind(j.at(-1), js.at(-1))
                if ahead and not last:
                    ahead(j.at(1), js.at(1))

            if ahead:
                ahead(Turn(0), Turn(layer * MAX_TILES))
            for k in range(peel):
                step(k, first=(k == 0))
            passes = (MAX_TILES - peel) // AHEAD
            with eng.Fori(0, passes) as n:
                for u in range(AHEAD):
                    step(peel + u, n)
            for k in range(peel + passes * AHEAD, MAX_TILES):
                step(k, last=(k == MAX_TILES - 1))
            if behind:
                behind(Turn(MAX_TILES - 1), Turn((layer + 1) * MAX_TILES - 1))

        def loads(j, layer, each):
            return j.part(AHEAD, each, each * (1 + layer * TILES_OF[j.quad]))

        block = ctx.enter_context(nc.Block())

        def tiles(t):
            return bass.ds(t.count(TPS), TPS)

        def tile_at(t, j):
            return bass.ds(t.count(TPS, j), 1)

        def t_order(ap):
            return ap.rearrange("d (p j) -> d j p", j=TPS)

        @block.sync
        def _(sp):
            for b in range(B):
                sp.dma_start(X[:, b * TPS:(b + 1) * TPS, :], x_in[b]).then_inc(s["x_loaded"], 16)

            sp.wait_ge(s["pot_ready"], B)
            sp.dma_start(pot_d, potT[0:2, :]).then_inc(s["pot_stored"], 16)
            sp.wait_ge(s["pot_stored"], 16)
            sp.dma_start(cf[:, 0:2, :], pot_d.rearrange("k (p i) -> p k i", i=CH)).then_inc(s["pot_chunked"], 16)
            sp.wait_ge(s["gamma_ready"], 1)
            sp.dma_start(gamma_d.rearrange("(p i) -> p i", i=CH), cf[:, 5, :]).then_inc(s["gamma_stored"], 16)
            sp.wait_ge(s["gamma_stored"], 16)
            sp.dma_start(csr[0:NT, :], gamma_d.rearrange("(c i) -> c i", i=P)).then_inc(s["csr_loaded"], 16)
            sp.wait_ge(s["csum_ready"], 1)
            sp.dma_start(csum_d.rearrange("(c i) -> c i", i=P), csr2[0:NT, :]).then_inc(s["csum_stored"], 16)
            sp.wait_ge(s["csum_stored"], 16)
            sp.dma_start(decays[:, :], csum_d.rearrange("(a n) -> a n", a=1).to_broadcast([P, B * N]))\
                .then_inc(s["csum_spread"], 16)
            sp.wait_ge(s["maps_ready"], 1)
            sp.dma_start(maps_d.rearrange("r b k m -> (b k) r m"), cmap[:, :, :]).then_inc(s["maps_stored"], 16)
            sp.wait_ge(s["maps_stored"], 16)
            sp.dma_start(cmap16[0:B], maps_d[0]).then_inc(s["maps_loaded"], 16)
            sp.dma_start(cmap16[B:2 * B, ::-1, :], maps_d[1]).then_inc(s["maps_loaded"], 16)
            sp.wait_ge(s["states_ready"], 1)
            sp.dma_start(states_d[0], cst16[0:B, 0:NC, :]).then_inc(s["states_stored"], 16)
            sp.dma_start(states_d[1], cst16[B:2 * B, NC - 1::-1, :]).then_inc(s["states_stored"], 16)
            sp.wait_ge(s["states_stored"], 32)
            sp.dma_start(cstate[:, :, :], states_d.rearrange("r b k m -> (b k) r m")).then_inc(s["states_loaded"], 16)
            sp.wait_ge(s["green_ready"], 1)
            sp.dma_start(green_d.rearrange("k (p i) -> p k i", i=CH), green).then_inc(s["green_stored"], 16)
            sp.wait_ge(s["green_stored"], 16)
            def load_green(t):
                if started(v := t.count(1, -1)):
                    sp.wait_ge(s["bk_mm"], v)
                src = green_d[:, bass.ds(t.count(N), N)]
                sp.dma_start(gt[t.par][0:2, :], src).then_inc(s[f"gt_loaded{t.par}"], 16)

            sp.wait_ge(s["ones_set"], 2)
            load_green(Turn(0))
            load_green(Turn(1))
            with sp.Fori(0, (B - 2) // 2) as n:
                for u in range(2):
                    load_green(Turn(2 + u, n))
            sp.wait_ge(s["params_loaded"], 16 * PARAM_LOADS)
            for k in range(MAX_TILES - MIN_TILES):
                at = E_N * CAP + k * TT
                sp.dma_start(routed_d[at:at + TT, :].rearrange("(h p) r -> p h r", p=P), tail[:, :, :].bitcast(F32))\
                    .then_inc(s["spare_filled"], 16)

            def expert_tiles(layer):
                sp.wait_ge(s["tables_ready"], layer + 1)
                for q in range(2):
                    sp.wait_ge(s[f"scattered{q}"], (layer + 1) * NT * 16)
                for e in range(E_N):
                    at = sp.value_load(tail_row[0:1, e:e + 1], min_val=e * CAP, max_val=e * CAP + B * N)
                    sp.dma_start(routed_d[bass.ds(at, TT), :].rearrange("(h p) r -> p h r", p=P), tail[:, :, :].bitcast(F32))\
                        .then_inc(s["tails_filled"], 16)
                sp.wait_ge(s["tails_filled"], (layer + 1) * E_N * 16)
                sp.wait_ge(s["spare_filled"], (MAX_TILES - MIN_TILES) * 16)

                def load(j, js):
                    q = j.quad
                    e = sp.value_load(tile_e[0:1, bass.ds(j.count(), 1)], min_val=0, max_val=E_N - 1)
                    r = sp.value_load(tile_row[0:1, bass.ds(j.count(), 1)], min_val=0, max_val=ROWS_X - TT)
                    if started(v := js.count(1, -3)):
                        sp.wait_ge(s["y_mm"], v)
                    apart(sp)
                    if started(v := 1 + js.count(1, -3)):
                        sp.wait_ge(s["ey_ready"], v)
                    apart(sp)
                    if started(v := j.half(32, layer * RETURNS[q % 2] - 32)):
                        sp.wait_ge(s[f"returned{q % 2}"], v)
                    apart(sp)
                    sp.dma_start(ex[q][:, :, :], routed_d[bass.ds(r, TT), :].rearrange("(h p) r -> p h r", p=P))\
                        .then_inc(s[f"ex_loaded{q}"], 16)
                    sp.dma_start(ewt[q][:, :], experts_in[bass.ds(e, 1)].rearrange("a p c -> (a p) c")).then_inc(s[f"ewt_loaded{q}"], 16)
                    sp.dma_start(eb2[q][:, :], eb2_in[bass.ds(e, 1), :].to_broadcast([P, D])).then_inc(s[f"ewt_loaded{q}"], 16)

                tile_loop(sp, load, layer, peel=4)
                for q in range(2):
                    sp.wait_ge(s[f"returned{q}"], (layer + 1) * RETURNS[q])

                def load_back(t, ts):
                    q = t.par
                    if started(v := ts.count(1, -1)):
                        sp.wait_ge(s["combined"], v)
                    apart(sp)
                    for k in range(2):
                        src = back_d[bass.ds(t.count(N, k * B * N), N), :].rearrange("(p j) d -> p j d", j=TPS)
                        sp.dma_start(yb[q][k], src).then_inc(s[f"back_loaded{q}"], 16)

                pairs_of(sp, load_back, B, shift=layer * B)

            expert_tiles(0)
            expert_tiles(1)

            def store(t, _):
                sp.wait_ge(s["combined"], t.count(1, B + 1))
                apart(sp)
                sp.dma_start(out[bass.ds(t.count(), 1)].rearrange("a p j d -> (a p) j d"), X[:, tiles(t), :])\
                    .then_inc(s["stored"], 16)

            pairs_of(sp, store, B)
            sp.wait_ge(s["stored"], 16 * B)

        @block.gpsimd
        def _(pool):
            for name in ("xres_ready",):
                pool.sem_inc(s[name], 1)
            pool.memset(powc[:, :], -0.5).then_inc(s["powc_set"], 1)
            for q in range(2):
                pool.memset(gt[q][:, :], 1.0).then_inc(s["ones_set"], 1)
                pool.memset(pay[q][:, :, :, :], 0.0).then_inc(s["pay_set"], 1)
            pool.wait_ge(s["powc_set"], 1)
            v, t, ra, rb, rab = sm[:, 2, :], sm[:, 3, :], sm[:, 4, :], sm[:, 5, :], sm[:, 6, :]
            link = Link(pool, s["pool_order"])
            pool.wait_ge(s["var_ready"], 1)
            link(pool.tensor_scalar(t, v, EPS, None, ALU.add))
            link(pool.tensor_tensor(ra, t, powc[:, :], ALU.pow))
            link(pool.tensor_tensor(t, ra, ra, ALU.mult))
            link(pool.tensor_tensor(t, t, v, ALU.mult))
            link(pool.tensor_scalar(t, t, EPS, None, ALU.add))
            link(pool.tensor_tensor(rb, t, powc[:, :], ALU.pow))
            pool.tensor_tensor(rab, ra, rb, ALU.mult).then_inc(s["rab_ready"], 1)
            pool.wait_ge(s["csT_ready"], 1)
            pool.wait_ge(s["csum_spread"], 16)
            for c in range(NT):
                pool.tensor_scalar(dmat[:, c * P:(c + 1) * P], decays[:, c * P:(c + 1) * P], csT[:, c:c + 1], None,
                                   ALU.max).then_inc(s["dmax_ready"], 1)
            for m in range(TPS - 1):
                pool.memset(wst[m], 0.0)
            pool.wait_ge(s["dexp_ready"], NT)
            for b in range(B):
                seq = dmat[:, b * N:(b + 1) * N].rearrange("p (c t) -> p c t", t=P)
                pool.tensor_tensor(seq, seq, C("mask").unsqueeze(1).to_broadcast([P, TPS, P]), ALU.mult)\
                    .then_inc(s["dmat_ready"], 1)
            def rstd(var, tmp, dst, ready):
                apart(pool)
                link(pool.tensor_scalar(tmp, var, EPS, None, ALU.add))
                pool.tensor_tensor(dst, tmp, powc[:, 0:TPS], ALU.pow).then_inc(s[ready], 1)

            def prepare(t):
                pool.wait_ge(s["mv_ready"], t.count(1, 1))
                rstd(mv[:, :, 1], ve[:, :], rs[:, :], "rs_ready")
                pool.wait_ge(s["x2_ready"], t.count(1, 1))
                if started(v := t.count(1, -1)):
                    pool.wait_ge(s["x3_ready"], v)
                pool.tensor_tensor(x2b[t.par][:, :, :], x2[t.par][:, :, :],
                                   row("b_out").unsqueeze(1).to_broadcast([P, TPS, D]), ALU.add).then_inc(s["x2b_ready"], 1)

            def finish_norm(t):
                pool.wait_ge(s["mv3_ready"], t.count(1, 1))
                rstd(mv3[:, :, 1], ve3[:, :], rs3[:, :], "rs3_ready")

            def finish_residual(t):
                pool.wait_ge(s["x1_ready"], 1 + t.count())
                apart(pool)
                link(pool.tensor_tensor(xres[:, :, :], x3[:, :, :], X[:, tiles(t), :], ALU.add))
                pool.tensor_tensor(xres[:, :, :], xres[:, :, :], row("b_ff2").unsqueeze(1).to_broadcast([P, TPS, D]),
                                   ALU.add).then_inc(s["xres_ready"], 1)

            def scale_heads(t):
                for p in range(PAIRS):
                    pool.wait_ge(s["qk_ready"], t.count(2 * PAIRS, 2 * p + 1))
                    apart(pool)
                    pool.tensor_tensor(qd[:, p, :], qT[:, p, :], decays[:, bass.ds(t.count(N), N)], ALU.mult)\
                        .then_inc(s["qd_ready"], 1)
                for m in range(TPS):
                    pool.wait_ge(s["tok_ready"], t.count(2 * TPS, 2 * m + 2))
                    apart(pool)
                    pool.tensor_tensor(vdec[:, m, :], vtok[:, m, :], decC[:, tile_at(t, m)].to_broadcast([P, H * HD]), ALU.mult)\
                        .then_inc(s["vdec_ready"], 1)

            def a_item(t, first=False, last=False):
                if not last:
                    prepare(t.at(1))
                if not first:
                    finish_norm(t.at(-1))
                    finish_residual(t.at(-1))
                scale_heads(t)

            pool.wait_ge(s["decC_ready"], 1)
            prepare(Turn(0))
            a_item(Turn(0), first=True)
            with pool.Fori(0, (B - 2) // 2) as n:
                link.enter(n, 6, 0)
                for u in range(2):
                    a_item(Turn(1 + u, n))
            link.leave((B - 2) // 2)
            a_item(Turn(B - 1), last=True)
            finish_norm(Turn(B - 1))
            finish_residual(Turn(B - 1))
            def route_norm(ts):
                pool.wait_ge(s["rmv_ready"], ts.count(1, 1))
                rstd(mv3[:, :, 1], ve3[:, :], rs3[:, :], "rrs_ready")

            def route_rows(ts):
                q = ts.par
                pool.wait_ge(s["slots_ready"], ts.count(1, 1))
                pool.wait_ge(s["pay2_ready"], ts.count(1, 1))
                apart(pool)
                for j in range(TPS):
                    for k in range(2):
                        pool.indirect_dma_start(routed_d, bass.IndirectOffsetOnAxis(ap=slots[q][:, k, j:j + 1], axis=0),
                                                pay[q][:, j, k, :], None).then_inc(s[f"scattered{q}"], 16)

            def route_item(t, ts, last=False):
                if not last:
                    route_norm(ts.at(1))
                route_rows(ts)

            def experts(layer):
                ts = layer * B
                pool.wait_ge(s["x_final"], layer + 1)
                route_norm(Turn(ts))
                route_loop(pool, route_item, ts, link, 2)

                def give_back(j, js):
                    q = j.par
                    pool.wait_ge(s["ey_ready"], 1 + js.count(1, 1))
                    apart(pool)
                    for h in range(TH):
                        pool.indirect_dma_start(back_d, bass.IndirectOffsetOnAxis(ap=ex[j.quad][:, h, D:D + 1].bitcast(I32), axis=0),
                                                ey[q][:, h, :], None, bounds_check=2 * B * N - 1, oob_is_err=False)\
                            .then_inc(s[f"returned{j.par}"], 16)

                tile_loop(pool, give_back, layer)

            experts(0)

            def scan_norm(t):
                pool.wait_ge(s["gmv_ready"], t.half(1, 1))
                apart(pool)
                v, a, r = gmv[:, :, :, 1], gr[:, 0], gr[:, 1]
                power = powc[:, 0:2 * TPS].rearrange("p (q j) -> p q j", q=2)
                link(pool.tensor_scalar(a, v, EPS, None, ALU.add))
                link(pool.tensor_tensor(r, a, power, ALU.pow))
                link(pool.tensor_tensor(a, r, r, ALU.mult))
                link(pool.tensor_tensor(a, a, v, ALU.mult))
                apart(pool)
                link(pool.tensor_scalar(a, a, RMS_EPS, None, ALU.add))
                pool.tensor_tensor(gr[:, 2], a, power, ALU.pow).then_inc(s["grs_ready"], 1)

            def scan_residual(t):
                at = X[:, tiles(t), :]
                pool.wait_ge(s["gxh_ready"], t.count(1, 1))
                apart(pool)
                link(pool.tensor_tensor(at, at, x2[t.par][:, :, :], ALU.add))
                apart(pool)
                pool.tensor_tensor(at, at, row("b_outb").unsqueeze(1).to_broadcast([P, TPS, D]), ALU.add).then_inc(s["gres_ready"], 1)

            def scan_pass(n, last=False):
                if not last:
                    scan_norm(Turn(2, n))
                for q in range(2):
                    scan_residual(Turn(q, n))

            scan_norm(Turn(0))
            with pool.Fori(0, B // 2 - 1) as n:
                link.enter(n, 7, 0)
                scan_pass(n)
            link.leave(B // 2 - 1)
            for q in range(2):
                scan_residual(Turn(B - 2 + q))
            experts(1)

        @block.scalar
        def _(act):
            for name in ("ff_ready", "x3T_ready",):
                act.sem_inc(s[name], 1)
            for dst, src in ((cols, cols_in), (cst, consts), (rows, rows_in.to_broadcast([P, ROWS_N])), (wbk, wbk_in),
                             (ids, ids_in), (tail, tail_in)):
                full = tuple(slice(None) for _ in dst.shape)
                act.dma_start(dst[full], src).then_inc(s["params_loaded"], 16)
            act.dma_start(wts[:, :], wts_in).then_inc(s["wts_loaded"], 16)
            link = Link(act, s["act_order"])
            act.wait_ge(s["params_loaded"], 16 * PARAM_LOADS)

            def first_pass(t, _):
                act.wait_ge(s["t1_mm"], t.count(1, 1))
                if started(v := t.count(1, -1)):
                    act.wait_ge(s["pot_mm"], v)
                act.activation(t_order(xnT[t.par][:, :]), ps_t[:, :].rearrange("d (j p) -> d j p", j=TPS), ACT.Copy)\
                    .then_inc(s["xn1T_ready"], 1)
                act.wait_ge(s["pot_mm"], t.count(1, 1))
                act.activation(potT[0:2, bass.ds(t.count(N), N)], ps_p[t.par][0:2, :], ACT.Identity, bias=potb[0:2, :])\
                    .then_inc(s["pot_ready"], 1)

            act.wait_ge(s["potb_ready"], 1)
            pairs_of(act, first_pass, B)
            act.wait_ge(s["vabs_ready"], 1)
            link(act.activation(cf[:, 3, :], cf[:, 2, :], ACT.Exp, scale=-1.0))
            act.activation(cf[:, 4, :], cf[:, 3, :], ACT.Ln, bias=1.0).then_inc(s["log_ready"], 1)
            for c in range(NT):
                act.wait_ge(s["dmax_ready"], c + 1)
                act.activation(dmat[:, c * P:(c + 1) * P], dmat[:, c * P:(c + 1) * P], ACT.Exp, scale=-DT,
                               bias=csr[:, c:c + 1]).then_inc(s["dexp_ready"], 1)
            act.wait_ge(s["decC_arg_ready"], 1)
            link(act.activation(decays[:, :], decays[:, :], ACT.Exp, scale=-DT))
            act.activation(sm[:, 8, :], sm[:, 7, :], ACT.Exp, scale=-DT).then_inc(s["decC_exp_ready"], 1)
            def heads_evac(t):
                for n in range(2 * PAIRS):
                    p, key = n // 2, n % 2
                    act.wait_ge(s["qk_mm"], t.count(2 * PAIRS, n + 1))
                    if n == 0:
                        if started(v := t.count(PAIRS)):
                            act.wait_ge(s["qd_ready"], v)
                    act.activation((kT if key else qT)[:, p, :], ps_p[n % 2][:, :], ACT.Identity,
                                   bias=col("bk" if key else "bq", p)).then_inc(s["qk_ready"], 1)

            def prepare(t):
                act.wait_ge(s["t2_mm"], t.count(1, 1))
                act.activation(t_order(xnT[t.par][:, :]), ps_t[:, :].rearrange("d (j p) -> d j p", j=TPS), ACT.Identity,
                               scale=col("g2"), bias=col("b2")).then_inc(s["xnT_ready"], 1)

            def finish(t):
                act.wait_ge(s["t3_mm"], t.count(1, 1))
                act.activation(x3T[:, :], ps_t[:, :], ACT.Identity, scale=col("g3"), bias=col("b3"))\
                    .then_inc(s["x3T_ready"], 1)
                for c in range(FC):
                    act.wait_ge(s["ff1_mm"], t.count(FC, c + 1))
                    act.activation(hff[:, c, :], ps_p[c % 2][:, :], ACT.Gelu_apprx_tanh, bias=col("bff1", c))\
                        .then_inc(s["ff_ready"], 1)

            def heb_evac(t):
                for m in range(TPS):
                    act.wait_ge(s["pv_mm"], t.count(TPS, m + 1))
                    act.activation(hebT[:, :, m * P:(m + 1) * P], ps_h[:, :].rearrange("e (p t) -> e p t", p=PAIRS), ACT.Copy)\
                        .then_inc(s["heb_ready"], 1)

            def a_item(t, first=False, last=False):
                heads_evac(t)
                if not last:
                    prepare(t.at(1))
                if not first:
                    finish(t.at(-1))
                heb_evac(t)

            prepare(Turn(0))
            a_item(Turn(0), first=True)
            with act.Fori(0, (B - 2) // 2) as n:
                for u in range(2):
                    a_item(Turn(1 + u, n))
            a_item(Turn(B - 1), last=True)
            finish(Turn(B - 1))
            def route_xT(t, ts):
                act.wait_ge(s["rt_mm"], ts.count(1, 1))
                act.activation(xnT[t.par][:, :], ps_t[:, :], ACT.Copy).then_inc(s["rxT_ready"], 1)

            def route_pay(t, ts):
                q = t.par
                act.wait_ge(s["pay_ready"], ts.count(1, 1))
                if started(v := ts.half(TPS * 2 * 16)):
                    act.wait_ge(s[f"scattered{q}"], v)
                act.activation(pay[q][:, :, 1, 0:D], pay[q][:, :, 0, 0:D], ACT.Copy).then_inc(s["pay2_ready"], 1)

            def route_weights(t, ts):
                act.wait_ge(s["m_ready"], ts.count(1, 1))
                act.activation(rv[:, 4, :], rv[:, 3, :], ACT.Exp).then_inc(s["e2_ready"], 1)

            def route_item(t, ts, last=False):
                if not last:
                    route_pay(t.at(1), ts.at(1))
                    route_xT(t.at(1), ts.at(1))
                route_weights(t, ts)

            def experts(layer):
                ts = layer * B
                route_pay(Turn(0), Turn(ts))
                route_xT(Turn(0), Turn(ts))
                route_loop(act, route_item, ts)

                def x_evac(j, js):
                    act.wait_ge(s["et_mm"], js.count(1, 1))
                    if started(v := js.count(FC, -FC)):
                        act.wait_ge(s["h_mm"], v)
                    act.activation(exT[j.par], (ps_t, ps_u)[j.par][:, 0:TT], ACT.Copy).then_inc(s["exT_ready"], 1)

                def hidden_evac(j, js):
                    q = j.par
                    if started(v := js.count(1, -1)):
                        act.wait_ge(s["y_mm"], v)
                    for c in range(FC):
                        act.wait_ge(s["h_mm"], js.count(FC, c // 2 * 2 + 2))
                        if c == 0:
                            act.wait_ge(s[f"ewt_loaded{j.quad}"], loads(j, layer, 32))
                        src = (ps_s, ps_p)[q][c // 2][:, (c % 2) * TT:(c % 2 + 1) * TT]
                        b1 = EXP_AT["b1"][0] + c
                        act.activation(ehT[q][:, c, :], src, ACT.Gelu_apprx_tanh, bias=ewt[j.quad][:, b1:b1 + 1])\
                            .then_inc(s["ehT_ready"], 1)

                tile_loop(act, hidden_evac, layer, ahead=x_evac)

            experts(0)

            def scan_xT(t):
                act.wait_ge(s["gt_mm"], t.count(1, 1))
                act.activation(t_order(xnT[t.par][:, :]), ps_t[:, :].rearrange("d (j p) -> d j p", j=TPS), ACT.Identity,
                               scale=col("norm_w")).then_inc(s["gxT_ready"], 1)

            def scan_uz(t):
                act.wait_ge(s["guz_mm"], t.count(1, 1))
                if started(v := t.count(1, -1)):
                    act.wait_ge(s["gx_mm"], v)
                act.activation(uz[t.par], ps_p[t.par][:, :], ACT.Identity, bias=col("b_uz")).then_inc(s["guz_ready"], 1)

            def scan_pass(n):
                for q in range(2):
                    scan_xT(Turn(q, n))
                for q in range(2):
                    scan_uz(Turn(q, n))
                t = Turn(0, n)
                act.wait_ge(s["g_mm"], t.count(1, 2))
                if started(v := t.half()):
                    act.wait_ge(s["gy_ready"], v)
                act.activation(sg, ps_u[:, :], ACT.Sigmoid, bias=col("b_g")).then_inc(s["gsg_ready"], 1)
                act.wait_ge(s["gx_mm"], t.count(1, 2))
                act.activation(dtm, ps_s[1][:, :], ACT.Sigmoid, bias=col("b_dt")).then_inc(s["gdt_ready"], 1)
                act.activation(ut, ps_s[0][:, :], ACT.Tanh, bias=col("b_x")).then_inc(s["gut_ready"], 1)

            scan_pass(None)
            with act.Fori(1, B // 2) as n:
                scan_pass(n)
            experts(1)

        @block.tensor
        def _(pe):
            pe.wait_ge(s["params_loaded"], 16 * PARAM_LOADS)
            pe.matmul(ps_o[0:2, 0:1], cols[:, COLS_AT["w_pot"][0]:COLS_AT["w_pot"][1]], col("b1"), start=True, stop=True)\
                .then_inc(s["potb_mm"], 1)
            pe.wait_ge(s["gw_ready"], 1)

            def first_pass(t, _):
                pe.wait_ge(s["xh1_ready"], t.count(1, 1))
                if started(v := t.count()):
                    pe.wait_ge(s["xn1T_ready"], v)
                for j in range(TPS):
                    mm = pe.transpose(ps_t[:, j * P:(j + 1) * P], xh[t.par][:, j, :], ident)
                mm.then_inc(s["t1_mm"], 1)
                pe.wait_ge(s["xn1T_ready"], t.count(1, 1))
                if started(v := t.count(1, -1)):
                    pe.wait_ge(s["pot_ready"], v)
                pe.matmul(ps_p[t.par][0:2, :], gw, xnT[t.par][:, :], start=True, stop=True).then_inc(s["pot_mm"], 1)

            pairs_of(pe, first_pass, B)
            pe.wait_ge(s["csum_ready"], 1)
            pe.transpose(ps_o[:, 0:NT], csr2[0:NT, :], ident[0:NT, 0:NT]).then_inc(s["csT_mm"], 1)
            pe.wait_ge(s["wts_loaded"], 16)
            def add_bk(t):
                pe.wait_ge(s[f"gt_loaded{t.par}"], t.half(16, 16))
                if started(v := t.count()):
                    pe.wait_ge(s["xnT_ready"], v)
                if started(v := 1 + t.count(1, -2)):
                    pe.wait_ge(s["x3T_ready"], v)
                for j in range(TPS):
                    mm = pe.matmul(ps_t[:, j * P:(j + 1) * P], gt[t.par][0:3, j::TPS], wbk[:, :], start=True, stop=True)
                mm.then_inc(s["bk_mm"], 1)

            def transpose2(t):
                pe.wait_ge(s["xh_ready"], t.count(1, 1))
                for j in range(TPS):
                    mm = pe.transpose(ps_t[:, j * P:(j + 1) * P], xh[t.par][:, j, :], ident)
                mm.then_inc(s["t2_mm"], 1)

            def heb_out(t):
                pe.wait_ge(s["heb_ready"], t.count(TPS, TPS))
                pe.wait_ge(s["x1_ready"], 1 + t.count())
                for j in range(TPS):
                    for p in range(PAIRS):
                        mm = pe.matmul(ps_o[:, j * P:(j + 1) * P], hebT[:, p, j::TPS], W("w_out", p * D, (p + 1) * D),
                                       start=(p == 0), stop=(p == PAIRS - 1))
                mm.then_inc(s["wo_mm"], 1)

            def heads_in(t):
                pe.wait_ge(s["xnT_ready"], t.count(1, 1))
                for n in range(2 * PAIRS):
                    p, key = n // 2, n % 2
                    if n < 2:
                        if started(v := 1 + t.count(FC, -FC)):
                            pe.wait_ge(s["ff_ready"], v)
                    else:
                        pe.wait_ge(s["qk_ready"], t.count(2 * PAIRS, n - 1))
                    pe.matmul(ps_p[n % 2][:, :], W("k" if key else "q", p * P, (p + 1) * P), xnT[t.par][:, :],
                              start=True, stop=True).then_inc(s["qk_mm"], 1)
                for n in range(2 * TPS):
                    m, val = n // 2, n % 2
                    if n < 2:
                        pe.wait_ge(s["qk_ready"], t.count(2 * PAIRS, 2 * PAIRS - 1 + n))
                    else:
                        pe.wait_ge(s["tok_ready"], t.count(2 * TPS, n - 1))
                    pe.matmul(ps_p[n % 2][:, :], xnT[t.par][:, m * P:(m + 1) * P], W("v" if val else "k"),
                              start=True, stop=True).then_inc(s["tok_mm"], 1)

            def mlp_in(t, tail=False):
                pe.wait_ge(s["xh3_ready"], t.count(1, 1))
                if not tail:
                    pe.wait_ge(s["xnT_ready"], t.count(1, 3))
                for j in range(TPS):
                    mm = pe.transpose(ps_t[:, j * P:(j + 1) * P], x3h[:, j, :], ident)
                mm.then_inc(s["t3_mm"], 1)

            def mlp_hidden(t, tail=False):
                pe.wait_ge(s["x3T_ready"], 1 + t.count(1, 1))
                for c in range(FC):
                    if c < 2 and tail:
                        pe.wait_ge(s["ff_ready"], 1 + t.count(FC))
                    elif c < 2:
                        pe.wait_ge(s["tok_ready"], t.count(2 * TPS, 4 * TPS - 1 + c))
                    else:
                        pe.wait_ge(s["ff_ready"], 1 + t.count(FC, c - 1))
                    pe.matmul(ps_p[c % 2][:, :], W("ff1", c * P, (c + 1) * P), x3T[:, :], start=True, stop=True)\
                        .then_inc(s["ff1_mm"], 1)

            def mlp_out(t):
                pe.wait_ge(s["ff_ready"], 1 + t.count(FC, FC))
                pe.wait_ge(s["x3_ready"], t.count(1, 1))
                for j in range(TPS):
                    for c in range(FC):
                        mm = pe.matmul(ps_o[:, j * P:(j + 1) * P], hff[:, c, j * P:(j + 1) * P], W("ff2", c * D, (c + 1) * D),
                                       start=(c == 0), stop=(c == FC - 1))
                mm.then_inc(s["ff2_mm"], 1)

            def scores(t, m):
                pe.wait_ge(s["qk_ready"], t.count(2 * PAIRS, 2 * PAIRS))
                if started(v := t.count(TPS, m)):
                    pe.wait_ge(s["pT_ready"], v)
                ch = slice(m * P, (m + 1) * P)
                for p in range(PAIRS):
                    for o in range(2):
                        h = slice(o * HD, (o + 1) * HD)
                        mm = pe.matmul(ps_s[o][:, p * P:(p + 1) * P], kT[h, p, ch], qT[h, p, ch], start=True, stop=True)
                mm.then_inc(s["sc_mm"], 1)

            def update(t, m):
                pe.wait_ge(s["vdec_ready"], t.count(TPS, m + 1))
                if started(v := t.count(TPS - 1, m)):
                    pe.wait_ge(s["w_ready"], v)
                for p in range(PAIRS):
                    c = slice(p * P, (p + 1) * P)
                    mm = pe.matmul(ps_u[:, c], ktok[:, m, c], vdec[:, m, c], start=True, stop=True)
                mm.then_inc(s["u_mm"], 1)

            def outputs(t, m):
                pe.wait_ge(s["pT_ready"], t.count(TPS, m + 1))
                if started(v := t.count(TPS, m)):
                    pe.wait_ge(s["heb_ready"], v)
                if m:
                    pe.wait_ge(s["w_ready"], t.count(TPS - 1, m))
                    pe.wait_ge(s["qd_ready"], t.count(PAIRS, PAIRS))
                for p in range(PAIRS):
                    c = slice(p * P, (p + 1) * P)
                    if m:
                        pe.matmul(ps_h[:, c], wst[m - 1][:, p, :], qd[:, p, m * P:(m + 1) * P], start=True, stop=False,
                                  skip_group_check=True)
                    for o in range(2):
                        hd = (2 * p + o) * HD
                        mm = pe.matmul(ps_h[o * HD:(o + 1) * HD, c], vtok[:, m, hd:hd + HD], pT[m % 2][o][:, p, :],
                                       start=(m == 0), stop=True, skip_group_check=True)
                mm.then_inc(s["pv_mm"], 1)

            def heb(t):
                for m in range(TPS):
                    scores(t, m)
                    if m:
                        outputs(t, m - 1)
                    if m < TPS - 1:
                        update(t, m)
                outputs(t, TPS - 1)

            def a_item(t, first=False, last=False):
                if not last:
                    add_bk(t.at(1))
                if not first:
                    heb_out(t.at(-1))
                heads_in(t)
                if not last:
                    transpose2(t.at(1))
                if not first:
                    mlp_in(t.at(-1), last)
                    mlp_hidden(t.at(-1))
                heb(t)
                if not first:
                    mlp_out(t.at(-1))

            add_bk(Turn(0))
            transpose2(Turn(0))
            a_item(Turn(0), first=True)
            with pe.Fori(0, (B - 2) // 2) as n:
                for u in range(2):
                    a_item(Turn(1 + u, n))
            a_item(Turn(B - 1), last=True)
            t = Turn(B - 1)
            heb_out(t)
            mlp_in(t, True)
            mlp_hidden(t, True)
            mlp_out(t)
            def route_t(t, ts):
                pe.wait_ge(s["pay_ready"], ts.count(1, 1))
                if started(v := ts.count()):
                    pe.wait_ge(s["rxT_ready"], v)
                for j in range(TPS):
                    mm = pe.transpose(ps_t[:, j * P:(j + 1) * P], pay[t.par][:, j, 0, 0:D], ident)
                mm.then_inc(s["rt_mm"], 1)

            def route_item(t, ts, last=False):
                pe.wait_ge(s["rxT_ready"], ts.count(1, 1))
                if started(v := ts.count()):
                    pe.wait_ge(s["slots_ready"], v)
                for j in range(TPS):
                    mm = pe.matmul(ps_u[:, j * E_N:(j + 1) * E_N], xnT[t.par][:, j * P:(j + 1) * P], W("wr"), start=True, stop=True)
                mm.then_inc(s["score_mm"], 1)
                if not last:
                    route_t(t.at(1), ts.at(1))
                pe.wait_ge(s["m_ready"], ts.count(1, 1))
                flat = rt[:, 8, :, :].rearrange("p j e -> p (j e)")
                pe.matmul(ps_u[:, 64:64 + TPS * E_N], C("before"), flat, start=True, stop=True)
                pe.matmul(ps_u[:, 128:128 + TPS * E_N], C("ones"), flat, start=True, stop=True).then_inc(s["rank_mm"], 1)

            def experts(layer):
                ts = layer * B
                route_t(Turn(0), Turn(ts))
                route_loop(pe, route_item, ts)
                pe.wait_ge(s["slots_ready"], ts + B)

                def x_t(j, js):
                    pe.wait_ge(s[f"ex_loaded{j.quad}"], loads(j, layer, 16))
                    if started(v := js.count(1, -1)):
                        pe.wait_ge(s["exT_ready"], v)
                    for h in range(TH):
                        mm = pe.transpose((ps_t, ps_u)[j.par][:, h * P:(h + 1) * P], ex[j.quad][:, h, 0:D], ident)
                    mm.then_inc(s["et_mm"], 1)

                def hidden(j, js):
                    pe.wait_ge(s["exT_ready"], js.count(1, 1))
                    pe.wait_ge(s[f"ewt_loaded{j.quad}"], loads(j, layer, 32))
                    if started(v := js.count(FC, -FC)):
                        pe.wait_ge(s["ehT_ready"], v)
                    for c in range(FC):
                        w1 = EXP_AT["w1"][0] + c * P
                        pe.matmul((ps_s, ps_p)[j.par][c // 2][:, (c % 2) * TT:(c % 2 + 1) * TT], ewt[j.quad][:, w1:w1 + P],
                                  exT[j.par], start=True, stop=True).then_inc(s["h_mm"], 1)

                def result(j, js):
                    pe.wait_ge(s["ehT_ready"], js.count(FC, FC))
                    if started(v := 1 + js.count(1, -1)):
                        pe.wait_ge(s["ey_ready"], v)
                    for h in range(TH):
                        for c in range(FC):
                            w2 = EXP_AT["w2"][0] + c * D
                            mm = pe.matmul((ps_o, ps_h)[j.par][:, h * D:(h + 1) * D], ehT[j.par][:, c, h * P:(h + 1) * P],
                                           ewt[j.quad][:, w2:w2 + D], start=(c == 0), stop=(c == FC - 1))
                    mm.then_inc(s["y_mm"], 1)

                tile_loop(pe, hidden, layer, ahead=x_t, behind=result)

            experts(0)

            def scan_t(t):
                pe.wait_ge(s["gxh_ready"], t.count(1, 1))
                if started(v := t.count()):
                    pe.wait_ge(s["gxT_ready"], v)
                for j in range(TPS):
                    mm = pe.transpose(ps_t[:, j * P:(j + 1) * P], xh[t.par][:, j, :], ident)
                mm.then_inc(s["gt_mm"], 1)

            def scan_in(t):
                q = t.par
                pe.wait_ge(s["gxT_ready"], t.count(1, 1))
                if started(v := t.count(1, -1)):
                    pe.wait_ge(s["guz_ready"], v)
                if q == 0:
                    if started(v := t.half()):
                        pe.wait_ge(s["gsg_ready"], v)
                pe.matmul(ps_p[q][:, :], W("w_in", 0, 2 * S), xnT[q][:, :], start=True, stop=True).then_inc(s["guz_mm"], 1)
                pe.matmul(ps_u[q * S:(q + 1) * S, :], W("w_in", 2 * S, 3 * S), xnT[q][:, :], start=True, stop=True)\
                    .then_inc(s["g_mm"], 1)

            def scan_gates(t):
                q = t.par
                pe.wait_ge(s["guz_ready"], t.count(1, 1))
                if q == 0:
                    if started(v := t.half()):
                        pe.wait_ge(s["gut_ready"], v)
                    if started(v := t.half()):
                        pe.wait_ge(s["gdt_ready"], v)
                apart(pe)
                for k in range(2):
                    h = slice(k * S, (k + 1) * S)
                    mm = pe.matmul(ps_s[k][q * S:(q + 1) * S, :], W("w_xdt")[h, :], uz[q][h, :], start=True, stop=True)
                mm.then_inc(s["gx_mm"], 1)

            def scan_out(t):
                q = t.par
                pe.wait_ge(s["gy_ready"], t.half(1, 1))
                if started(v := t.count(1, -1)):
                    pe.wait_ge(s["scanned"], v)
                for j in range(TPS):
                    h = slice(q * S, (q + 1) * S)
                    mm = pe.matmul((ps_o, ps_h)[q][:, j * D:(j + 1) * D], ym[h, j::TPS], W("w_outb")[h, :], start=True, stop=True)
                mm.then_inc(s["gout_mm"], 1)

            def scan_pass(n, first=False):
                for q in range(2):
                    scan_t(Turn(q, n))
                for q in range(2):
                    scan_in(Turn(q, n))
                if not first:
                    for q in range(2):
                        scan_out(Turn(q - 2, n))
                for q in range(2):
                    scan_gates(Turn(q, n))

            scan_pass(None, first=True)
            scan_pass(1)
            with pe.Fori(2, B // 2) as n:
                scan_pass(n)
            for q in range(2):
                scan_out(Turn(B - 2 + q))
            experts(1)

        @block.vector
        def _(dve):
            for name in ("x1_ready", "ey_ready",):
                dve.sem_inc(s[name], 1)
            link = Link(dve, s["dve_order"])
            dve.wait_ge(s["params_loaded"], 16 * PARAM_LOADS)
            link(dve.tensor_scalar(gw, cols[:, COLS_AT["w_pot"][0]:COLS_AT["w_pot"][1]], col("g1"), None, ALU.mult))
            dve.wait_ge(s["potb_mm"], 1)
            dve.tensor_tensor(potb[0:2, :], ps_o[0:2, 0:1], col("b_pot")[0:2, :], ALU.add).then_inc(s["potb_ready"], 1)
            dve.memset(cstep[:, :, :], 0.0).then_inc(s["gw_ready"], 1)

            dve.wait_ge(s["x_loaded"], 16 * B)
            with dve.Fori(0, NT // TPS) as n:
                link.enter(n, TPS, 0)
                for j in range(TPS):
                    link.mark(dve.bn_stats(st1[:, bass.ds(n * TPS + j, 1), :].squeeze(1) if False else
                                           st1[:, bass.ds(n * TPS + j, 1), :], X[:, bass.ds(n * TPS + j, 1), :]))
            link.leave(NT // TPS)
            link.sync()
            m, dm, v, t = sm[:, 0, :], sm[:, 1, :], sm[:, 2, :], sm[:, 3, :]
            rab = sm[:, 6, :]
            link.mark(dve.tensor_tensor(m, st1[:, :, 1], st1[:, :, 4], ALU.add))
            link.mark(dve.tensor_tensor(dm, st1[:, :, 1], st1[:, :, 4], ALU.subtract))
            link(dve.tensor_tensor(v, st1[:, :, 2], st1[:, :, 5], ALU.add))
            link.mark(dve.tensor_scalar(m, m, 0.5, None, ALU.mult))
            link.mark(dve.tensor_tensor(dm, dm, dm, ALU.mult))
            link(dve.tensor_scalar(v, v, 1.0 / D, None, ALU.mult))
            dve.scalar_tensor_tensor(out=v, in0=dm, scalar=0.25, in1=v, op0=ALU.mult, op1=ALU.add)\
                .then_inc(s["var_ready"], 1)
            dve.wait_ge(s["rab_ready"], 1)

            def first_pass(t, _):
                if started(v := t.count(1, -1)):
                    dve.wait_ge(s["t1_mm"], v)
                for j in range(TPS):
                    at = tile_at(t, j)
                    ins = dve.tensor_scalar(xh[t.par][:, j, :], X[:, at, :], sm[:, 0, at], sm[:, 6, at],
                                            ALU.subtract, ALU.mult)
                    if j < TPS - 1:
                        link.mark(ins)
                ins.then_inc(s["xh1_ready"], 1)

            pairs_of(dve, first_pass, B, link=link, per=2 * (TPS - 1))

            dve.wait_ge(s["pot_chunked"], 16)
            u, v, va, gm = cf[:, 0, :], cf[:, 1, :], cf[:, 2, :], cf[:, 5, :]
            link(dve.tensor_scalar(va, v, -1.0, None, ALU.mult))
            dve.tensor_tensor(va, v, va, ALU.max).then_inc(s["vabs_ready"], 1)
            link.mark(dve.tensor_scalar(u, u, 2.0, None, ALU.add))
            dve.wait_ge(s["log_ready"], 1)
            link(dve.scalar_tensor_tensor(out=gm, in0=v, scalar=0.0, in1=cf[:, 4, :], op0=ALU.max, op1=ALU.add))
            link.mark(dve.tensor_scalar(gm, gm, GAMMA_FLOOR, None, ALU.add))
            dve.memset(pseq[:, :, :, :], 0.0).then_inc(s["gamma_ready"], 1)
            link.sync()
            link.mark(dve.tensor_copy(dre[:, :, 0], u))
            link.mark(dve.tensor_copy(dre[:, :, 1], u[:, ::-1]))
            link.mark(dve.tensor_copy(dim2[:, :, 0, 0], gm))
            link.mark(dve.tensor_copy(dim2[:, :, 1, 0], gm[:, ::-1]))
            link.mark(dve.tensor_scalar(dim2[:, :, 0, 1], gm, -1.0, None, ALU.mult))
            link.mark(dve.tensor_scalar(dim2[:, :, 1, 1], gm[:, ::-1], -1.0, None, ALU.mult))
            dve.wait_ge(s["csr_loaded"], 16)
            dve.wait_ge(s["gamma_ready"], 1)
            dve.tensor_tensor_scan(csr2[0:NT, :], C("ones")[0:NT, :], csr[0:NT, :], 0.0, ALU.mult, ALU.add)\
                .then_inc(s["csum_ready"], 1)

            def slot(g, i):
                return pseq[:, g, i, :]

            link.mark(dve.memset(slot(0, 1).rearrange("p (r a c) -> p r a c", r=2, a=2)[:, :, 0, 0], 1.0))
            link(dve.memset(slot(0, 0).rearrange("p (r a c) -> p r a c", r=2, a=2)[:, :, 1, 0], 1.0))

            def norm(g, out):
                both = pseq[:, g, SEG:SEG + 2, :]
                link(dve.tensor_reduce(cnrm[:, 0, :], both.rearrange("p i (r m) -> p r i m", r=2), mybir.AxisListType.XY,
                                       ALU.add, apply_absolute_value=True))
                link(dve.reciprocal(cnrm[:, 1, :], cnrm[:, 0, :]))
                for r in range(2):
                    link.mark(dve.tensor_scalar(out[:, :, 4 * r:4 * r + 4], both[:, :, 4 * r:4 * r + 4], cnrm[:, 1, r:r + 1],
                                                None, ALU.mult))
                link.sync()

            for g in range(2):
                if g:
                    norm(0, pseq[:, 1, 0:2, :])
                for i in range(SEG):
                    k = g * SEG + i
                    cur, last, new = slot(g, i + 1), slot(g, i), slot(g, i + 2)
                    swapped = cur.rearrange("p (r a c) -> p r a c", r=2, a=2)[:, :, :, ::-1]
                    link.mark(dve.tensor_tensor(cstep[:, 0, :].rearrange("p (r a c) -> p r a c", r=2, a=2), swapped,
                                                dim2[:, k, :, :].unsqueeze(2).to_broadcast([P, 2, 2, 2]), ALU.mult))
                    for r in range(2):
                        at = slice(4 * r, 4 * r + 4)
                        link.mark(dve.scalar_tensor_tensor(out=cstep[:, 1, at], in0=cur[:, at], scalar=dre[:, k, r:r + 1],
                                                           in1=last[:, at], op0=ALU.mult, op1=ALU.subtract))
                    link.sync()
                    link(dve.tensor_tensor(new, cstep[:, 0, :], cstep[:, 1, :], ALU.add))

            fin = pval[:, 0, 0:16].rearrange("p (i m) -> p i m", i=2)
            norm(1, fin)
            for w in range(2):
                pw = fin[:, 1 - w, :].rearrange("p (r a c) -> p r a c", r=2, a=2)
                mw = cmap[:, :, 8 * w:8 * w + 8].rearrange("p r (o a c) -> p r o a c", o=2, a=2)
                link.mark(dve.tensor_copy(mw[:, :, 0, :, 0], pw[:, :, :, 0]))
                link.mark(dve.tensor_scalar(mw[:, :, 0, :, 1], pw[:, :, :, 1], -1.0, None, ALU.mult))
                link.mark(dve.tensor_copy(mw[:, :, 1, :, 0], pw[:, :, :, 1]))
                link.mark(dve.tensor_copy(mw[:, :, 1, :, 1], pw[:, :, :, 0]))
            link.sync()
            R = 2 * B
            dve.memset(cst16[0:R, :, :], 0.0).then_inc(s["maps_ready"], 1)
            dve.wait_ge(s["csT_mm"], 1)
            link(dve.tensor_copy(csT, ps_o[:, 0:NT]))
            dve.tensor_scalar(csr[:, 0:NT], csT, DT, None, ALU.mult).then_inc(s["csT_ready"], 1)
            dve.wait_ge(s["csum_spread"], 16)
            ends = decays[:, :].rearrange("p (c i) -> p c i", i=P)[:, :, P - 1]
            dve.tensor_tensor(sm[:, 7, :], ends, csT, ALU.subtract).then_inc(s["decC_arg_ready"], 1)
            dve.wait_ge(s["maps_ready"], 1)
            link(dve.memset(cst16[0:R, 0, 0:1], 1.0))
            dve.wait_ge(s["maps_loaded"], 32)
            for k in range(NC - 1):
                link(dve.tensor_tensor(cprod16[0:R, :].rearrange("p (o i) -> p o i", o=4),
                                       cmap16[0:R, k, :].rearrange("p (o i) -> p o i", o=4),
                                       cst16[0:R, k, :].unsqueeze(1).to_broadcast([R, 4, 4]), ALU.mult))
                link(dve.tensor_reduce(cst16[0:R, k + 1, :], cprod16[0:R, :].rearrange("p (o i) -> p o i", o=4), X_AXIS, ALU.add))
            link(dve.tensor_reduce(cnrm16[0:R, 0, :], cst16[0:R, 0:NC, :], X_AXIS, ALU.add, apply_absolute_value=True))
            link(dve.reciprocal(cnrm16[0:R, 1, :], cnrm16[0:R, 0, :]))
            dve.tensor_tensor(cst16[0:R, 0:NC, :], cst16[0:R, 0:NC, :],
                              cnrm16[0:R, 1, :].unsqueeze(2).to_broadcast([R, NC, 4]), ALU.mult).then_inc(s["states_ready"], 1)
            dve.wait_ge(s["states_loaded"], 16)
            link(dve.tensor_scalar(cneg, cstate, -1.0, None, ALU.mult))
            flat = pseq.rearrange("p g i m -> p (g i) m")
            for term in range(4):
                for r in range(2):
                    for c in range(2):
                        a, im = term // 2, term % 2
                        src = flat[:, :, 4 * r + 2 * a + (c ^ im)]
                        sc = (cneg if im and not c else cstate)[:, r, term:term + 1]
                        dst = pval[:, 2 * r + c, :]
                        if term == 0:
                            link.mark(dve.tensor_scalar(dst, src, sc, None, ALU.mult))
                        else:
                            link.mark(dve.scalar_tensor_tensor(out=dst, in0=src, scalar=sc, in1=dst, op0=ALU.mult, op1=ALU.add))
                link.sync()
            pv = pval.rearrange("p (r c) (g i) -> p r c g i", r=2, g=2)

            def val(r, c, back):
                return pv[:, r, c, :, 2 - back:2 - back + SEG]

            def half(x, r):
                return cw[:, x, r, :].rearrange("p (g i) -> p g i", g=2)

            def both(f):
                for r in range(2):
                    link.mark(f(r))
                link.sync()

            both(lambda r: dve.scalar_tensor_tensor(out=half(0, r), in0=val(r, 0, 1), scalar=-1.0, in1=val(r, 0, 1), op0=ALU.mult, op1=ALU.max))
            both(lambda r: dve.scalar_tensor_tensor(out=half(1, r), in0=val(r, 1, 1), scalar=-1.0, in1=val(r, 1, 1), op0=ALU.mult, op1=ALU.max))
            link(dve.tensor_tensor(cw[:, 0], cw[:, 0], cw[:, 1], ALU.add))
            link(dve.reciprocal(cw[:, 1], cw[:, 0]))
            for c in range(2):
                both(lambda r: dve.tensor_tensor(half(2 + c, r), val(r, c, 1), half(1, r), ALU.mult))
                both(lambda r: dve.tensor_tensor(half(4 + c, r), val(r, c, 0), half(1, r), ALU.mult))
            qr, qi, pr, pi = cw[:, 2], cw[:, 3], cw[:, 4], cw[:, 5]
            link.mark(dve.tensor_tensor(cw[:, 6], qr, qr, ALU.mult))
            link.mark(dve.tensor_tensor(cw[:, 7], qi, qi, ALU.mult))
            link.mark(dve.tensor_tensor(cw[:, 8], pr, qr, ALU.mult))
            link.mark(dve.tensor_tensor(cw[:, 9], pi, qi, ALU.mult))
            link.sync()
            link.mark(dve.tensor_tensor(cw[:, 6], cw[:, 6], cw[:, 7], ALU.add))
            link.mark(dve.tensor_tensor(cw[:, 8], cw[:, 8], cw[:, 9], ALU.add))
            link.sync()
            link.mark(dve.tensor_tensor(cw[:, 7], pi, qr, ALU.mult))
            link.mark(dve.tensor_tensor(cw[:, 9], pr, qi, ALU.mult))
            link.mark(dve.reciprocal(cw[:, 0], cw[:, 6]))
            link.sync()
            link.mark(dve.tensor_tensor(cw[:, 7], cw[:, 7], cw[:, 9], ALU.subtract))
            link.mark(dve.tensor_tensor(cw[:, 1], cw[:, 8], cw[:, 0], ALU.mult))
            link.sync()
            link(dve.tensor_tensor(cw[:, 2], cw[:, 7], cw[:, 0], ALU.mult))
            for x, dst in ((1, 3), (2, 4)):
                link.mark(dve.tensor_tensor(cw[:, dst, 0, :], cw[:, x, 0, :], cw[:, x, 1, ::-1], ALU.add))
            link.sync()
            link.mark(dve.tensor_tensor(cw[:, 3, 0, :], cw[:, 3, 0, :], u, ALU.subtract))
            link.mark(dve.tensor_tensor(cw[:, 4, 0, :], cw[:, 4, 0, :], gm, ALU.add))
            link.sync()
            sr, si = cw[:, 3, 0, :], cw[:, 4, 0, :]
            link.mark(dve.tensor_tensor(cw[:, 5, 0, :], sr, sr, ALU.mult))
            link.mark(dve.tensor_tensor(cw[:, 6, 0, :], si, si, ALU.mult))
            link.sync()
            link(dve.tensor_tensor(cw[:, 5, 0, :], cw[:, 5, 0, :], cw[:, 6, 0, :], ALU.add))
            link(dve.reciprocal(cw[:, 6, 0, :], cw[:, 5, 0, :]))
            link(dve.tensor_tensor(green[:, 0, :], sr, cw[:, 6, 0, :], ALU.mult))
            dve.scalar_tensor_tensor(out=green[:, 1, :], in0=si, scalar=-1.0, in1=cw[:, 6, 0, :], op0=ALU.mult,
                                     op1=ALU.mult).then_inc(s["green_ready"], 1)
            dve.wait_ge(s["decC_exp_ready"], 1)
            link(dve.tensor_scalar(decC[:, :], sm[:, 8, :], ETA, None, ALU.mult))
            dve.memset(cneg[:, 0, 0:1], 0.0).then_inc(s["decC_ready"], 1)

            def norm_stats(x, stat, mv, ready):
                for j in range(TPS):
                    link.mark(dve.bn_stats(stat[:, j, :], x[:, j, :]))
                link.sync()
                apart(dve)
                for j in range(TPS):
                    ins = dve.bn_aggr(mv[:, j, :], stat[:, j, :])
                    if j < TPS - 1:
                        link.mark(ins)
                ins.then_inc(s[ready], 1)

            def normalise(dst, x, mv, rs, ready):
                for j in range(TPS):
                    ins = dve.tensor_scalar(dst[:, j, :], x[:, j, :], mv[:, j, 0:1], rs[:, j:j + 1], ALU.subtract, ALU.mult)
                    if j < TPS - 1:
                        link.mark(ins)
                ins.then_inc(s[ready], 1)

            def prepare(t):
                q = t.par
                if started(v := t.count(1, -1)):
                    dve.wait_ge(s["x2b_ready"], v)
                for j in range(TPS):
                    at = tile_at(t, j)
                    link.mark(dve.tensor_scalar(x2[q][:, j, :], X[:, at, :], sm[:, 0, at], sm[:, 4, at], ALU.subtract, ALU.mult))
                link.sync()
                dve.wait_ge(s["bk_mm"], t.count(1, 1))
                flat = x2[q][:, :, :].rearrange("p j d -> p (j d)")
                dve.tensor_tensor(flat, ps_t[:, :], flat, ALU.add).then_inc(s["x2_ready"], 1)
                dve.wait_ge(s["x2_ready"], t.count(1, 1))
                norm_stats(x2[q], stat, mv, "mv_ready")

            def prepare_norm(t):
                dve.wait_ge(s["rs_ready"], t.count(1, 1))
                normalise(xh[t.par], x2[t.par], mv, rs, "xh_ready")

            def finish(t):
                dve.wait_ge(s["wo_mm"], t.count(1, 1))
                dve.wait_ge(s["xres_ready"], 1 + t.count())
                dve.tensor_tensor(x3[:, :, :].rearrange("p j d -> p (j d)"), ps_o[:, :],
                                  x2b[t.par][:, :, :].rearrange("p j d -> p (j d)"), ALU.add).then_inc(s["x3_ready"], 1)
                dve.wait_ge(s["x3_ready"], t.count(1, 1))
                norm_stats(x3, stat3, mv3, "mv3_ready")

            def finish_norm(t):
                dve.wait_ge(s["rs3_ready"], t.count(1, 1))
                normalise(x3h, x3, mv3, rs3, "xh3_ready")

            def finish_out(t):
                dve.wait_ge(s["ff2_mm"], t.count(1, 1))
                dve.wait_ge(s["xres_ready"], 1 + t.count(1, 1))
                dve.tensor_tensor(X[:, tiles(t), :], ps_o[:, :].rearrange("p (j d) -> p j d", j=TPS), xres[:, :, :], ALU.add)\
                    .then_inc(s["x1_ready"], 1)

            def tokens_evac(t):
                if started(v := t.count(TPS)):
                    dve.wait_ge(s["vdec_ready"], v)
                for n in range(2 * TPS):
                    m, val = n // 2, n % 2
                    dve.wait_ge(s["tok_mm"], t.count(2 * TPS, n + 1))
                    dve.tensor_tensor((vtok if val else ktok)[:, m, :], ps_p[n % 2][:, :], row("bv" if val else "bk"), ALU.add)\
                        .then_inc(s["tok_ready"], 1)

            def heb(t):
                def weigh(m):
                    dve.wait_ge(s["sc_mm"], t.count(TPS, m + 1))
                    dm = dmat[:, bass.ds(t.count(N, m * P), P)].unsqueeze(1).to_broadcast([P, PAIRS, P])
                    for o in range(2):
                        ins = dve.tensor_tensor(pT[m % 2][o], ps_s[o][:, :].rearrange("s (p t) -> s p t", p=PAIRS), dm, ALU.mult)
                        if o == 0:
                            link.mark(ins)
                    ins.then_inc(s["pT_ready"], 1)

                def store(m):
                    dve.wait_ge(s["u_mm"], t.count(TPS - 1, m + 1))
                    if m:
                        dve.wait_ge(s["w_ready"], t.count(TPS - 1, m))
                    for o in range(2):
                        h = slice(o * HD, (o + 1) * HD)
                        add = ps_u[h, :].rearrange("d (p e) -> d p e", p=PAIRS)[:, :, h]
                        if m == 0:
                            ins = dve.tensor_copy(wst[m][h, :, h], add)
                        else:
                            ins = dve.scalar_tensor_tensor(out=wst[m][h, :, h], in0=wst[m - 1][h, :, h],
                                                           scalar=decays[h, bass.ds(t.count(N, m * P + P - 1), 1)], in1=add,
                                                           op0=ALU.mult, op1=ALU.add)
                        if o == 0:
                            link.mark(ins)
                    ins.then_inc(s["w_ready"], 1)

                for m in range(TPS):
                    weigh(m)
                    if m < TPS - 1:
                        store(m)

            def a_item(t, first=False, last=False):
                if not last:
                    prepare(t.at(1))
                if not first:
                    finish(t.at(-1))
                if not last:
                    prepare_norm(t.at(1))
                if not first:
                    finish_norm(t.at(-1))
                tokens_evac(t)
                heb(t)
                if not first:
                    finish_out(t.at(-1))

            prepare(Turn(0))
            prepare_norm(Turn(0))
            a_item(Turn(0), first=True)
            with dve.Fori(0, (B - 2) // 2) as n:
                link.enter(n, PER_A, 0)
                for u in range(2):
                    a_item(Turn(1 + u, n))
            link.leave((B - 2) // 2)
            a_item(Turn(B - 1), last=True)
            t = Turn(B - 1)
            finish(t)
            finish_norm(t)
            finish_out(t)
            def route_stats(t, ts):
                for j in range(TPS):
                    link.mark(dve.bn_stats(stat3[:, j, :], X[:, tile_at(t, j), :]))
                link.sync()
                apart(dve)
                for j in range(TPS):
                    ins = dve.bn_aggr(mv3[:, j, :], stat3[:, j, :])
                    if j < TPS - 1:
                        link.mark(ins)
                ins.then_inc(s["rmv_ready"], 1)

            def route_norm(t, ts):
                q = t.par
                dve.wait_ge(s["rrs_ready"], ts.count(1, 1))
                if started(v := ts.half(TPS * 2 * 16)):
                    dve.wait_ge(s[f"scattered{q}"], v)
                if started(v := ts.count(1, -1)):
                    dve.wait_ge(s["pay2_ready"], v)
                apart(dve)
                link.mark(dve.tensor_copy(pay[q][:, :, :, D].bitcast(I32), ids[:, tiles(t), :]))
                for j in range(TPS):
                    link.mark(dve.tensor_scalar(pay[q][:, j, 0, 0:D], X[:, tile_at(t, j), :], mv3[:, j, 0:1], rs3[:, j:j + 1],
                                                ALU.subtract, ALU.mult))
                link.sync()
                dve.sem_inc(s["pay_ready"], 1)

            def route_choose(t, ts):
                def wide(v):
                    return v.unsqueeze(2).to_broadcast([P, TPS, E_N])

                dve.wait_ge(s["score_mm"], ts.count(1, 1))
                link(dve.tensor_tensor(rt[:, 0], ps_u[:, 0:TPS * E_N].rearrange("p (j e) -> p j e", j=TPS),
                                       row("br").unsqueeze(1).to_broadcast([P, TPS, E_N]), ALU.add))
                for k in range(2):
                    sc, eq, pri, oh = rt[:, 4 * k], rt[:, 4 * k + 1], rt[:, 4 * k + 2], rt[:, 4 * k + 3]
                    link(dve.tensor_reduce(rv[:, k], sc, X_AXIS, ALU.max))
                    link(dve.tensor_tensor(eq, sc, wide(rv[:, k]), ALU.is_equal))
                    link(dve.tensor_tensor(pri, eq, C("rev").unsqueeze(1).to_broadcast([P, TPS, E_N]), ALU.mult))
                    link(dve.tensor_reduce(rv[:, 2], pri, X_AXIS, ALU.max))
                    link(dve.tensor_tensor(oh, pri, wide(rv[:, 2]), ALU.is_equal))
                    if k == 0:
                        link(dve.scalar_tensor_tensor(out=rt[:, 4], in0=oh, scalar=NEG_BIG, in1=sc, op0=ALU.mult, op1=ALU.add))
                if started(v := ts.count()):
                    dve.wait_ge(s["rank_mm"], v)
                if started(v := ts.count()):
                    dve.wait_ge(s["e2_ready"], v)
                link.mark(dve.tensor_tensor(rv[:, 3], rv[:, 1], rv[:, 0], ALU.subtract))
                link.mark(dve.tensor_tensor(rt[:, 8], rt[:, 3], rt[:, 7], ALU.add))
                link.sync()
                dve.sem_inc(s["m_ready"], 1)

            def route_slots(t, ts):
                q = t.par
                dve.wait_ge(s["rank_mm"], ts.count(1, 1))
                for j in range(TPS):
                    link(dve.tensor_tensor(cnt[:, j + 1, :], ps_u[:, 128 + j * E_N:128 + (j + 1) * E_N], cnt[:, j, :], ALU.add))
                link(dve.tensor_tensor(rt[:, 9], ps_u[:, 64:64 + TPS * E_N].rearrange("p (j e) -> p j e", j=TPS), cnt[:, 0:TPS, :], ALU.add))
                for k in range(2):
                    link.mark(dve.tensor_tensor(rt[:, 10 + k], rt[:, 3 + 4 * k], rt[:, 9], ALU.mult))
                link.mark(dve.tensor_copy(cnt[:, 0, :], cnt[:, TPS, :]))
                link.sync()
                link(dve.tensor_reduce(rsl[:, :, :], rt[:, 10:12], X_AXIS, ALU.add))
                if started(v := ts.half(TPS * 2 * 16)):
                    dve.wait_ge(s[f"scattered{q}"], v)
                apart(dve)
                dve.tensor_copy(slots[q], rsl[:, :, :]).then_inc(s["slots_ready"], 1)
                dve.wait_ge(s["e2_ready"], ts.count(1, 1))
                link(dve.tensor_scalar(rv[:, 5], rv[:, 4], 1.0, None, ALU.add))
                link(dve.reciprocal(wtok[:, 0, tiles(t)], rv[:, 5]))
                link.mark(dve.tensor_tensor(wtok[:, 1, tiles(t)], wtok[:, 0, tiles(t)], rv[:, 4], ALU.mult))

            def route_item(t, ts, last=False):
                if not last:
                    route_stats(t.at(1), ts.at(1))
                route_choose(t, ts)
                if not last:
                    route_norm(t.at(1), ts.at(1))
                route_slots(t, ts)

            def tile_tables(layer):
                o = slice(0, 1)
                link(dve.tensor_copy(tail_row[o, :], cnt[o, TPS, :]))
                link(dve.tensor_tensor(tl[o, 0, :], cnt[o, TPS, :], C("ebase")[o, :], ALU.subtract))
                link(dve.tensor_tensor(tlk[o], tl[o, 0, :].unsqueeze(2).to_broadcast([1, E_N, 16]),
                                       C("kthr")[o, :].unsqueeze(1).to_broadcast([1, E_N, 16]), ALU.is_gt))
                link(dve.tensor_reduce(tl[o, 1, :], tlk[o], X_AXIS, ALU.add))
                link(dve.tensor_tensor_scan(tl[o, 2, :], C("ones")[o, 0:E_N], tl[o, 1, :], 0.0, ALU.mult, ALU.add))
                wide = [1, MAX_TILES, E_N]
                link(dve.tensor_tensor(tlj[o], C("jj")[o, :].unsqueeze(2).to_broadcast(wide),
                                       tl[o, 2, :].unsqueeze(1).to_broadcast(wide), ALU.is_ge))
                link(dve.tensor_reduce(tlr[o, 0, :], tlj[o], X_AXIS, ALU.add))
                link(dve.tensor_tensor(tlj[o], tlj[o], tl[o, 1, :].unsqueeze(1).to_broadcast(wide), ALU.mult))
                link(dve.tensor_reduce(tlr[o, 1, :], tlj[o], X_AXIS, ALU.add))
                link(dve.tensor_tensor(tlr[o, 1, :], C("jj")[o, :], tlr[o, 1, :], ALU.subtract))
                link(dve.tensor_scalar(tlr[o, 1, :], tlr[o, 1, :], float(TT), None, ALU.mult))
                link(dve.scalar_tensor_tensor(out=tlr[o, 2, :], in0=tlr[o, 0, :], scalar=float(CAP), in1=tlr[o, 1, :],
                                              op0=ALU.mult, op1=ALU.add))
                link(dve.tensor_scalar(tlr[o, 3, :], tlr[o, 0, :], float(E_N - 1), None, ALU.min))
                link(dve.tensor_copy(tile_row[o, :], tlr[o, 2, :]))
                dve.tensor_copy(tile_e[o, :], tlr[o, 3, :]).then_inc(s["tables_ready"], 1)

            def experts(layer):
                ts = layer * B
                link(dve.tensor_copy(cnt[:, 0, :], C("ebase")))
                dve.sem_inc(s["x_final"], 1)
                dve.wait_ge(s["pay_set"], 2)
                route_stats(Turn(0), Turn(ts))
                route_norm(Turn(0), Turn(ts))
                route_loop(dve, route_item, ts, link, PER_R)
                link.sync()
                tile_tables(layer)

                def result(j, js):
                    q = j.par
                    dve.wait_ge(s["y_mm"], js.count(1, 1))
                    dve.wait_ge(s[f"ewt_loaded{j.quad}"], loads(j, layer, 32))
                    if started(v := j.half(32, layer * RETURNS[q])):
                        dve.wait_ge(s[f"returned{q}"], v)
                    dve.tensor_tensor(ey[q], (ps_o, ps_h)[q][:, 0:TH * D].rearrange("p (h d) -> p h d", h=TH),
                                      eb2[j.quad].unsqueeze(1).to_broadcast([P, TH, D]), ALU.add).then_inc(s["ey_ready"], 1)

                tile_loop(dve, result, layer)

                def combine(t, ts):
                    dve.wait_ge(s[f"back_loaded{t.par}"], ts.half(32, 32))
                    for k in range(2):
                        for j in range(TPS):
                            at = tile_at(t, j)
                            link.mark(dve.scalar_tensor_tensor(out=X[:, at, :], in0=yb[t.par][k][:, j, :], scalar=wtok[:, k, at],
                                                               in1=X[:, at, :], op0=ALU.mult, op1=ALU.add))
                        link.sync()
                    dve.sem_inc(s["combined"], 1)

                pairs_of(dve, combine, B, link=link, per=4 * TPS, shift=layer * B)

            dve.wait_ge(s["x1_ready"], 1 + B)
            experts(0)

            def scan_stats(n):
                for q in range(2):
                    for j in range(TPS):
                        link.mark(dve.bn_stats(gstat[:, q, j, :], X[:, tile_at(Turn(q, n), j), :]))
                link.sync()
                apart(dve)
                for q in range(2):
                    for j in range(TPS):
                        link.mark(dve.bn_aggr(gmv[:, q, j, :], gstat[:, q, j, :]))
                link.sync()
                dve.sem_inc(s["gmv_ready"], 1)

            def scan_norm(t):
                q = t.par
                dve.wait_ge(s["grs_ready"], t.half(1, 1))
                if started(v := t.count(1, -1)):
                    dve.wait_ge(s["gres_ready"], v)
                if started(v := t.count(1, -1)):
                    dve.wait_ge(s["gt_mm"], v)
                for j in range(TPS):
                    link.mark(dve.tensor_scalar(x2[q][:, j, :], X[:, tile_at(t, j), :], gmv[:, q, j, 0:1], gr[:, 1, q, j:j + 1],
                                                ALU.subtract, ALU.mult))
                link.sync()
                for j in range(TPS):
                    link.mark(dve.tensor_scalar(xh[q][:, j, :], x2[q][:, j, :], gr[:, 2, q, j:j + 1], None, ALU.mult))
                link.sync()
                dve.sem_inc(s["gxh_ready"], 1)

            def scan_scan(t):
                dve.wait_ge(s["gdt_ready"], t.half(1, 1))
                link(dve.tensor_scalar(am, dtm, -1.0, 1.0, ALU.mult, ALU.add))
                dve.wait_ge(s["gut_ready"], t.half(1, 1))
                link(dve.tensor_tensor(bm, dtm, ut, ALU.mult))
                link(dve.tensor_tensor_scan(hm, am, bm, 0.0, ALU.mult, ALU.add))
                dve.wait_ge(s["gsg_ready"], t.half(1, 1))
                if started(v := t.count()):
                    dve.wait_ge(s["gout_mm"], v)
                dve.tensor_tensor(ym, hm, sg, ALU.mult).then_inc(s["gy_ready"], 1)

            def scan_out(t):
                dve.wait_ge(s["gout_mm"], t.count(1, 1))
                dve.wait_ge(s["gres_ready"], t.count(1, 1))
                dve.tensor_tensor(X[:, tiles(t), :], (ps_o, ps_h)[t.par][:, :].rearrange("p (j d) -> p j d", j=TPS),
                                  X[:, tiles(t), :], ALU.add).then_inc(s["scanned"], 1)

            def scan_pass(n, first=False, last=False):
                for q in range(2):
                    scan_norm(Turn(q, n))
                if not last:
                    scan_stats(1 if n is None else n + 1)
                if not first:
                    for q in range(2):
                        scan_out(Turn(q - 2, n))
                scan_scan(Turn(0, n))

            scan_stats(None)
            scan_pass(None, first=True)
            with dve.Fori(1, B // 2 - 1) as n:
                link.enter(n, PER_G, 1)
                scan_pass(n)
            link.leave(B // 2 - 1 - 1)
            scan_pass(B // 2 - 1, last=True)
            for q in range(2):
                scan_out(Turn(B - 2 + q))
            dve.wait_ge(s["scanned"], B)
            experts(1)


def kernel(**inputs):
    import numpy as np
    import concourse.bacc as _bacc
    from concourse import mybir as _mybir
    from concourse.bass_utils import run_bass_kernel_spmd as _run

    a = {k: np.asarray(v) for k, v in inputs.items()}
    A, G, M = "L0_attn_a_", "L0_attn_b_", "L0_ffn_"

    def chunks(w, n):
        return w.reshape(n, P, -1).transpose(1, 0, 2).reshape(P, -1)

    def pack(parts, widths, height):
        assert [p.shape for p in parts.values()] == [(height, w) for w in widths.values()] and list(parts) == list(widths)
        return np.ascontiguousarray(np.concatenate(list(parts.values()), axis=1))

    hh = H * HD
    wqkv, bqkv = a[A + "w_qkv"], a[A + "b_qkv"]
    b_pot = np.zeros((P, 1), np.float32)
    b_pot[0:2, 0] = a[A + "b_pot"]
    one = lambda v: v.reshape(P, 1)
    col = lambda v: v.reshape(-1, P).T
    cols = pack(dict(
        w_pot=a[A + "w_pot"], g1=one(a[A + "ln1_g"]), b1=one(a[A + "ln1_b"]), g2=one(a[A + "ln2_g"]), b2=one(a[A + "ln2_b"]),
        g3=one(a[A + "ln3_g"]), b3=one(a[A + "ln3_b"]), bq=col(bqkv[0:hh]), bk=col(bqkv[hh:2 * hh]), bff1=col(a[A + "b_ff1"]),
        norm_w=one(a[G + "norm_w"]), b_uz=one(a[G + "b_in"][0:2 * S]), b_g=one(np.tile(a[G + "b_in"][2 * S:], 2)),
        b_x=one(np.tile(a[G + "b_x"], 2)), b_dt=one(np.tile(a[G + "b_dt"], 2)), b_pot=b_pot), COLS_W, P)
    rows = pack(dict(bk=bqkv[None, hh:2 * hh], bv=bqkv[None, 2 * hh:], b_out=a[A + "b_out"][None], b_ff2=a[A + "b_ff2"][None],
                     b_outb=a[G + "b_out"][None], br=a[M + "br"][None]), ROWS_W, 1)
    wts = pack(dict(q=wqkv[:, 0:hh], k=wqkv[:, hh:2 * hh], v=wqkv[:, 2 * hh:], w_out=chunks(a[A + "w_out"], PAIRS), ff1=a[A + "w_ff1"],
                    ff2=chunks(a[A + "w_ff2"], FC), w_in=a[G + "W_in"], w_xdt=np.concatenate([a[G + "W_x"], a[G + "W_dt"]]),
                    w_outb=np.tile(a[G + "W_out"], (2, 1)), wr=a[M + "Wr"]), WTS_W, P)
    wbk = np.concatenate([a[A + "w_bk"], a[A + "b_bk"][None]])
    experts = np.stack([pack(dict(w1=a[M + "W1"][e], w2=chunks(a[M + "W2"][e], FC), b1=col(a[M + "b1"][e])), EXP_W, P)
                        for e in range(E_N)])
    f32 = np.float32
    k, e = np.arange(P), np.arange(E_N)
    every = lambda v: np.broadcast_to(np.asarray(v, f32), (P, len(v)))
    consts = pack(dict(ident=np.eye(P, dtype=f32), ones=np.ones((P, P), f32), before=(k[:, None] < k).astype(f32),
                       mask=np.where(k[:, None] <= k, f32(ETA), f32(0)), rev=every(E_N - e), ebase=every(e * CAP),
                       kthr=every(np.arange(16) * TT), jj=every(np.arange(MAX_TILES))), CONST_W, P)
    token = (np.arange(B)[None, :, None] * N + k[:, None, None] * TPS + np.arange(TPS)[None, None, :]).reshape(P, NT)
    ids = np.stack([token, token + B * N], axis=-1).astype(np.int32)
    tail = np.zeros((P, TH, ROW), np.int32)
    tail[:, :, D] = NOWHERE
    arrays = dict(x_in=np.ascontiguousarray(a[A + "x"].reshape(B, P, TPS, D)), consts=consts, ids_in=ids, tail_in=tail, cols_in=cols,
                  rows_in=rows, wts_in=wts, wbk_in=wbk, experts_in=experts, eb2_in=a[M + "b2"])
    nc = _bacc.Bacc("TRN2", target_bir_lowering=False, num_devices=1)
    args = {n: nc.dram_tensor(n, v.shape, _mybir.dt.from_np(v.dtype), kind="ExternalInput").ap() for n, v in arrays.items()}
    out = nc.dram_tensor("out", (B, P, TPS, D), F32, kind="ExternalOutput").ap()
    hybrid_kernel(nc, **args, out=out)
    r = _run(nc, [arrays], core_ids=[0])
    return r.results[0]["out"].reshape(B, N, D)
```

```python
from contextlib import ExitStack

import concourse.bass as bass
from concourse import mybir

F32 = mybir.dt.float32
I32 = mybir.dt.int32
ALU = mybir.AluOpType
ACT = mybir.ActivationFunctionType
X_AXIS = mybir.AxisListType.X

B, N, D = 8, 512, 128
P = 128
TPS = N // P
NT = B * TPS
H, HD = 8, 64
PAIRS = H // 2
FF = 512
FC = FF // P
ETA, DT, GAMMA_FLOOR, EPS = 0.1, 0.01, 0.1, 1e-5
RMS_EPS = 1e-8
S = 64
E_N = 8
CH = 32
NC = N // CH
SEG = CH // 2
TT = 256
TH = TT // P
CAP = B * N + TT
MAX_TILES = 2 * B * N // TT + E_N - 1
MIN_TILES = 2 * B * N // TT
ROW = 132
ROWS_X = E_N * CAP + (MAX_TILES - MIN_TILES) * TT
NOWHERE = 1 << 20
NEG_BIG = -3e38

CONST_W = dict(ident=P, ones=P, before=P, mask=P, rev=E_N, ebase=E_N, kthr=16, jj=MAX_TILES)
COLS_W = dict(w_pot=2, g1=1, b1=1, g2=1, b2=1, g3=1, b3=1, bq=PAIRS, bk=PAIRS, bff1=FC, norm_w=1,
              b_uz=1, b_g=1, b_x=1, b_dt=1, b_pot=1)
ROWS_W = dict(bk=H * HD, bv=H * HD, b_out=D, b_ff2=D, b_outb=D, br=E_N)
WTS_W = dict(q=H * HD, k=H * HD, v=H * HD, w_out=PAIRS * D, ff1=FF, ff2=FC * D, w_in=3 * S, w_xdt=S, w_outb=D, wr=E_N)
EXP_W = dict(w1=FF, w2=FC * D, b1=FC)


def offsets(widths):
    at, out = 0, {}
    for name, w in widths.items():
        out[name] = (at, at + w)
        at += w
    return out, at


CONST_AT, CONST_N = offsets(CONST_W)
COLS_AT, COLS_N = offsets(COLS_W)
ROWS_AT, ROWS_N = offsets(ROWS_W)
WTS_AT, WTS_N = offsets(WTS_W)
EXP_AT, EXP_N = offsets(EXP_W)


WORK = 22000
PARAM_LOADS = 6
PER_A = 2 * 69
AHEAD = 4
TILES_OF = [len(range(q, MAX_TILES, AHEAD)) for q in range(AHEAD)]
SPARE = 16
RETURNS = [len(range(q, MAX_TILES, 2)) * TH * 16 for q in range(2)]


class Turn:

    def __init__(self, k, n=None, unroll=2):
        self.k, self.n, self.unroll = k, n, unroll

    def at(self, d):
        return Turn(self.k + d, self.n, self.unroll)

    @property
    def par(self):
        return self.k % 2

    @property
    def quad(self):
        return self.k % AHEAD

    def count(self, each=1, more=0):
        if self.n is None:
            return each * self.k + more
        return self.n * (self.unroll * each) + (each * self.k + more)

    def part(self, of, each=1, more=0):
        if self.n is None:
            return each * (self.k // of) + more
        return self.n * (self.unroll // of * each) + (each * (self.k // of) + more)

    def half(self, each=1, more=0):
        return self.part(2, each, more)


class Link:

    def __init__(self, eng, sem):
        self.eng, self.sem, self.base, self.k = eng, sem, 0, 0

    def mark(self, ins):
        ins.then_inc(self.sem, 1)
        self.k += 1

    def sync(self):
        self.eng.wait_ge(self.sem, self.base + self.k)

    def __call__(self, ins):
        self.mark(ins)
        self.sync()

    def enter(self, n, per, first):
        self.start, self.per = self.base + self.k, per
        self.base, self.k = n * per + (self.start - first * per), 0

    def leave(self, passes):
        assert self.k == self.per, f"a pass adds {self.k}, not {self.per}"
        self.base, self.k = self.start + passes * self.per, 0


def hybrid_kernel(nc, x_in, consts, ids_in, tail_in, cols_in, rows_in, wts_in, wbk_in, experts_in, eb2_in, out):
    def dram(name, shape, dt=F32):
        return nc.dram_tensor(name, shape, dt, kind="Internal").ap()

    pot_d = dram("pot_d", (2, B * N))
    gamma_d = dram("gamma_d", (B * N,))
    csum_d = dram("csum_d", (B * N,))
    maps_d = dram("maps_d", (2, B, NC, 16))
    states_d = dram("states_d", (2, B, NC, 4))
    green_d = dram("green_d", (2, B * N))
    routed_d = dram("routed_d", (ROWS_X, ROW))
    back_d = dram("back_d", (2 * B * N, D))

    with ExitStack() as ctx:
        def sb(name, shape, dt=F32):
            return ctx.enter_context(nc.sbuf_tensor(name, shape, dt))

        def sem(name):
            return ctx.enter_context(nc.semaphore(name))

        cst = sb("cst", [P, CONST_N])
        ids = sb("ids", [P, NT, 2], I32)
        tail = sb("tail", [P, ROW], I32)
        cols = sb("cols", [P, COLS_N])
        rows = sb("rows", [P, ROWS_N])
        wts = sb("wts", [P, WTS_N])
        wbk = sb("wbk", [3, D])

        def C(name):
            a, b = CONST_AT[name]
            return cst[:, a:b]

        def col(name, i=0):
            a, _ = COLS_AT[name]
            return cols[:, a + i:a + i + 1]

        def row(name):
            a, b = ROWS_AT[name]
            return rows[:, a:b]

        def W(name, a=0, b=None):
            lo, hi = WTS_AT[name]
            return wts[:, lo + a:hi if b is None else lo + b]

        ident = C("ident")

        X = sb("X", [P, NT, D])
        decays = sb("decays", [P, B * N])
        dmat = sb("dmat", [P, B * N])
        decC = sb("decC", [P, NT])
        sm = sb("sm", [P, 10, NT])
        powc = sb("powc", [P, NT])
        gt = [sb(f"gt{q}", [3, N]) for q in range(2)]
        x2 = [sb(f"x2{q}", [P, TPS, D]) for q in range(2)]
        x2b = [sb(f"x2b{q}", [P, TPS, D]) for q in range(2)]
        xh = [sb(f"xh{q}", [P, TPS, D]) for q in range(2)]
        xnT = [sb(f"xnT{q}", [P, N]) for q in range(2)]
        xres, x3, x3h = (sb(n, [P, TPS, D]) for n in ("xres", "x3", "x3h"))
        x3T = sb("x3T", [P, N])
        stat, stat3 = sb("stat", [P, TPS, 6]), sb("stat3", [P, TPS, 6])
        mv, mv3 = sb("mv", [P, TPS, 2]), sb("mv3", [P, TPS, 2])
        ve, ve3 = sb("ve", [P, TPS]), sb("ve3", [P, TPS])
        rs, rs3 = sb("rs", [P, TPS]), sb("rs3", [P, TPS])
        rms = sb("rms", [P, 3, TPS])
        pay = [sb(f"pay{q}", [P, TPS, 2, ROW]) for q in range(2)]
        wtok = sb("wtok", [P, 2, NT])
        cnt = sb("cnt", [P, TPS + 1, E_N])

        pool = sb("work", [P, WORK])
        used = [0]

        def carve(*shape, dt=F32):
            n = 1
            for s in shape:
                n *= s
            a = used[0]
            used[0] = a + n
            assert used[0] <= WORK, used[0]
            v = pool[:, a:a + n]
            if dt is not F32:
                v = v.bitcast(dt)
            names = " ".join("abcde"[:len(shape)])
            return v.rearrange(f"p ({names}) -> p {names}", **dict(zip("abcde", shape))) if len(shape) > 1 else v

        st1 = carve(NT, 6)
        cf = carve(6, CH)
        dre, dim2 = carve(CH, 2), carve(CH, 2, 2)
        pseq = carve(2, SEG + 2, 8)
        cstep, cnrm = carve(2, 8), carve(2, 2)
        cmap, cstate, cneg = carve(2, 16), carve(2, 4), carve(2, 4)
        cmap16, cst16, cprod16, cnrm16 = carve(NC, 16), carve(NC + 1, 4), carve(16), carve(2, NC)
        pval = carve(4, 2 * (SEG + 2))
        cw = carve(10, 2, CH)
        green = carve(2, CH)
        gw, potT, potb = carve(2), carve(B * N), carve(1)
        csr, csr2, csT = carve(P), carve(P), carve(NT)
        used[0] = 0
        qT, kT, qd = carve(PAIRS, N), carve(PAIRS, N), carve(PAIRS, N)
        ktok, vtok, vdec = carve(TPS, H * HD), carve(TPS, H * HD), carve(TPS, H * HD)
        pT = [[carve(PAIRS, P) for _ in range(2)] for _ in range(2)]
        wst = [carve(PAIRS, P) for _ in range(TPS - 1)]
        hebT, hff = carve(PAIRS, N), carve(FC, N)
        rt, rv = carve(12, TPS, E_N), carve(6, TPS)
        rxT, rsl = carve(N), carve(2, TPS)
        rstat, rmv, rve, rrs = carve(2, TPS, 6), carve(2, TPS, 2), carve(2, TPS), carve(2, TPS)
        slots = [carve(2, TPS, dt=I32) for _ in range(2)]
        used[0] = 0
        tl, tlk, tlj, tlr = carve(4, E_N), carve(E_N, 16), carve(MAX_TILES, E_N), carve(4, MAX_TILES)
        tile_e, tile_row, tail_row = carve(MAX_TILES, dt=I32), carve(MAX_TILES, dt=I32), carve(E_N, dt=I32)
        ewt = [carve(EXP_N) for _ in range(4)]
        eb2 = [carve(D) for _ in range(4)]
        ex = [carve(TH, ROW) for _ in range(4)]
        back_row = [carve(TH, dt=I32) for _ in range(4)]
        exT = [carve(TT) for _ in range(2)]
        ehT = [carve(FC, TT) for _ in range(2)]
        ey = [carve(TH, D) for _ in range(2)]
        yb = [[carve(TPS, D) for _ in range(2)] for _ in range(4)]
        gstat, gmv, gr = carve(2, TPS, 6), carve(2, TPS, 2), carve(4, 2, TPS)
        uz = [carve(N) for _ in range(2)]
        sg, ut, dtm, am, bm, hm, ym = (carve(N) for _ in range(7))

        psb = [ctx.enter_context(nc.psum_tensor(f"ps{i}", [P, 512], F32)) for i in range(8)]
        ps_t, ps_p, ps_s, ps_h, ps_u, ps_o = psb[0], psb[1:3], psb[3:5], psb[5], psb[6], psb[7]

        class Sems(dict):
            def __missing__(self, name):
                self[name] = sem(name)
                return self[name]

        s = Sems()

        def started(value):
            return not isinstance(value, int) or value > 0

        def apart(eng):
            eng.sem_inc(s["passed"], 1)

        def pairs_of(eng, body, items, first=2, link=None, per=0, shift=0):
            for k in range(first):
                body(Turn(k), Turn(k + shift))
            with eng.Fori(first // 2, items // 2) as n:
                if link:
                    link.enter(n, per, first // 2)
                for u in range(2):
                    body(Turn(u, n), Turn(u + shift, n))
            if link:
                link.leave(items // 2 - first // 2)

        def a_loop(eng, item, link=None, per=0):
            item(Turn(0), first=True)
            item(Turn(1), route=False)
            with eng.Fori(1, B // 2 - 1) as n:
                if link:
                    link.enter(n, per, 1)
                for u in range(2):
                    item(Turn(u, n))
            if link:
                link.leave(B // 2 - 2)
            item(Turn(B - 2))
            item(Turn(B - 1), last=True)

        def tile_loop(eng, body, layer, ahead=None, behind=None, peel=2):
            def step(k, n=None, first=False, last=False):
                j = Turn(k, n, AHEAD)
                js = j.at(layer * MAX_TILES)
                body(j, js)
                if ahead and not last:
                    ahead(j.at(1), js.at(1))
                if behind and not first:
                    behind(j.at(-1), js.at(-1))

            if ahead:
                ahead(Turn(0), Turn(layer * MAX_TILES))
            for k in range(peel):
                step(k, first=(k == 0))
            passes = (MAX_TILES - peel) // AHEAD
            with eng.Fori(0, passes) as n:
                for u in range(AHEAD):
                    step(peel + u, n)
            for k in range(peel + passes * AHEAD, MAX_TILES):
                step(k, last=(k == MAX_TILES - 1))
            if behind:
                behind(Turn(MAX_TILES - 1), Turn((layer + 1) * MAX_TILES - 1))

        def routed_in(p):
            if p == 0:
                return []
            return list(range(2 * p - 3, B if p == B // 2 else 2 * p - 1))

        def loads(j, layer, each):
            return j.part(AHEAD, each, each * (1 + layer * TILES_OF[j.quad]))

        block = ctx.enter_context(nc.Block())

        def tiles(t):
            return bass.ds(t.count(TPS), TPS)

        def tile_at(t, j):
            return bass.ds(t.count(TPS, j), 1)

        def t_order(ap):
            return ap.rearrange("d (p j) -> d j p", j=TPS)

        @block.sync
        def _(sp):
            for b in range(B):
                sp.dma_start(X[:, b * TPS:(b + 1) * TPS, :], x_in[b]).then_inc(s["x_loaded"], 16)

            sp.wait_ge(s["pot_ready"], B)
            sp.dma_start(pot_d, potT[0:2, :]).then_inc(s["pot_stored"], 16)
            sp.wait_ge(s["pot_stored"], 16)
            sp.dma_start(cf[:, 0:2, :], pot_d.rearrange("k (p i) -> p k i", i=CH)).then_inc(s["pot_chunked"], 16)
            sp.wait_ge(s["gamma_ready"], 1)
            sp.dma_start(gamma_d.rearrange("(p i) -> p i", i=CH), cf[:, 5, :]).then_inc(s["gamma_stored"], 16)
            sp.wait_ge(s["gamma_stored"], 16)
            sp.dma_start(csr[0:NT, :], gamma_d.rearrange("(c i) -> c i", i=P)).then_inc(s["csr_loaded"], 16)
            sp.wait_ge(s["csum_ready"], 1)
            sp.dma_start(csum_d.rearrange("(c i) -> c i", i=P), csr2[0:NT, :]).then_inc(s["csum_stored"], 16)
            sp.wait_ge(s["csum_stored"], 16)
            sp.dma_start(decays[:, :], csum_d.rearrange("(a n) -> a n", a=1).to_broadcast([P, B * N]))\
                .then_inc(s["csum_spread"], 16)
            sp.wait_ge(s["maps_ready"], 1)
            sp.dma_start(maps_d.rearrange("r b k m -> (b k) r m"), cmap[:, :, :]).then_inc(s["maps_stored"], 16)
            sp.wait_ge(s["maps_stored"], 16)
            sp.dma_start(cmap16[0:B], maps_d[0]).then_inc(s["maps_loaded"], 16)
            sp.dma_start(cmap16[B:2 * B, ::-1, :], maps_d[1]).then_inc(s["maps_loaded"], 16)
            sp.wait_ge(s["states_ready"], 1)
            sp.dma_start(states_d[0], cst16[0:B, 0:NC, :]).then_inc(s["states_stored"], 16)
            sp.dma_start(states_d[1], cst16[B:2 * B, NC - 1::-1, :]).then_inc(s["states_stored"], 16)
            sp.wait_ge(s["states_stored"], 32)
            sp.dma_start(cstate[:, :, :], states_d.rearrange("r b k m -> (b k) r m")).then_inc(s["states_loaded"], 16)
            sp.wait_ge(s["green_ready"], 1)
            sp.dma_start(green_d.rearrange("k (p i) -> p k i", i=CH), green).then_inc(s["green_stored"], 16)
            sp.wait_ge(s["green_stored"], 16)
            def load_green(t):
                if started(v := t.count(1, -1)):
                    sp.wait_ge(s["bk_mm"], v)
                src = green_d[:, bass.ds(t.count(N), N)]
                sp.dma_start(gt[t.par][0:2, :], src).then_inc(s[f"gt_loaded{t.par}"], 16)

            sp.wait_ge(s["ones_set"], 2)
            load_green(Turn(0))
            load_green(Turn(1))
            with sp.Fori(0, (B - 2) // 2) as n:
                for u in range(2):
                    load_green(Turn(2 + u, n))
            def expert_tiles(layer):
                sp.wait_ge(s["tables_ready"], layer + 1)
                for q in range(2):
                    sp.wait_ge(s[f"scattered{q}"], SPARE + (layer + 1) * NT * 16)
                for e in range(E_N):
                    at = sp.value_load(tail_row[0:1, e:e + 1], min_val=e * CAP, max_val=e * CAP + B * N)
                    sp.dma_start(routed_d[bass.ds(at, TT), :].rearrange("(h p) r -> p h r", p=P),
                                 tail[:, :].bitcast(F32).unsqueeze(1).to_broadcast([P, TH, ROW]))\
                        .then_inc(s["tails_filled"], 16)
                sp.wait_ge(s["tails_filled"], (layer + 1) * E_N * 16)

                def load(j, js):
                    q = j.quad
                    e = sp.value_load(tile_e[0:1, bass.ds(j.count(), 1)], min_val=0, max_val=E_N - 1)
                    r = sp.value_load(tile_row[0:1, bass.ds(j.count(), 1)], min_val=0, max_val=ROWS_X - TT)
                    if started(v := js.count(1, -3)):
                        sp.wait_ge(s["et_mm"], v)
                    apart(sp)
                    if started(v := js.count(1, -3)):
                        sp.wait_ge(s["back_row_ready"], v)
                    apart(sp)
                    sp.dma_start(ex[q][:, :, :], routed_d[bass.ds(r, TT), :].rearrange("(h p) r -> p h r", p=P))\
                        .then_inc(s[f"ex_loaded{q}"], 16)
                    if started(v := js.count(1, -3)):
                        sp.wait_ge(s["y_mm"], v)
                    apart(sp)
                    sp.dma_start(ewt[q][:, :], experts_in[bass.ds(e, 1)].rearrange("a p c -> (a p) c")).then_inc(s[f"ewt_loaded{q}"], 16)
                    if started(v := 1 + js.count(1, -3)):
                        sp.wait_ge(s["ey_ready"], v)
                    apart(sp)
                    sp.dma_start(eb2[q][:, :], eb2_in[bass.ds(e, 1), :].to_broadcast([P, D])).then_inc(s[f"ewt_loaded{q}"], 16)

                tile_loop(sp, load, layer, peel=4)
                for q in range(2):
                    sp.wait_ge(s[f"returned{q}"], (layer + 1) * RETURNS[q])

                for b in range(B):
                    q = b % 4
                    if started(v := layer * B + b - 3):
                        sp.wait_ge(s["combined"], v)
                    for k in range(2):
                        src = back_d[(k * B + b) * N:(k * B + b + 1) * N, :].rearrange("(p j) d -> p j d", j=TPS)
                        sp.dma_start(yb[q][k], src).then_inc(s[f"back_loaded{q}"], 16)

            expert_tiles(0)
            expert_tiles(1)

            for b in range(B):
                sp.wait_ge(s["combined"], B + b + 1)
                sp.dma_start(out[b], X[:, b * TPS:(b + 1) * TPS, :]).then_inc(s["stored"], 16)
            sp.wait_ge(s["stored"], 16 * B)

        @block.gpsimd
        def _(pool):
            for name in ("xres_ready",):
                pool.sem_inc(s[name], 1)
            pool.memset(powc[:, :], -0.5).then_inc(s["powc_set"], 1)
            for q in range(2):
                pool.memset(gt[q][:, :], 1.0).then_inc(s["ones_set"], 1)
                pool.memset(pay[q][:, :, :, :], 0.0).then_inc(s["pay_set"], 1)
            pool.wait_ge(s["powc_set"], 1)
            v, t, ra, rb, rab = sm[:, 2, :], sm[:, 3, :], sm[:, 4, :], sm[:, 5, :], sm[:, 6, :]
            link = Link(pool, s["pool_order"])
            pool.wait_ge(s["var_ready"], 1)
            link(pool.tensor_scalar(t, v, EPS, None, ALU.add))
            link(pool.tensor_tensor(ra, t, powc[:, :], ALU.pow))
            link(pool.tensor_tensor(t, ra, ra, ALU.mult))
            link(pool.tensor_tensor(t, t, v, ALU.mult))
            link(pool.tensor_scalar(t, t, EPS, None, ALU.add))
            link(pool.tensor_tensor(rb, t, powc[:, :], ALU.pow))
            pool.tensor_tensor(rab, ra, rb, ALU.mult).then_inc(s["rab_ready"], 1)
            pool.wait_ge(s["csT_ready"], 1)
            pool.wait_ge(s["csum_spread"], 16)
            for c in range(NT):
                pool.tensor_scalar(dmat[:, c * P:(c + 1) * P], decays[:, c * P:(c + 1) * P], csT[:, c:c + 1], None,
                                   ALU.max).then_inc(s["dmax_ready"], 1)
            for m in range(TPS - 1):
                pool.memset(wst[m], 0.0)
            pool.wait_ge(s["dexp_ready"], NT)
            for b in range(B):
                seq = dmat[:, b * N:(b + 1) * N].rearrange("p (c t) -> p c t", t=P)
                pool.tensor_tensor(seq, seq, C("mask").unsqueeze(1).to_broadcast([P, TPS, P]), ALU.mult)\
                    .then_inc(s["dmat_ready"], 1)
            def rstd(var, tmp, dst, ready):
                apart(pool)
                link(pool.tensor_scalar(tmp, var, EPS, None, ALU.add))
                pool.tensor_tensor(dst, tmp, powc[:, 0:TPS], ALU.pow).then_inc(s[ready], 1)

            def prepare(t):
                pool.wait_ge(s["mv_ready"], t.count(1, 1))
                rstd(mv[:, :, 1], ve[:, :], rs[:, :], "rs_ready")
                pool.wait_ge(s["x2_ready"], t.count(1, 1))
                if started(v := t.count(1, -1)):
                    pool.wait_ge(s["x3_ready"], v)
                pool.tensor_tensor(x2b[t.par][:, :, :], x2[t.par][:, :, :],
                                   row("b_out").unsqueeze(1).to_broadcast([P, TPS, D]), ALU.add).then_inc(s["x2b_ready"], 1)

            def finish_norm(t):
                pool.wait_ge(s["mv3_ready"], t.count(1, 1))
                rstd(mv3[:, :, 1], ve3[:, :], rs3[:, :], "rs3_ready")

            def finish_residual(t):
                if started(v := 1 + t.count()):
                    pool.wait_ge(s["x1_ready"], v)
                apart(pool)
                link(pool.tensor_tensor(xres[:, :, :], x3[:, :, :], X[:, tiles(t), :], ALU.add))
                pool.tensor_tensor(xres[:, :, :], xres[:, :, :], row("b_ff2").unsqueeze(1).to_broadcast([P, TPS, D]),
                                   ALU.add).then_inc(s["xres_ready"], 1)

            def scale_heads(t):
                for p in range(PAIRS):
                    pool.wait_ge(s["qk_ready"], t.count(2 * PAIRS, 2 * p + 1))
                    apart(pool)
                    pool.tensor_tensor(qd[:, p, :], qT[:, p, :], decays[:, bass.ds(t.count(N), N)], ALU.mult)\
                        .then_inc(s["qd_ready"], 1)
                for m in range(TPS):
                    pool.wait_ge(s["tok_ready"], t.count(2 * TPS, 2 * m + 2))
                    apart(pool)
                    pool.tensor_tensor(vdec[:, m, :], vtok[:, m, :], decC[:, tile_at(t, m)].to_broadcast([P, H * HD]), ALU.mult)\
                        .then_inc(s["vdec_ready"], 1)

            def route_norm(ts):
                pool.wait_ge(s["rmv_ready"], ts.count(1, 1))
                q = ts.par
                rstd(rmv[:, q, :, 1], rve[:, q, :], rrs[:, q, :], "rrs_ready")

            def route_rows(ts):
                q = ts.par
                pool.wait_ge(s["slots_ready"], 1 + ts.count(1, 1))
                apart(pool)
                pool.wait_ge(s["pay2_ready"], ts.count(1, 1))
                apart(pool)
                for j in range(TPS):
                    for k in range(2):
                        pool.indirect_dma_start(routed_d, bass.IndirectOffsetOnAxis(ap=slots[q][:, k, j:j + 1], axis=0),
                                                pay[q][:, j, k, :], None).then_inc(s[f"scattered{q}"], 16)

            def a_item(t, first=False, last=False, route=True):
                if not last:
                    prepare(t.at(1))
                if not first:
                    finish_norm(t.at(-1))
                if not first and route:
                    route_norm(t.at(-2))
                if not first:
                    finish_residual(t.at(-1))
                scale_heads(t)
                if not first and route:
                    route_rows(t.at(-2))

            pool.wait_ge(s["params_loaded"], 16 * PARAM_LOADS)
            half = (MAX_TILES - MIN_TILES + 1) // 2
            for q, (lo, hi) in enumerate(((0, half), (half, MAX_TILES - MIN_TILES))):
                dst = routed_d[E_N * CAP + lo * TT:E_N * CAP + hi * TT, :].rearrange("(g p) r -> p g r", p=P)
                src = tail[:, :].bitcast(F32).unsqueeze(1).to_broadcast([P, (hi - lo) * TH, ROW])
                pool.dma_start(dst, src).then_inc(s[f"scattered{q}"], SPARE)
            pool.wait_ge(s["decC_ready"], 1)
            prepare(Turn(0))
            a_loop(pool, a_item, link, 8)
            t = Turn(B - 1)
            finish_norm(t)
            route_norm(t.at(-1))
            finish_residual(t)
            route_norm(t)
            route_rows(t.at(-1))
            route_rows(t)
            def experts(layer):
                def give_back(j, js):
                    q = j.par
                    pool.wait_ge(s["ey_ready"], 1 + js.count(1, 1))
                    apart(pool)
                    for h in range(TH):
                        pool.indirect_dma_start(back_d, bass.IndirectOffsetOnAxis(ap=back_row[j.quad][:, h:h + 1], axis=0),
                                                ey[q][:, h, :], None, bounds_check=2 * B * N - 1, oob_is_err=False)\
                            .then_inc(s[f"returned{j.par}"], 16)

                tile_loop(pool, give_back, layer)

            experts(0)

            def scan_norm(t):
                pool.wait_ge(s["gmv_ready"], t.half(1, 1))
                apart(pool)
                v, a, r = gmv[:, :, :, 1], gr[:, 0], gr[:, 1]
                power = powc[:, 0:2 * TPS].rearrange("p (q j) -> p q j", q=2)
                link(pool.tensor_scalar(a, v, EPS, None, ALU.add))
                link(pool.tensor_tensor(r, a, power, ALU.pow))
                link(pool.tensor_tensor(a, r, r, ALU.mult))
                link(pool.tensor_tensor(a, a, v, ALU.mult))
                apart(pool)
                link(pool.tensor_scalar(a, a, RMS_EPS, None, ALU.add))
                pool.tensor_tensor(gr[:, 2], a, power, ALU.pow).then_inc(s["grs_ready"], 1)

            scan_norm(Turn(0))
            for p in range(B // 2 + 1):
                if p < B // 2 - 1:
                    scan_norm(Turn(2 * p + 2))
                if p:
                    route_norm(Turn(B + 2 * p - 2))
                    route_norm(Turn(B + 2 * p - 1))
                for r in routed_in(p):
                    if r >= 0:
                        route_rows(Turn(B + r))
            experts(1)

        @block.scalar
        def _(act):
            for name in ("ff_ready", "x3T_ready", "rxT_ready", "e2_ready",):
                act.sem_inc(s[name], 1)
            for dst, src in ((cols, cols_in), (cst, consts), (rows, rows_in.to_broadcast([P, ROWS_N])), (wbk, wbk_in),
                             (ids, ids_in), (tail, tail_in)):
                full = tuple(slice(None) for _ in dst.shape)
                act.dma_start(dst[full], src).then_inc(s["params_loaded"], 16)
            act.dma_start(wts[:, :], wts_in).then_inc(s["wts_loaded"], 16)
            link = Link(act, s["act_order"])
            act.wait_ge(s["params_loaded"], 16 * PARAM_LOADS)

            def first_pass(t, _):
                act.wait_ge(s["t1_mm"], t.count(1, 1))
                if started(v := t.count(1, -1)):
                    act.wait_ge(s["pot_mm"], v)
                act.activation(t_order(xnT[t.par][:, :]), ps_t[:, :].rearrange("d (j p) -> d j p", j=TPS), ACT.Copy)\
                    .then_inc(s["xn1T_ready"], 1)
                act.wait_ge(s["pot_mm"], t.count(1, 1))
                act.activation(potT[0:2, bass.ds(t.count(N), N)], ps_p[t.par][0:2, :], ACT.Identity, bias=potb[0:2, :])\
                    .then_inc(s["pot_ready"], 1)

            act.wait_ge(s["potb_ready"], 1)
            pairs_of(act, first_pass, B)
            act.wait_ge(s["vabs_ready"], 1)
            link(act.activation(cf[:, 3, :], cf[:, 2, :], ACT.Exp, scale=-1.0))
            act.activation(cf[:, 4, :], cf[:, 3, :], ACT.Ln, bias=1.0).then_inc(s["log_ready"], 1)
            for c in range(NT):
                act.wait_ge(s["dmax_ready"], c + 1)
                act.activation(dmat[:, c * P:(c + 1) * P], dmat[:, c * P:(c + 1) * P], ACT.Exp, scale=-DT,
                               bias=csr[:, c:c + 1]).then_inc(s["dexp_ready"], 1)
            act.wait_ge(s["decC_arg_ready"], 1)
            link(act.activation(decays[:, :], decays[:, :], ACT.Exp, scale=-DT))
            act.activation(sm[:, 8, :], sm[:, 7, :], ACT.Exp, scale=-DT).then_inc(s["decC_exp_ready"], 1)
            def heads_evac(t):
                for n in range(2 * PAIRS):
                    p, key = n // 2, n % 2
                    act.wait_ge(s["qk_mm"], t.count(2 * PAIRS, n + 1))
                    if n == 0:
                        if started(v := t.count(PAIRS)):
                            act.wait_ge(s["qd_ready"], v)
                    act.activation((kT if key else qT)[:, p, :], ps_p[n % 2][:, :], ACT.Identity,
                                   bias=col("bk" if key else "bq", p)).then_inc(s["qk_ready"], 1)

            def prepare(t):
                act.wait_ge(s["t2_mm"], t.count(1, 1))
                act.activation(t_order(xnT[t.par][:, :]), ps_t[:, :].rearrange("d (j p) -> d j p", j=TPS), ACT.Identity,
                               scale=col("g2"), bias=col("b2")).then_inc(s["xnT_ready"], 1)

            def finish(t):
                act.wait_ge(s["t3_mm"], t.count(1, 1))
                act.activation(x3T[:, :], ps_t[:, :], ACT.Identity, scale=col("g3"), bias=col("b3"))\
                    .then_inc(s["x3T_ready"], 1)
                for c in range(FC):
                    act.wait_ge(s["ff1_mm"], t.count(FC, c + 1))
                    act.activation(hff[:, c, :], ps_p[c % 2][:, :], ACT.Gelu_apprx_tanh, bias=col("bff1", c))\
                        .then_inc(s["ff_ready"], 1)

            def heb_evac(t, lo, hi):
                for m in range(lo, hi):
                    act.wait_ge(s["pv_mm"], t.count(TPS, m + 1))
                    act.activation(hebT[:, :, m * P:(m + 1) * P], ps_h[:, :].rearrange("e (p t) -> e p t", p=PAIRS), ACT.Copy)\
                        .then_inc(s["heb_ready"], 1)

            def route_xT(ts):
                act.wait_ge(s["rt_mm"], ts.count(1, 1))
                act.wait_ge(s["score_mm"], 1 + ts.count())
                act.activation(rxT, ps_t[:, :], ACT.Copy).then_inc(s["rxT_ready"], 1)

            def route_pay(ts):
                q = ts.par
                act.wait_ge(s["pay_ready"], ts.count(1, 1))
                act.wait_ge(s[f"scattered{q}"], ts.half(TPS * 2 * 16, SPARE))
                act.activation(pay[q][:, :, 1, 0:D], pay[q][:, :, 0, 0:D], ACT.Copy).then_inc(s["pay2_ready"], 1)

            def route_weights(ts):
                act.wait_ge(s["m_ready"], ts.count(1, 1))
                act.activation(rv[:, 4, :], rv[:, 3, :], ACT.Exp).then_inc(s["e2_ready"], 1)

            def a_item(t, first=False, last=False, route=True):
                heads_evac(t)
                if not last:
                    prepare(t.at(1))
                if not first:
                    finish(t.at(-1))
                if not first and route:
                    route_pay(t.at(-2))
                    route_xT(t.at(-2))
                heb_evac(t, 0, 2)
                if not first and route:
                    route_weights(t.at(-2))
                heb_evac(t, 2, TPS)

            prepare(Turn(0))
            a_loop(act, a_item)
            t = Turn(B - 1)
            finish(t)
            for r in (t.at(-1), t):
                route_pay(r)
                route_xT(r)
                route_weights(r)
            def experts(layer):
                def x_evac(j, js):
                    act.wait_ge(s["et_mm"], js.count(1, 1))
                    if started(v := js.count(FC, -FC)):
                        act.wait_ge(s["h_mm"], v)
                    act.activation(exT[j.par], (ps_t, ps_u)[j.par][:, 0:TT], ACT.Copy).then_inc(s["exT_ready"], 1)

                def hidden_evac(j, js):
                    q = j.par
                    if started(v := js.count(1, -1)):
                        act.wait_ge(s["y_mm"], v)
                    for c in range(FC):
                        act.wait_ge(s["h_mm"], js.count(FC, c // 2 * 2 + 2))
                        if c == 0:
                            act.wait_ge(s[f"ewt_loaded{j.quad}"], loads(j, layer, 32))
                        src = (ps_s, ps_p)[q][c // 2][:, (c % 2) * TT:(c % 2 + 1) * TT]
                        b1 = EXP_AT["b1"][0] + c
                        act.activation(ehT[q][:, c, :], src, ACT.Gelu_apprx_tanh, bias=ewt[j.quad][:, b1:b1 + 1])\
                            .then_inc(s["ehT_ready"], 1)

                tile_loop(act, hidden_evac, layer, ahead=x_evac)

            experts(0)

            def scan_xT(t):
                act.wait_ge(s["gt_mm"], t.count(1, 1))
                act.activation(t_order(xnT[t.par][:, :]), ps_t[:, :].rearrange("d (j p) -> d j p", j=TPS), ACT.Identity,
                               scale=col("norm_w")).then_inc(s["gxT_ready"], 1)

            def scan_uz(t):
                act.wait_ge(s["guz_mm"], t.count(1, 1))
                if started(v := t.count(1, -1)):
                    act.wait_ge(s["gx_mm"], v)
                act.activation(uz[t.par], ps_p[t.par][:, :], ACT.Identity, bias=col("b_uz")).then_inc(s["guz_ready"], 1)

            def scan_pass(n):
                for q in range(2):
                    scan_xT(Turn(q, n))
                for q in range(2):
                    scan_uz(Turn(q, n))
                t = Turn(0, n)
                act.wait_ge(s["g_mm"], t.count(1, 2))
                if started(v := t.half()):
                    act.wait_ge(s["gy_ready"], v)
                act.activation(sg, ps_u[:, :], ACT.Sigmoid, bias=col("b_g")).then_inc(s["gsg_ready"], 1)
                act.wait_ge(s["gx_mm"], t.count(1, 2))
                act.activation(dtm, ps_s[1][:, :], ACT.Sigmoid, bias=col("b_dt")).then_inc(s["gdt_ready"], 1)
                act.activation(ut, ps_s[0][:, :], ACT.Tanh, bias=col("b_x")).then_inc(s["gut_ready"], 1)

            def route_item(r):
                if r < B - 1:
                    route_pay(Turn(B + r + 1))
                    route_xT(Turn(B + r + 1))
                if r >= 0:
                    route_weights(Turn(B + r))

            for p in range(B // 2 + 1):
                if p < B // 2:
                    scan_pass(p)
                for r in routed_in(p):
                    route_item(r)
            experts(1)

        @block.tensor
        def _(pe):
            for name in ("rank_mm", "score_mm",):
                pe.sem_inc(s[name], 1)
            pe.wait_ge(s["params_loaded"], 16 * PARAM_LOADS)
            pe.matmul(ps_o[0:2, 0:1], cols[:, COLS_AT["w_pot"][0]:COLS_AT["w_pot"][1]], col("b1"), start=True, stop=True)\
                .then_inc(s["potb_mm"], 1)
            pe.wait_ge(s["gw_ready"], 1)

            def first_pass(t, _):
                pe.wait_ge(s["xh1_ready"], t.count(1, 1))
                if started(v := t.count()):
                    pe.wait_ge(s["xn1T_ready"], v)
                for j in range(TPS):
                    mm = pe.transpose(ps_t[:, j * P:(j + 1) * P], xh[t.par][:, j, :], ident)
                mm.then_inc(s["t1_mm"], 1)
                pe.wait_ge(s["xn1T_ready"], t.count(1, 1))
                if started(v := t.count(1, -1)):
                    pe.wait_ge(s["pot_ready"], v)
                pe.matmul(ps_p[t.par][0:2, :], gw, xnT[t.par][:, :], start=True, stop=True).then_inc(s["pot_mm"], 1)

            pairs_of(pe, first_pass, B)
            pe.wait_ge(s["csum_ready"], 1)
            pe.transpose(ps_o[:, 0:NT], csr2[0:NT, :], ident[0:NT, 0:NT]).then_inc(s["csT_mm"], 1)
            pe.wait_ge(s["wts_loaded"], 16)
            def add_bk(t):
                pe.wait_ge(s[f"gt_loaded{t.par}"], t.half(16, 16))
                if started(v := t.count()):
                    pe.wait_ge(s["xnT_ready"], v)
                if started(v := 1 + t.count(1, -2)):
                    pe.wait_ge(s["x3T_ready"], v)
                if started(v := 1 + t.count(1, -3)):
                    pe.wait_ge(s["rxT_ready"], v)
                for j in range(TPS):
                    mm = pe.matmul(ps_t[:, j * P:(j + 1) * P], gt[t.par][0:3, j::TPS], wbk[:, :], start=True, stop=True)
                mm.then_inc(s["bk_mm"], 1)

            def transpose2(t):
                pe.wait_ge(s["xh_ready"], t.count(1, 1))
                for j in range(TPS):
                    mm = pe.transpose(ps_t[:, j * P:(j + 1) * P], xh[t.par][:, j, :], ident)
                mm.then_inc(s["t2_mm"], 1)

            def heb_out(t):
                pe.wait_ge(s["heb_ready"], t.count(TPS, TPS))
                if started(v := 1 + t.count()):
                    pe.wait_ge(s["x1_ready"], v)
                for j in range(TPS):
                    for p in range(PAIRS):
                        mm = pe.matmul(ps_o[:, j * P:(j + 1) * P], hebT[:, p, j::TPS], W("w_out", p * D, (p + 1) * D),
                                       start=(p == 0), stop=(p == PAIRS - 1))
                mm.then_inc(s["wo_mm"], 1)

            def heads_in(t):
                pe.wait_ge(s["xnT_ready"], t.count(1, 1))
                for n in range(2 * PAIRS):
                    p, key = n // 2, n % 2
                    if n < 2:
                        if started(v := 1 + t.count(FC, -FC)):
                            pe.wait_ge(s["ff_ready"], v)
                    else:
                        pe.wait_ge(s["qk_ready"], t.count(2 * PAIRS, n - 1))
                    pe.matmul(ps_p[n % 2][:, :], W("k" if key else "q", p * P, (p + 1) * P), xnT[t.par][:, :],
                              start=True, stop=True).then_inc(s["qk_mm"], 1)
                for n in range(2 * TPS):
                    m, val = n // 2, n % 2
                    if n < 2:
                        pe.wait_ge(s["qk_ready"], t.count(2 * PAIRS, 2 * PAIRS - 1 + n))
                    else:
                        pe.wait_ge(s["tok_ready"], t.count(2 * TPS, n - 1))
                    pe.matmul(ps_p[n % 2][:, :], xnT[t.par][:, m * P:(m + 1) * P], W("v" if val else "k"),
                              start=True, stop=True).then_inc(s["tok_mm"], 1)

            def mlp_in(t, tail=False):
                pe.wait_ge(s["xh3_ready"], t.count(1, 1))
                if tail:
                    pe.wait_ge(s["rxT_ready"], 1 + t.count(1, -1))
                if not tail:
                    pe.wait_ge(s["xnT_ready"], t.count(1, 3))
                for j in range(TPS):
                    mm = pe.transpose(ps_t[:, j * P:(j + 1) * P], x3h[:, j, :], ident)
                mm.then_inc(s["t3_mm"], 1)

            def mlp_hidden(t, tail=False):
                pe.wait_ge(s["x3T_ready"], 1 + t.count(1, 1))
                for c in range(FC):
                    if c < 2 and tail:
                        pe.wait_ge(s["ff_ready"], 1 + t.count(FC))
                    elif c < 2:
                        pe.wait_ge(s["tok_ready"], t.count(2 * TPS, 4 * TPS - 1 + c))
                    else:
                        pe.wait_ge(s["ff_ready"], 1 + t.count(FC, c - 1))
                    pe.matmul(ps_p[c % 2][:, :], W("ff1", c * P, (c + 1) * P), x3T[:, :], start=True, stop=True)\
                        .then_inc(s["ff1_mm"], 1)

            def mlp_out(t):
                pe.wait_ge(s["ff_ready"], 1 + t.count(FC, FC))
                pe.wait_ge(s["x3_ready"], t.count(1, 1))
                if started(v := 1 + t.count()):
                    pe.wait_ge(s["slots_ready"], v)
                for j in range(TPS):
                    for c in range(FC):
                        mm = pe.matmul(ps_o[:, j * P:(j + 1) * P], hff[:, c, j * P:(j + 1) * P], W("ff2", c * D, (c + 1) * D),
                                       start=(c == 0), stop=(c == FC - 1))
                mm.then_inc(s["ff2_mm"], 1)

            def scores(t, m):
                pe.wait_ge(s["qk_ready"], t.count(2 * PAIRS, 2 * PAIRS))
                if started(v := t.count(TPS, m)):
                    pe.wait_ge(s["pT_ready"], v)
                ch = slice(m * P, (m + 1) * P)
                for p in range(PAIRS):
                    for o in range(2):
                        h = slice(o * HD, (o + 1) * HD)
                        mm = pe.matmul(ps_s[o][:, p * P:(p + 1) * P], kT[h, p, ch], qT[h, p, ch], start=True, stop=True)
                mm.then_inc(s["sc_mm"], 1)

            def update(t, m):
                pe.wait_ge(s["vdec_ready"], t.count(TPS, m + 1))
                if started(v := t.count(TPS - 1, m)):
                    pe.wait_ge(s["w_ready"], v)
                for p in range(PAIRS):
                    c = slice(p * P, (p + 1) * P)
                    mm = pe.matmul(ps_u[:, c], ktok[:, m, c], vdec[:, m, c], start=True, stop=True)
                mm.then_inc(s["u_mm"], 1)

            def outputs(t, m):
                pe.wait_ge(s["pT_ready"], t.count(TPS, m + 1))
                if started(v := t.count(TPS, m)):
                    pe.wait_ge(s["heb_ready"], v)
                if m:
                    pe.wait_ge(s["w_ready"], t.count(TPS - 1, m))
                    pe.wait_ge(s["qd_ready"], t.count(PAIRS, PAIRS))
                for p in range(PAIRS):
                    c = slice(p * P, (p + 1) * P)
                    if m:
                        pe.matmul(ps_h[:, c], wst[m - 1][:, p, :], qd[:, p, m * P:(m + 1) * P], start=True, stop=False,
                                  skip_group_check=True)
                    for o in range(2):
                        hd = (2 * p + o) * HD
                        mm = pe.matmul(ps_h[o * HD:(o + 1) * HD, c], vtok[:, m, hd:hd + HD], pT[m % 2][o][:, p, :],
                                       start=(m == 0), stop=True, skip_group_check=True)
                mm.then_inc(s["pv_mm"], 1)

            def heb(t, route):
                for m in range(TPS):
                    scores(t, m)
                    if m:
                        outputs(t, m - 1)
                    if m < TPS - 1:
                        update(t, m)
                    if route and m == 0:
                        route_scores(t.at(-2), t.at(-1))
                    if route and m == 2:
                        route_ranks(t.at(-2))
                outputs(t, TPS - 1)

            def route_t(ts):
                pe.wait_ge(s["pay_ready"], ts.count(1, 1))
                for j in range(TPS):
                    mm = pe.transpose(ps_t[:, j * P:(j + 1) * P], pay[ts.par][:, j, 0, 0:D], ident)
                mm.then_inc(s["rt_mm"], 1)

            def route_scores(ts, after=None):
                pe.wait_ge(s["rxT_ready"], 1 + ts.count(1, 1))
                if after:
                    pe.wait_ge(s["x3_ready"], after.count(1, 1))
                for j in range(TPS):
                    mm = pe.matmul(ps_o[:, j * E_N:(j + 1) * E_N], rxT[:, j * P:(j + 1) * P], W("wr"), start=True, stop=True)
                mm.then_inc(s["score_mm"], 1)

            def route_ranks(ts):
                pe.wait_ge(s["m_ready"], ts.count(1, 1))
                flat = rt[:, 8, :, :].rearrange("p j e -> p (j e)")
                pe.matmul(ps_o[:, 64:64 + TPS * E_N], C("before"), flat, start=True, stop=True)
                pe.matmul(ps_o[:, 128:128 + TPS * E_N], C("ones"), flat, start=True, stop=True).then_inc(s["rank_mm"], 1)

            def a_item(t, first=False, last=False, route=True):
                route = route and not first
                if not last:
                    add_bk(t.at(1))
                if not first:
                    heb_out(t.at(-1))
                heads_in(t)
                if not last:
                    transpose2(t.at(1))
                if not first:
                    mlp_in(t.at(-1), last)
                    mlp_hidden(t.at(-1))
                if route:
                    route_t(t.at(-2))
                heb(t, route)
                if not first:
                    mlp_out(t.at(-1))

            add_bk(Turn(0))
            transpose2(Turn(0))
            a_loop(pe, a_item)
            t = Turn(B - 1)
            heb_out(t)
            mlp_in(t, True)
            mlp_hidden(t, True)
            route_t(t.at(-1))
            route_scores(t.at(-1), t)
            route_ranks(t.at(-1))
            mlp_out(t)
            pe.wait_ge(s["x1_ready"], 1 + B)
            route_t(t)
            route_scores(t)
            route_ranks(t)
            def experts(layer):
                def x_t(j, js):
                    pe.wait_ge(s[f"ex_loaded{j.quad}"], loads(j, layer, 16))
                    if started(v := js.count(1, -1)):
                        pe.wait_ge(s["exT_ready"], v)
                    for h in range(TH):
                        mm = pe.transpose((ps_t, ps_u)[j.par][:, h * P:(h + 1) * P], ex[j.quad][:, h, 0:D], ident)
                    mm.then_inc(s["et_mm"], 1)

                def hidden(j, js):
                    pe.wait_ge(s["exT_ready"], js.count(1, 1))
                    pe.wait_ge(s[f"ewt_loaded{j.quad}"], loads(j, layer, 32))
                    if started(v := js.count(FC, -FC)):
                        pe.wait_ge(s["ehT_ready"], v)
                    for c in range(FC):
                        w1 = EXP_AT["w1"][0] + c * P
                        pe.matmul((ps_s, ps_p)[j.par][c // 2][:, (c % 2) * TT:(c % 2 + 1) * TT], ewt[j.quad][:, w1:w1 + P],
                                  exT[j.par], start=True, stop=True).then_inc(s["h_mm"], 1)

                def result(j, js):
                    pe.wait_ge(s["ehT_ready"], js.count(FC, FC))
                    if started(v := 1 + js.count(1, -1)):
                        pe.wait_ge(s["ey_ready"], v)
                    for h in range(TH):
                        for c in range(FC):
                            w2 = EXP_AT["w2"][0] + c * D
                            mm = pe.matmul((ps_o, ps_h)[j.par][:, h * D:(h + 1) * D], ehT[j.par][:, c, h * P:(h + 1) * P],
                                           ewt[j.quad][:, w2:w2 + D], start=(c == 0), stop=(c == FC - 1))
                    mm.then_inc(s["y_mm"], 1)

                tile_loop(pe, hidden, layer, ahead=x_t, behind=result)

            experts(0)

            def scan_t(t):
                pe.wait_ge(s["gxh_ready"], t.count(1, 1))
                if started(v := t.count()):
                    pe.wait_ge(s["gxT_ready"], v)
                pe.wait_ge(s["rxT_ready"], 1 + B + max(0, t.k // 2 * 2 - 2))
                for j in range(TPS):
                    mm = pe.transpose(ps_t[:, j * P:(j + 1) * P], xh[t.par][:, j, :], ident)
                mm.then_inc(s["gt_mm"], 1)

            def scan_in(t):
                q = t.par
                pe.wait_ge(s["gxT_ready"], t.count(1, 1))
                if started(v := t.count(1, -1)):
                    pe.wait_ge(s["guz_ready"], v)
                if q == 0:
                    if started(v := t.half()):
                        pe.wait_ge(s["gsg_ready"], v)
                pe.matmul(ps_p[q][:, :], W("w_in", 0, 2 * S), xnT[q][:, :], start=True, stop=True).then_inc(s["guz_mm"], 1)
                pe.matmul(ps_u[q * S:(q + 1) * S, :], W("w_in", 2 * S, 3 * S), xnT[q][:, :], start=True, stop=True)\
                    .then_inc(s["g_mm"], 1)

            def scan_gates(t):
                q = t.par
                pe.wait_ge(s["guz_ready"], t.count(1, 1))
                if q == 0:
                    if started(v := t.half()):
                        pe.wait_ge(s["gut_ready"], v)
                    if started(v := t.half()):
                        pe.wait_ge(s["gdt_ready"], v)
                apart(pe)
                for k in range(2):
                    h = slice(k * S, (k + 1) * S)
                    mm = pe.matmul(ps_s[k][q * S:(q + 1) * S, :], W("w_xdt")[h, :], uz[q][h, :], start=True, stop=True)
                mm.then_inc(s["gx_mm"], 1)

            def scan_out(t):
                q = t.par
                pe.wait_ge(s["gy_ready"], t.half(1, 1))
                if started(v := t.count(1, -1)):
                    pe.wait_ge(s["scanned"], v)
                pe.wait_ge(s["slots_ready"], 1 + B + max(0, t.k // 2 * 2 - 1))
                for j in range(TPS):
                    h, at = slice(q * S, (q + 1) * S), (ps_o, ps_h)[q][:, j * D:(j + 1) * D]
                    pe.matmul(at, C("ones")[0:1, :], row("b_outb")[0:1, :], start=True, stop=False)
                    mm = pe.matmul(at, ym[h, j::TPS], W("w_outb")[h, :], start=False, stop=True)
                mm.then_inc(s["gout_mm"], 1)

            def route_item(r):
                if r >= 0:
                    pe.wait_ge(s["scanned"], min(B, (r + 3) // 2 * 2 - 1))
                    pe.wait_ge(s["slots_ready"], 1 + B + r)
                    route_scores(Turn(B + r))
                if r < B - 1:
                    pe.wait_ge(s["gxT_ready"], min(B, (r + 3) // 2 * 2 + 2))
                    pe.wait_ge(s["rxT_ready"], 1 + B + r + 1)
                    route_t(Turn(B + r + 1))
                if r >= 0:
                    route_ranks(Turn(B + r))

            for p in range(B // 2 + 1):
                if p < B // 2:
                    for q in range(2):
                        scan_t(Turn(2 * p + q))
                    for q in range(2):
                        scan_in(Turn(2 * p + q))
                if p:
                    for q in range(2):
                        scan_out(Turn(2 * p - 2 + q))
                if p < B // 2:
                    for q in range(2):
                        scan_gates(Turn(2 * p + q))
                for r in routed_in(p):
                    route_item(r)
            experts(1)

        @block.vector
        def _(dve):
            for name in ("x1_ready", "ey_ready", "slots_ready",):
                dve.sem_inc(s[name], 1)
            link = Link(dve, s["dve_order"])
            dve.wait_ge(s["params_loaded"], 16 * PARAM_LOADS)
            link(dve.tensor_scalar(gw, cols[:, COLS_AT["w_pot"][0]:COLS_AT["w_pot"][1]], col("g1"), None, ALU.mult))
            dve.wait_ge(s["potb_mm"], 1)
            dve.tensor_tensor(potb[0:2, :], ps_o[0:2, 0:1], col("b_pot")[0:2, :], ALU.add).then_inc(s["potb_ready"], 1)
            dve.memset(cstep[:, :, :], 0.0).then_inc(s["gw_ready"], 1)

            dve.wait_ge(s["x_loaded"], 16 * B)
            with dve.Fori(0, NT // TPS) as n:
                link.enter(n, TPS, 0)
                for j in range(TPS):
                    link.mark(dve.bn_stats(st1[:, bass.ds(n * TPS + j, 1), :].squeeze(1) if False else
                                           st1[:, bass.ds(n * TPS + j, 1), :], X[:, bass.ds(n * TPS + j, 1), :]))
            link.leave(NT // TPS)
            link.sync()
            m, dm, v, t = sm[:, 0, :], sm[:, 1, :], sm[:, 2, :], sm[:, 3, :]
            rab = sm[:, 6, :]
            link.mark(dve.tensor_tensor(m, st1[:, :, 1], st1[:, :, 4], ALU.add))
            link.mark(dve.tensor_tensor(dm, st1[:, :, 1], st1[:, :, 4], ALU.subtract))
            link(dve.tensor_tensor(v, st1[:, :, 2], st1[:, :, 5], ALU.add))
            link.mark(dve.tensor_scalar(m, m, 0.5, None, ALU.mult))
            link.mark(dve.tensor_tensor(dm, dm, dm, ALU.mult))
            link(dve.tensor_scalar(v, v, 1.0 / D, None, ALU.mult))
            dve.scalar_tensor_tensor(out=v, in0=dm, scalar=0.25, in1=v, op0=ALU.mult, op1=ALU.add)\
                .then_inc(s["var_ready"], 1)
            dve.wait_ge(s["rab_ready"], 1)

            def first_pass(t, _):
                if started(v := t.count(1, -1)):
                    dve.wait_ge(s["t1_mm"], v)
                for j in range(TPS):
                    at = tile_at(t, j)
                    ins = dve.tensor_scalar(xh[t.par][:, j, :], X[:, at, :], sm[:, 0, at], sm[:, 6, at],
                                            ALU.subtract, ALU.mult)
                    if j < TPS - 1:
                        link.mark(ins)
                ins.then_inc(s["xh1_ready"], 1)

            pairs_of(dve, first_pass, B, link=link, per=2 * (TPS - 1))

            dve.wait_ge(s["pot_chunked"], 16)
            u, v, va, gm = cf[:, 0, :], cf[:, 1, :], cf[:, 2, :], cf[:, 5, :]
            link(dve.tensor_scalar(va, v, -1.0, None, ALU.mult))
            dve.tensor_tensor(va, v, va, ALU.max).then_inc(s["vabs_ready"], 1)
            link.mark(dve.tensor_scalar(u, u, 2.0, None, ALU.add))
            dve.wait_ge(s["log_ready"], 1)
            link(dve.scalar_tensor_tensor(out=gm, in0=v, scalar=0.0, in1=cf[:, 4, :], op0=ALU.max, op1=ALU.add))
            link.mark(dve.tensor_scalar(gm, gm, GAMMA_FLOOR, None, ALU.add))
            dve.memset(pseq[:, :, :, :], 0.0).then_inc(s["gamma_ready"], 1)
            link.sync()
            link.mark(dve.tensor_copy(dre[:, :, 0], u))
            link.mark(dve.tensor_copy(dre[:, :, 1], u[:, ::-1]))
            link.mark(dve.tensor_copy(dim2[:, :, 0, 0], gm))
            link.mark(dve.tensor_copy(dim2[:, :, 1, 0], gm[:, ::-1]))
            link.mark(dve.tensor_scalar(dim2[:, :, 0, 1], gm, -1.0, None, ALU.mult))
            link.mark(dve.tensor_scalar(dim2[:, :, 1, 1], gm[:, ::-1], -1.0, None, ALU.mult))
            dve.wait_ge(s["csr_loaded"], 16)
            dve.wait_ge(s["gamma_ready"], 1)
            dve.tensor_tensor_scan(csr2[0:NT, :], C("ones")[0:NT, :], csr[0:NT, :], 0.0, ALU.mult, ALU.add)\
                .then_inc(s["csum_ready"], 1)

            def slot(g, i):
                return pseq[:, g, i, :]

            link.mark(dve.memset(slot(0, 1).rearrange("p (r a c) -> p r a c", r=2, a=2)[:, :, 0, 0], 1.0))
            link(dve.memset(slot(0, 0).rearrange("p (r a c) -> p r a c", r=2, a=2)[:, :, 1, 0], 1.0))

            def norm(g, out):
                both = pseq[:, g, SEG:SEG + 2, :]
                link(dve.tensor_reduce(cnrm[:, 0, :], both.rearrange("p i (r m) -> p r i m", r=2), mybir.AxisListType.XY,
                                       ALU.add, apply_absolute_value=True))
                link(dve.reciprocal(cnrm[:, 1, :], cnrm[:, 0, :]))
                for r in range(2):
                    link.mark(dve.tensor_scalar(out[:, :, 4 * r:4 * r + 4], both[:, :, 4 * r:4 * r + 4], cnrm[:, 1, r:r + 1],
                                                None, ALU.mult))
                link.sync()

            for g in range(2):
                if g:
                    norm(0, pseq[:, 1, 0:2, :])
                for i in range(SEG):
                    k = g * SEG + i
                    cur, last, new = slot(g, i + 1), slot(g, i), slot(g, i + 2)
                    swapped = cur.rearrange("p (r a c) -> p r a c", r=2, a=2)[:, :, :, ::-1]
                    link.mark(dve.tensor_tensor(cstep[:, 0, :].rearrange("p (r a c) -> p r a c", r=2, a=2), swapped,
                                                dim2[:, k, :, :].unsqueeze(2).to_broadcast([P, 2, 2, 2]), ALU.mult))
                    for r in range(2):
                        at = slice(4 * r, 4 * r + 4)
                        link.mark(dve.scalar_tensor_tensor(out=cstep[:, 1, at], in0=cur[:, at], scalar=dre[:, k, r:r + 1],
                                                           in1=last[:, at], op0=ALU.mult, op1=ALU.subtract))
                    link.sync()
                    link(dve.tensor_tensor(new, cstep[:, 0, :], cstep[:, 1, :], ALU.add))

            fin = pval[:, 0, 0:16].rearrange("p (i m) -> p i m", i=2)
            norm(1, fin)
            for w in range(2):
                pw = fin[:, 1 - w, :].rearrange("p (r a c) -> p r a c", r=2, a=2)
                mw = cmap[:, :, 8 * w:8 * w + 8].rearrange("p r (o a c) -> p r o a c", o=2, a=2)
                link.mark(dve.tensor_copy(mw[:, :, 0, :, 0], pw[:, :, :, 0]))
                link.mark(dve.tensor_scalar(mw[:, :, 0, :, 1], pw[:, :, :, 1], -1.0, None, ALU.mult))
                link.mark(dve.tensor_copy(mw[:, :, 1, :, 0], pw[:, :, :, 1]))
                link.mark(dve.tensor_copy(mw[:, :, 1, :, 1], pw[:, :, :, 0]))
            link.sync()
            R = 2 * B
            dve.memset(cst16[0:R, :, :], 0.0).then_inc(s["maps_ready"], 1)
            dve.wait_ge(s["csT_mm"], 1)
            link(dve.tensor_copy(csT, ps_o[:, 0:NT]))
            dve.tensor_scalar(csr[:, 0:NT], csT, DT, None, ALU.mult).then_inc(s["csT_ready"], 1)
            dve.wait_ge(s["csum_spread"], 16)
            ends = decays[:, :].rearrange("p (c i) -> p c i", i=P)[:, :, P - 1]
            dve.tensor_tensor(sm[:, 7, :], ends, csT, ALU.subtract).then_inc(s["decC_arg_ready"], 1)
            dve.wait_ge(s["maps_ready"], 1)
            link(dve.memset(cst16[0:R, 0, 0:1], 1.0))
            dve.wait_ge(s["maps_loaded"], 32)
            for k in range(NC - 1):
                link(dve.tensor_tensor(cprod16[0:R, :].rearrange("p (o i) -> p o i", o=4),
                                       cmap16[0:R, k, :].rearrange("p (o i) -> p o i", o=4),
                                       cst16[0:R, k, :].unsqueeze(1).to_broadcast([R, 4, 4]), ALU.mult))
                link(dve.tensor_reduce(cst16[0:R, k + 1, :], cprod16[0:R, :].rearrange("p (o i) -> p o i", o=4), X_AXIS, ALU.add))
            link(dve.tensor_reduce(cnrm16[0:R, 0, :], cst16[0:R, 0:NC, :], X_AXIS, ALU.add, apply_absolute_value=True))
            link(dve.reciprocal(cnrm16[0:R, 1, :], cnrm16[0:R, 0, :]))
            dve.tensor_tensor(cst16[0:R, 0:NC, :], cst16[0:R, 0:NC, :],
                              cnrm16[0:R, 1, :].unsqueeze(2).to_broadcast([R, NC, 4]), ALU.mult).then_inc(s["states_ready"], 1)
            dve.wait_ge(s["states_loaded"], 16)
            link(dve.tensor_scalar(cneg, cstate, -1.0, None, ALU.mult))
            flat = pseq.rearrange("p g i m -> p (g i) m")
            for term in range(4):
                for r in range(2):
                    for c in range(2):
                        a, im = term // 2, term % 2
                        src = flat[:, :, 4 * r + 2 * a + (c ^ im)]
                        sc = (cneg if im and not c else cstate)[:, r, term:term + 1]
                        dst = pval[:, 2 * r + c, :]
                        if term == 0:
                            link.mark(dve.tensor_scalar(dst, src, sc, None, ALU.mult))
                        else:
                            link.mark(dve.scalar_tensor_tensor(out=dst, in0=src, scalar=sc, in1=dst, op0=ALU.mult, op1=ALU.add))
                link.sync()
            pv = pval.rearrange("p (r c) (g i) -> p r c g i", r=2, g=2)

            def val(r, c, back):
                return pv[:, r, c, :, 2 - back:2 - back + SEG]

            def half(x, r):
                return cw[:, x, r, :].rearrange("p (g i) -> p g i", g=2)

            def both(f):
                for r in range(2):
                    link.mark(f(r))
                link.sync()

            both(lambda r: dve.scalar_tensor_tensor(out=half(0, r), in0=val(r, 0, 1), scalar=-1.0, in1=val(r, 0, 1), op0=ALU.mult, op1=ALU.max))
            both(lambda r: dve.scalar_tensor_tensor(out=half(1, r), in0=val(r, 1, 1), scalar=-1.0, in1=val(r, 1, 1), op0=ALU.mult, op1=ALU.max))
            link(dve.tensor_tensor(cw[:, 0], cw[:, 0], cw[:, 1], ALU.add))
            link(dve.reciprocal(cw[:, 1], cw[:, 0]))
            for c in range(2):
                both(lambda r: dve.tensor_tensor(half(2 + c, r), val(r, c, 1), half(1, r), ALU.mult))
                both(lambda r: dve.tensor_tensor(half(4 + c, r), val(r, c, 0), half(1, r), ALU.mult))
            qr, qi, pr, pi = cw[:, 2], cw[:, 3], cw[:, 4], cw[:, 5]
            link.mark(dve.tensor_tensor(cw[:, 6], qr, qr, ALU.mult))
            link.mark(dve.tensor_tensor(cw[:, 7], qi, qi, ALU.mult))
            link.mark(dve.tensor_tensor(cw[:, 8], pr, qr, ALU.mult))
            link.mark(dve.tensor_tensor(cw[:, 9], pi, qi, ALU.mult))
            link.sync()
            link.mark(dve.tensor_tensor(cw[:, 6], cw[:, 6], cw[:, 7], ALU.add))
            link.mark(dve.tensor_tensor(cw[:, 8], cw[:, 8], cw[:, 9], ALU.add))
            link.sync()
            link.mark(dve.tensor_tensor(cw[:, 7], pi, qr, ALU.mult))
            link.mark(dve.tensor_tensor(cw[:, 9], pr, qi, ALU.mult))
            link.mark(dve.reciprocal(cw[:, 0], cw[:, 6]))
            link.sync()
            link.mark(dve.tensor_tensor(cw[:, 7], cw[:, 7], cw[:, 9], ALU.subtract))
            link.mark(dve.tensor_tensor(cw[:, 1], cw[:, 8], cw[:, 0], ALU.mult))
            link.sync()
            link(dve.tensor_tensor(cw[:, 2], cw[:, 7], cw[:, 0], ALU.mult))
            for x, dst in ((1, 3), (2, 4)):
                link.mark(dve.tensor_tensor(cw[:, dst, 0, :], cw[:, x, 0, :], cw[:, x, 1, ::-1], ALU.add))
            link.sync()
            link.mark(dve.tensor_tensor(cw[:, 3, 0, :], cw[:, 3, 0, :], u, ALU.subtract))
            link.mark(dve.tensor_tensor(cw[:, 4, 0, :], cw[:, 4, 0, :], gm, ALU.add))
            link.sync()
            sr, si = cw[:, 3, 0, :], cw[:, 4, 0, :]
            link.mark(dve.tensor_tensor(cw[:, 5, 0, :], sr, sr, ALU.mult))
            link.mark(dve.tensor_tensor(cw[:, 6, 0, :], si, si, ALU.mult))
            link.sync()
            link(dve.tensor_tensor(cw[:, 5, 0, :], cw[:, 5, 0, :], cw[:, 6, 0, :], ALU.add))
            link(dve.reciprocal(cw[:, 6, 0, :], cw[:, 5, 0, :]))
            link(dve.tensor_tensor(green[:, 0, :], sr, cw[:, 6, 0, :], ALU.mult))
            dve.scalar_tensor_tensor(out=green[:, 1, :], in0=si, scalar=-1.0, in1=cw[:, 6, 0, :], op0=ALU.mult,
                                     op1=ALU.mult).then_inc(s["green_ready"], 1)
            dve.wait_ge(s["decC_exp_ready"], 1)
            link(dve.tensor_scalar(decC[:, :], sm[:, 8, :], ETA, None, ALU.mult))
            dve.memset(cneg[:, 0, 0:1], 0.0).then_inc(s["decC_ready"], 1)

            def norm_stats(x, stat, mv, ready):
                for j in range(TPS):
                    link.mark(dve.bn_stats(stat[:, j, :], x[:, j, :]))
                link.sync()
                apart(dve)
                for j in range(TPS):
                    ins = dve.bn_aggr(mv[:, j, :], stat[:, j, :])
                    if j < TPS - 1:
                        link.mark(ins)
                ins.then_inc(s[ready], 1)

            def normalise(dst, x, mv, rs, ready):
                for j in range(TPS):
                    ins = dve.tensor_scalar(dst[:, j, :], x[:, j, :], mv[:, j, 0:1], rs[:, j:j + 1], ALU.subtract, ALU.mult)
                    if j < TPS - 1:
                        link.mark(ins)
                ins.then_inc(s[ready], 1)

            def prepare(t):
                q = t.par
                if started(v := t.count(1, -1)):
                    dve.wait_ge(s["x2b_ready"], v)
                for j in range(TPS):
                    at = tile_at(t, j)
                    link.mark(dve.tensor_scalar(x2[q][:, j, :], X[:, at, :], sm[:, 0, at], sm[:, 4, at], ALU.subtract, ALU.mult))
                link.sync()
                dve.wait_ge(s["bk_mm"], t.count(1, 1))
                flat = x2[q][:, :, :].rearrange("p j d -> p (j d)")
                dve.tensor_tensor(flat, ps_t[:, :], flat, ALU.add).then_inc(s["x2_ready"], 1)
                dve.wait_ge(s["x2_ready"], t.count(1, 1))
                norm_stats(x2[q], stat, mv, "mv_ready")

            def prepare_norm(t):
                dve.wait_ge(s["rs_ready"], t.count(1, 1))
                normalise(xh[t.par], x2[t.par], mv, rs, "xh_ready")

            def finish(t):
                dve.wait_ge(s["wo_mm"], t.count(1, 1))
                if started(v := 1 + t.count()):
                    dve.wait_ge(s["xres_ready"], v)
                dve.tensor_tensor(x3[:, :, :].rearrange("p j d -> p (j d)"), ps_o[:, :],
                                  x2b[t.par][:, :, :].rearrange("p j d -> p (j d)"), ALU.add).then_inc(s["x3_ready"], 1)
                dve.wait_ge(s["x3_ready"], t.count(1, 1))
                norm_stats(x3, stat3, mv3, "mv3_ready")

            def finish_norm(t):
                dve.wait_ge(s["rs3_ready"], t.count(1, 1))
                normalise(x3h, x3, mv3, rs3, "xh3_ready")

            def finish_out(t):
                dve.wait_ge(s["ff2_mm"], t.count(1, 1))
                dve.wait_ge(s["xres_ready"], 1 + t.count(1, 1))
                dve.tensor_tensor(X[:, tiles(t), :], ps_o[:, :].rearrange("p (j d) -> p j d", j=TPS), xres[:, :, :], ALU.add)\
                    .then_inc(s["x1_ready"], 1)

            def tokens_evac(t):
                if started(v := t.count(TPS)):
                    dve.wait_ge(s["vdec_ready"], v)
                for n in range(2 * TPS):
                    m, val = n // 2, n % 2
                    dve.wait_ge(s["tok_mm"], t.count(2 * TPS, n + 1))
                    dve.tensor_tensor((vtok if val else ktok)[:, m, :], ps_p[n % 2][:, :], row("bv" if val else "bk"), ALU.add)\
                        .then_inc(s["tok_ready"], 1)

            def heb(t, route):
                def weigh(m):
                    dve.wait_ge(s["sc_mm"], t.count(TPS, m + 1))
                    dm = dmat[:, bass.ds(t.count(N, m * P), P)].unsqueeze(1).to_broadcast([P, PAIRS, P])
                    for o in range(2):
                        ins = dve.tensor_tensor(pT[m % 2][o], ps_s[o][:, :].rearrange("s (p t) -> s p t", p=PAIRS), dm, ALU.mult)
                        if o == 0:
                            link.mark(ins)
                    ins.then_inc(s["pT_ready"], 1)

                def store(m):
                    dve.wait_ge(s["u_mm"], t.count(TPS - 1, m + 1))
                    if m:
                        dve.wait_ge(s["w_ready"], t.count(TPS - 1, m))
                    for o in range(2):
                        h = slice(o * HD, (o + 1) * HD)
                        add = ps_u[h, :].rearrange("d (p e) -> d p e", p=PAIRS)[:, :, h]
                        if m == 0:
                            ins = dve.tensor_copy(wst[m][h, :, h], add)
                        else:
                            ins = dve.scalar_tensor_tensor(out=wst[m][h, :, h], in0=wst[m - 1][h, :, h],
                                                           scalar=decays[h, bass.ds(t.count(N, m * P + P - 1), 1)], in1=add,
                                                           op0=ALU.mult, op1=ALU.add)
                        if o == 0:
                            link.mark(ins)
                    ins.then_inc(s["w_ready"], 1)

                for m in range(TPS):
                    weigh(m)
                    if m < TPS - 1:
                        store(m)
                    if route and m == 0:
                        route_choose(t.at(-2), t.at(-2))
                    if route and m == 2:
                        route_slots(t.at(-2), t.at(-2))

            def route_stats(t, ts):
                for j in range(TPS):
                    link.mark(dve.bn_stats(rstat[:, ts.par, j, :], X[:, tile_at(t, j), :]))
                link.sync()
                apart(dve)
                for j in range(TPS):
                    ins = dve.bn_aggr(rmv[:, ts.par, j, :], rstat[:, ts.par, j, :])
                    if j < TPS - 1:
                        link.mark(ins)
                ins.then_inc(s["rmv_ready"], 1)

            def route_norm(t, ts):
                q = t.par
                dve.wait_ge(s["rrs_ready"], ts.count(1, 1))
                dve.wait_ge(s[f"scattered{q}"], ts.half(TPS * 2 * 16, SPARE))
                apart(dve)
                link.mark(dve.tensor_copy(pay[q][:, :, :, D].bitcast(I32), ids[:, tiles(t), :]))
                for j in range(TPS):
                    link.mark(dve.tensor_scalar(pay[q][:, j, 0, 0:D], X[:, tile_at(t, j), :], rmv[:, q, j, 0:1], rrs[:, q, j:j + 1],
                                                ALU.subtract, ALU.mult))
                link.sync()
                dve.sem_inc(s["pay_ready"], 1)

            def route_choose(t, ts):
                def wide(v):
                    return v.unsqueeze(2).to_broadcast([P, TPS, E_N])

                dve.wait_ge(s["score_mm"], 1 + ts.count(1, 1))
                link(dve.tensor_tensor(rt[:, 0], ps_o[:, 0:TPS * E_N].rearrange("p (j e) -> p j e", j=TPS),
                                       row("br").unsqueeze(1).to_broadcast([P, TPS, E_N]), ALU.add))
                for k in range(2):
                    sc, eq, pri, oh = rt[:, 4 * k], rt[:, 4 * k + 1], rt[:, 4 * k + 2], rt[:, 4 * k + 3]
                    link(dve.tensor_reduce(rv[:, k], sc, X_AXIS, ALU.max))
                    link(dve.tensor_tensor(eq, sc, wide(rv[:, k]), ALU.is_equal))
                    link(dve.tensor_tensor(pri, eq, C("rev").unsqueeze(1).to_broadcast([P, TPS, E_N]), ALU.mult))
                    link(dve.tensor_reduce(rv[:, 2], pri, X_AXIS, ALU.max))
                    link(dve.tensor_tensor(oh, pri, wide(rv[:, 2]), ALU.is_equal))
                    if k == 0:
                        link(dve.scalar_tensor_tensor(out=rt[:, 4], in0=oh, scalar=NEG_BIG, in1=sc, op0=ALU.mult, op1=ALU.add))
                dve.wait_ge(s["rank_mm"], 1 + ts.count())
                dve.wait_ge(s["e2_ready"], 1 + ts.count())
                link.mark(dve.tensor_tensor(rv[:, 3], rv[:, 1], rv[:, 0], ALU.subtract))
                link.mark(dve.tensor_tensor(rt[:, 8], rt[:, 3], rt[:, 7], ALU.add))
                link.sync()
                dve.sem_inc(s["m_ready"], 1)

            def route_slots(t, ts):
                q = t.par
                dve.wait_ge(s["rank_mm"], 1 + ts.count(1, 1))
                for j in range(TPS):
                    link(dve.tensor_tensor(cnt[:, j + 1, :], ps_o[:, 128 + j * E_N:128 + (j + 1) * E_N], cnt[:, j, :], ALU.add))
                link(dve.tensor_tensor(rt[:, 9], ps_o[:, 64:64 + TPS * E_N].rearrange("p (j e) -> p j e", j=TPS), cnt[:, 0:TPS, :], ALU.add))
                for k in range(2):
                    link.mark(dve.tensor_tensor(rt[:, 10 + k], rt[:, 3 + 4 * k], rt[:, 9], ALU.mult))
                link.mark(dve.tensor_copy(cnt[:, 0, :], cnt[:, TPS, :]))
                link.sync()
                link(dve.tensor_reduce(rsl[:, :, :], rt[:, 10:12], X_AXIS, ALU.add))
                dve.wait_ge(s[f"scattered{q}"], ts.half(TPS * 2 * 16, SPARE))
                apart(dve)
                dve.tensor_copy(slots[q], rsl[:, :, :]).then_inc(s["slots_ready"], 1)
                dve.wait_ge(s["e2_ready"], 1 + ts.count(1, 1))
                link(dve.tensor_scalar(rv[:, 5], rv[:, 4], 1.0, None, ALU.add))
                link(dve.reciprocal(wtok[:, 0, tiles(t)], rv[:, 5]))
                link.mark(dve.tensor_tensor(wtok[:, 1, tiles(t)], wtok[:, 0, tiles(t)], rv[:, 4], ALU.mult))

            def a_item(t, first=False, last=False, route=True):
                route = route and not first
                if not last:
                    prepare(t.at(1))
                if not first:
                    finish(t.at(-1))
                if route:
                    dve.wait_ge(s["x1_ready"], 1 + t.count(1, -1))
                    apart(dve)
                    route_stats(t.at(-2), t.at(-2))
                if not last:
                    prepare_norm(t.at(1))
                if not first:
                    finish_norm(t.at(-1))
                if route:
                    route_norm(t.at(-2), t.at(-2))
                tokens_evac(t)
                heb(t, route)
                if not first:
                    finish_out(t.at(-1))

            link(dve.tensor_copy(cnt[:, 0, :], C("ebase")))
            dve.wait_ge(s["pay_set"], 2)
            prepare(Turn(0))
            prepare_norm(Turn(0))
            a_loop(dve, a_item, link, PER_A)
            t = Turn(B - 1)
            finish(t)
            dve.wait_ge(s["x1_ready"], 1 + B - 1)
            route_stats(t.at(-1), t.at(-1))
            finish_norm(t)
            route_norm(t.at(-1), t.at(-1))
            route_choose(t.at(-1), t.at(-1))
            route_slots(t.at(-1), t.at(-1))
            finish_out(t)
            dve.wait_ge(s["x1_ready"], 1 + B)
            route_stats(t, t)
            route_norm(t, t)
            route_choose(t, t)
            route_slots(t, t)
            def tile_tables(layer):
                o = slice(0, 1)
                link(dve.tensor_copy(tail_row[o, :], cnt[o, TPS, :]))
                link(dve.tensor_tensor(tl[o, 0, :], cnt[o, TPS, :], C("ebase")[o, :], ALU.subtract))
                link(dve.tensor_tensor(tlk[o], tl[o, 0, :].unsqueeze(2).to_broadcast([1, E_N, 16]),
                                       C("kthr")[o, :].unsqueeze(1).to_broadcast([1, E_N, 16]), ALU.is_gt))
                link(dve.tensor_reduce(tl[o, 1, :], tlk[o], X_AXIS, ALU.add))
                link(dve.tensor_tensor_scan(tl[o, 2, :], C("ones")[o, 0:E_N], tl[o, 1, :], 0.0, ALU.mult, ALU.add))
                wide = [1, MAX_TILES, E_N]
                link(dve.tensor_tensor(tlj[o], C("jj")[o, :].unsqueeze(2).to_broadcast(wide),
                                       tl[o, 2, :].unsqueeze(1).to_broadcast(wide), ALU.is_ge))
                link(dve.tensor_reduce(tlr[o, 0, :], tlj[o], X_AXIS, ALU.add))
                link(dve.tensor_tensor(tlj[o], tlj[o], tl[o, 1, :].unsqueeze(1).to_broadcast(wide), ALU.mult))
                link(dve.tensor_reduce(tlr[o, 1, :], tlj[o], X_AXIS, ALU.add))
                link(dve.tensor_tensor(tlr[o, 1, :], C("jj")[o, :], tlr[o, 1, :], ALU.subtract))
                link(dve.tensor_scalar(tlr[o, 1, :], tlr[o, 1, :], float(TT), None, ALU.mult))
                link(dve.scalar_tensor_tensor(out=tlr[o, 2, :], in0=tlr[o, 0, :], scalar=float(CAP), in1=tlr[o, 1, :],
                                              op0=ALU.mult, op1=ALU.add))
                link(dve.tensor_scalar(tlr[o, 3, :], tlr[o, 0, :], float(E_N - 1), None, ALU.min))
                link(dve.tensor_copy(tile_row[o, :], tlr[o, 2, :]))
                dve.tensor_copy(tile_e[o, :], tlr[o, 3, :]).then_inc(s["tables_ready"], 1)

            def experts(layer):
                link.sync()
                tile_tables(layer)

                def result(j, js):
                    q = j.par
                    dve.wait_ge(s["y_mm"], js.count(1, 1))
                    dve.wait_ge(s[f"ewt_loaded{j.quad}"], loads(j, layer, 32))
                    if started(v := j.half(32, layer * RETURNS[q])):
                        dve.wait_ge(s[f"returned{q}"], v)
                    dve.tensor_tensor(ey[q], (ps_o, ps_h)[q][:, 0:TH * D].rearrange("p (h d) -> p h d", h=TH),
                                      eb2[j.quad].unsqueeze(1).to_broadcast([P, TH, D]), ALU.add).then_inc(s["ey_ready"], 1)

                def keep_back_row(j, js):
                    dve.wait_ge(s[f"ex_loaded{j.quad}"], loads(j, layer, 16))
                    dve.tensor_copy(back_row[j.quad], ex[j.quad][:, :, D].bitcast(I32)).then_inc(s["back_row_ready"], 1)

                tile_loop(dve, result, layer, ahead=keep_back_row)

            def combine(b, layer):
                q = b % 4
                dve.wait_ge(s[f"back_loaded{q}"], 32 * (layer * B // 4 + b // 4 + 1))
                for k in range(2):
                    for j in range(TPS):
                        at = b * TPS + j
                        link.mark(dve.scalar_tensor_tensor(out=X[:, at, :], in0=yb[q][k][:, j, :], scalar=wtok[:, k, at:at + 1],
                                                           in1=X[:, at, :], op0=ALU.mult, op1=ALU.add))
                    link.sync()
                dve.sem_inc(s["combined"], 1)

            experts(0)

            def scan_stats(n):
                for q in range(2):
                    for j in range(TPS):
                        link.mark(dve.bn_stats(gstat[:, q, j, :], X[:, tile_at(Turn(q, n), j), :]))
                link.sync()
                apart(dve)
                for q in range(2):
                    for j in range(TPS):
                        link.mark(dve.bn_aggr(gmv[:, q, j, :], gstat[:, q, j, :]))
                link.sync()
                dve.sem_inc(s["gmv_ready"], 1)

            def scan_norm(t):
                q = t.par
                dve.wait_ge(s["grs_ready"], t.half(1, 1))
                if started(v := t.count(1, -1)):
                    dve.wait_ge(s["gt_mm"], v)
                for j in range(TPS):
                    link.mark(dve.tensor_scalar(x2[q][:, j, :], X[:, tile_at(t, j), :], gmv[:, q, j, 0:1], gr[:, 1, q, j:j + 1],
                                                ALU.subtract, ALU.mult))
                link.sync()
                for j in range(TPS):
                    link.mark(dve.tensor_scalar(xh[q][:, j, :], x2[q][:, j, :], gr[:, 2, q, j:j + 1], None, ALU.mult))
                link.sync()
                dve.sem_inc(s["gxh_ready"], 1)
                link(dve.tensor_tensor(X[:, tiles(t), :], X[:, tiles(t), :], x2[q][:, :, :], ALU.add))

            def scan_scan(t):
                dve.wait_ge(s["gdt_ready"], t.half(1, 1))
                link(dve.tensor_scalar(am, dtm, -1.0, 1.0, ALU.mult, ALU.add))
                dve.wait_ge(s["gut_ready"], t.half(1, 1))
                link(dve.tensor_tensor(bm, dtm, ut, ALU.mult))
                link(dve.tensor_tensor_scan(hm, am, bm, 0.0, ALU.mult, ALU.add))
                dve.wait_ge(s["gsg_ready"], t.half(1, 1))
                if started(v := t.count()):
                    dve.wait_ge(s["gout_mm"], v)
                dve.tensor_tensor(ym, hm, sg, ALU.mult).then_inc(s["gy_ready"], 1)

            def scan_out(t):
                dve.wait_ge(s["gout_mm"], t.count(1, 1))
                dve.tensor_tensor(X[:, tiles(t), :], (ps_o, ps_h)[t.par][:, :].rearrange("p (j d) -> p j d", j=TPS),
                                  X[:, tiles(t), :], ALU.add).then_inc(s["scanned"], 1)

            def route_item(r):
                nxt, now = Turn(r + 1), Turn(r)
                if r >= 0:
                    route_choose(now, now.at(B))
                if r < B - 1:
                    route_norm(nxt, nxt.at(B))
                if r >= 0:
                    route_slots(now, now.at(B))

            link(dve.tensor_copy(cnt[:, 0, :], C("ebase")))
            for b in range(2):
                combine(b, 0)
            scan_stats(0)
            for p in range(B // 2 + 1):
                if p < B // 2:
                    for q in range(2):
                        scan_norm(Turn(2 * p + q))
                if p < B // 2 - 1:
                    for q in range(2):
                        combine(2 * p + 2 + q, 0)
                    scan_stats(p + 1)
                if p:
                    for q in range(2):
                        scan_out(Turn(2 * p - 2 + q))
                    dve.wait_ge(s["scanned"], 2 * p)
                    for q in range(2):
                        route_stats(Turn(2 * p - 2 + q), Turn(B + 2 * p - 2 + q))
                if p < B // 2:
                    scan_scan(Turn(2 * p))
                for r in routed_in(p):
                    route_item(r)
            experts(1)
            for b in range(B):
                combine(b, 1)


def kernel(**inputs):
    import numpy as np
    import concourse.bacc as _bacc
    from concourse import mybir as _mybir
    from concourse.bass_utils import run_bass_kernel_spmd as _run

    a = {k: np.asarray(v) for k, v in inputs.items()}
    A, G, M = "L0_attn_a_", "L0_attn_b_", "L0_ffn_"

    def chunks(w, n):
        return w.reshape(n, P, -1).transpose(1, 0, 2).reshape(P, -1)

    def pack(parts, widths, height):
        assert [p.shape for p in parts.values()] == [(height, w) for w in widths.values()] and list(parts) == list(widths)
        return np.ascontiguousarray(np.concatenate(list(parts.values()), axis=1))

    hh = H * HD
    wqkv, bqkv = a[A + "w_qkv"], a[A + "b_qkv"]
    b_pot = np.zeros((P, 1), np.float32)
    b_pot[0:2, 0] = a[A + "b_pot"]
    one = lambda v: v.reshape(P, 1)
    col = lambda v: v.reshape(-1, P).T
    cols = pack(dict(
        w_pot=a[A + "w_pot"], g1=one(a[A + "ln1_g"]), b1=one(a[A + "ln1_b"]), g2=one(a[A + "ln2_g"]), b2=one(a[A + "ln2_b"]),
        g3=one(a[A + "ln3_g"]), b3=one(a[A + "ln3_b"]), bq=col(bqkv[0:hh]), bk=col(bqkv[hh:2 * hh]), bff1=col(a[A + "b_ff1"]),
        norm_w=one(a[G + "norm_w"]), b_uz=one(a[G + "b_in"][0:2 * S]), b_g=one(np.tile(a[G + "b_in"][2 * S:], 2)),
        b_x=one(np.tile(a[G + "b_x"], 2)), b_dt=one(np.tile(a[G + "b_dt"], 2)), b_pot=b_pot), COLS_W, P)
    rows = pack(dict(bk=bqkv[None, hh:2 * hh], bv=bqkv[None, 2 * hh:], b_out=a[A + "b_out"][None], b_ff2=a[A + "b_ff2"][None],
                     b_outb=a[G + "b_out"][None], br=a[M + "br"][None]), ROWS_W, 1)
    wts = pack(dict(q=wqkv[:, 0:hh], k=wqkv[:, hh:2 * hh], v=wqkv[:, 2 * hh:], w_out=chunks(a[A + "w_out"], PAIRS), ff1=a[A + "w_ff1"],
                    ff2=chunks(a[A + "w_ff2"], FC), w_in=a[G + "W_in"], w_xdt=np.concatenate([a[G + "W_x"], a[G + "W_dt"]]),
                    w_outb=np.tile(a[G + "W_out"], (2, 1)), wr=a[M + "Wr"]), WTS_W, P)
    wbk = np.concatenate([a[A + "w_bk"], a[A + "b_bk"][None]])
    experts = np.stack([pack(dict(w1=a[M + "W1"][e], w2=chunks(a[M + "W2"][e], FC), b1=col(a[M + "b1"][e])), EXP_W, P)
                        for e in range(E_N)])
    f32 = np.float32
    k, e = np.arange(P), np.arange(E_N)
    every = lambda v: np.broadcast_to(np.asarray(v, f32), (P, len(v)))
    consts = pack(dict(ident=np.eye(P, dtype=f32), ones=np.ones((P, P), f32), before=(k[:, None] < k).astype(f32),
                       mask=np.where(k[:, None] <= k, f32(ETA), f32(0)), rev=every(E_N - e), ebase=every(e * CAP),
                       kthr=every(np.arange(16) * TT), jj=every(np.arange(MAX_TILES))), CONST_W, P)
    token = (np.arange(B)[None, :, None] * N + k[:, None, None] * TPS + np.arange(TPS)[None, None, :]).reshape(P, NT)
    ids = np.stack([token, token + B * N], axis=-1).astype(np.int32)
    tail = np.zeros((P, ROW), np.int32)
    tail[:, D] = NOWHERE
    arrays = dict(x_in=np.ascontiguousarray(a[A + "x"].reshape(B, P, TPS, D)), consts=consts, ids_in=ids, tail_in=tail, cols_in=cols,
                  rows_in=rows, wts_in=wts, wbk_in=wbk, experts_in=experts, eb2_in=a[M + "b2"])
    nc = _bacc.Bacc("TRN2", target_bir_lowering=False, num_devices=1)
    args = {n: nc.dram_tensor(n, v.shape, _mybir.dt.from_np(v.dtype), kind="ExternalInput").ap() for n, v in arrays.items()}
    out = nc.dram_tensor("out", (B, P, TPS, D), F32, kind="ExternalOutput").ap()
    hybrid_kernel(nc, **args, out=out)
    r = _run(nc, [arrays], core_ids=[0])
    return r.results[0]["out"].reshape(B, N, D)
```

```python
from contextlib import ExitStack

import concourse.bass as bass
from concourse import mybir

F32 = mybir.dt.float32
I32 = mybir.dt.int32
F32R = mybir.dt.float32r
ALU = mybir.AluOpType
ACT = mybir.ActivationFunctionType
X_AXIS = mybir.AxisListType.X

B, N, D = 8, 512, 128
P = 128
TPS = N // P
NT = B * TPS
H, HD = 8, 64
PAIRS = H // 2
FF = 512
FC = FF // P
ETA, DT, GAMMA_FLOOR, EPS = 0.1, 0.01, 0.1, 1e-5
RMS_EPS = 1e-8
S = 64
E_N = 8
CH = 32
NC = N // CH
SEG = CH // 2
TT = 256
TH = TT // P
CAP = B * N + TT
MAX_TILES = 2 * B * N // TT + E_N - 1
MIN_TILES = 2 * B * N // TT
ROW = 132
ROWS_X = E_N * CAP + (MAX_TILES - MIN_TILES) * TT
NOWHERE = 1 << 20
NEG_BIG = -3e38

CONST_W = dict(ident=P, ones=P, before=P, mask=P, rev=E_N, ebase=E_N, kthr=16, jj=MAX_TILES)
COLS_W = dict(w_pot=2, g1=1, b1=1, g2=1, b2=1, g3=1, b3=1, bq=PAIRS, bk=PAIRS, bff1=FC, norm_w=1,
              b_uz=1, b_g=1, b_x=1, b_dt=1, b_pot=1)
ROWS_W = dict(bk=H * HD, bv=H * HD, b_out=D, b_ff2=D, b_outb=D, br=E_N)
WTS_W = dict(q=H * HD, k=H * HD, v=H * HD, w_out=PAIRS * D, ff1=FF, ff2=FC * D, w_in=3 * S, w_xdt=S, w_outb=D, wr=E_N)
EXP_W = dict(w1=FF, w2=FC * D, b1=FC)


def offsets(widths):
    at, out = 0, {}
    for name, w in widths.items():
        out[name] = (at, at + w)
        at += w
    return out, at


CONST_AT, CONST_N = offsets(CONST_W)
COLS_AT, COLS_N = offsets(COLS_W)
ROWS_AT, ROWS_N = offsets(ROWS_W)
WTS_AT, WTS_N = offsets(WTS_W)
EXP_AT, EXP_N = offsets(EXP_W)


WORK = 20856
PARAM_LOADS = 6
PER_A = 2 * 64
AHEAD = 4
TILES_OF = [len(range(q, MAX_TILES, AHEAD)) for q in range(AHEAD)]
SPARE = 16
RETURNS = [len(range(q, MAX_TILES, 2)) * TH * 16 for q in range(2)]


class Turn:

    def __init__(self, k, n=None, unroll=2):
        self.k, self.n, self.unroll = k, n, unroll

    def at(self, d):
        return Turn(self.k + d, self.n, self.unroll)

    @property
    def par(self):
        return self.k % 2

    @property
    def quad(self):
        return self.k % AHEAD

    def count(self, each=1, more=0):
        if self.n is None:
            return each * self.k + more
        return self.n * (self.unroll * each) + (each * self.k + more)

    def part(self, of, each=1, more=0):
        if self.n is None:
            return each * (self.k // of) + more
        return self.n * (self.unroll // of * each) + (each * (self.k // of) + more)

    def half(self, each=1, more=0):
        return self.part(2, each, more)


class Link:

    def __init__(self, eng, sem):
        self.eng, self.sem, self.base, self.k = eng, sem, 0, 0

    def mark(self, ins):
        ins.then_inc(self.sem, 1)
        self.k += 1

    def sync(self):
        self.eng.wait_ge(self.sem, self.base + self.k)

    def __call__(self, ins):
        self.mark(ins)
        self.sync()

    def enter(self, n, per, first):
        self.start, self.per = self.base + self.k, per
        self.base, self.k = n * per + (self.start - first * per), 0

    def leave(self, passes):
        assert self.k == self.per, f"a pass adds {self.k}, not {self.per}"
        self.base, self.k = self.start + passes * self.per, 0


def hybrid_kernel(nc, x_in, consts, ids_in, tail_in, cols_in, rows_in, wts_in, wbk_in, experts_in, eb2_in, out):
    def dram(name, shape, dt=F32):
        return nc.dram_tensor(name, shape, dt, kind="Internal").ap()

    pot_d = dram("pot_d", (2, B * N))
    gamma_d = dram("gamma_d", (B * N,))
    csum_d = dram("csum_d", (B * N,))
    maps_d = dram("maps_d", (2, B, NC, 16))
    states_d = dram("states_d", (2, B, NC, 4))
    green_d = dram("green_d", (2, B * N))
    routed_d = dram("routed_d", (ROWS_X, ROW))
    back_d = dram("back_d", (2 * B * N, D))

    with ExitStack() as ctx:
        def sb(name, shape, dt=F32):
            return ctx.enter_context(nc.sbuf_tensor(name, shape, dt))

        def sem(name):
            return ctx.enter_context(nc.semaphore(name))

        cst = sb("cst", [P, CONST_N])
        ids = sb("ids", [P, NT, 2], I32)
        tail = sb("tail", [P, ROW], I32)
        cols = sb("cols", [P, COLS_N])
        rows = sb("rows", [P, ROWS_N])
        wts = sb("wts", [P, WTS_N])
        wbk = sb("wbk", [3, D])
        w_hi, w_lo = (sb(n, [P, 3 * H * HD], F32R) for n in ("w_hi", "w_lo"))
        x3T, *rxT = (wts[:, k * N:(k + 1) * N] for k in range(3))

        def C(name):
            a, b = CONST_AT[name]
            return cst[:, a:b]

        def col(name, i=0):
            a, _ = COLS_AT[name]
            return cols[:, a + i:a + i + 1]

        def row(name):
            a, b = ROWS_AT[name]
            return rows[:, a:b]

        def W(name, a=0, b=None):
            lo, hi = WTS_AT[name]
            return wts[:, lo + a:hi if b is None else lo + b]

        def W_parts(name, a=0, b=H * HD):
            lo = WTS_AT[name][0]
            return w_hi[:, lo + a:lo + b], w_lo[:, lo + a:lo + b]

        def passes(pe, dst, lhsT, rhs):
            pe.matmul(dst, lhsT[0], rhs[1], start=True, stop=False)
            pe.matmul(dst, lhsT[1], rhs[0], start=False, stop=False)
            return pe.matmul(dst, lhsT[0], rhs[0], start=False, stop=True)

        ident = C("ident")

        X = sb("X", [P, NT, D])
        decays = sb("decays", [P, B * N])
        dmat = sb("dmat", [P, B * N])
        decC = sb("decC", [P, NT])
        sm = sb("sm", [P, 10, NT])
        powc = sb("powc", [P, NT])
        gt = [sb(f"gt{q}", [3, N]) for q in range(2)]
        x2 = [sb(f"x2{q}", [P, TPS, D]) for q in range(2)]
        x2b = [sb(f"x2b{q}", [P, TPS, D]) for q in range(2)]
        xh = [sb(f"xh{q}", [P, TPS, D]) for q in range(2)]
        xnT = [sb(f"xnT{q}", [P, N]) for q in range(2)]
        xnT_hi, xnT_lo = (sb(n, [P, N], F32R) for n in ("xnT_hi", "xnT_lo"))
        xres, x3, x3h = (sb(n, [P, TPS, D]) for n in ("xres", "x3", "x3h"))
        stat, stat3 = sb("stat", [P, TPS, 6]), sb("stat3", [P, TPS, 6])
        mv, mv3 = sb("mv", [P, TPS, 2]), sb("mv3", [P, TPS, 2])
        ve, ve3 = sb("ve", [P, TPS]), sb("ve3", [P, TPS])
        rs, rs3 = sb("rs", [P, TPS]), sb("rs3", [P, TPS])
        pay = [sb(f"pay{q}", [P, TPS, 2, ROW])[:, :, :, :] for q in range(2)]
        for q in range(2):
            n = TPS * 2 * ROW
            pay.append(dmat[:, q * n:(q + 1) * n].rearrange("p (j k r) -> p j k r", j=TPS, k=2))
        wtok = sb("wtok", [P, 2, NT])
        dtok = sb("dtok", [P, NT])
        etok = sb("etok", [P, NT])
        slots = sb("slots", [P, 4, 2, TPS], I32)
        cadd, csum, crun = (sb(n, [P, E_N, 2 * TPS + 1]) for n in ("cadd", "csum", "crun"))

        pool = sb("work", [P, WORK])
        used = [0]

        def carve(*shape, dt=F32):
            n = 1
            for s in shape:
                n *= s
            a = used[0]
            used[0] = a + n
            assert used[0] <= WORK, used[0]
            v = pool[:, a:a + n]
            if dt is not F32:
                v = v.bitcast(dt)
            names = " ".join("abcde"[:len(shape)])
            return v.rearrange(f"p ({names}) -> p {names}", **dict(zip("abcde", shape))) if len(shape) > 1 else v

        st1 = carve(NT, 6)
        cf = carve(6, CH)
        dre, dim2 = carve(CH, 2), carve(CH, 2, 2)
        pseq = carve(2, SEG + 2, 8)
        cstep, cnrm = carve(2, 8), carve(2, 2)
        cmap, cstate, cneg = carve(2, 16), carve(2, 4), carve(2, 4)
        cmap16, cst16, cprod16, cnrm16 = carve(NC, 16), carve(NC + 1, 4), carve(16), carve(2, NC)
        pval = carve(4, 2 * (SEG + 2))
        cw = carve(10, 2, CH)
        green = carve(2, CH)
        gw, potT, potb = carve(2), carve(B * N), carve(1)
        csr, csr2, csT = carve(P), carve(P), carve(NT)
        used[0] = 0
        qT, kT, qd = carve(PAIRS, N), carve(PAIRS, N), carve(PAIRS, N)
        ktok, vtok, vdec = carve(TPS, H * HD), carve(TPS, H * HD), carve(TPS, H * HD)
        pT = [[carve(PAIRS, P) for _ in range(2)] for _ in range(2)]
        wst = [carve(PAIRS, P) for _ in range(TPS - 1)]
        hebT, hff = carve(PAIRS, N), carve(FC, N)
        rt, rv = carve(12, 2 * TPS, E_N), carve(3, 2 * TPS)
        rsl = carve(2, 2 * TPS)
        rstat, rmv, rve, rrs = carve(2, TPS, 6), carve(2, TPS, 2), carve(2, TPS), carve(2, TPS)
        used[0] = 0
        tl, tlk, tlj, tlr = carve(4, E_N), carve(E_N, 16), carve(MAX_TILES, E_N), carve(4, MAX_TILES)
        tile_e, tile_row, tail_row = carve(MAX_TILES, dt=I32), carve(MAX_TILES, dt=I32), carve(E_N, dt=I32)
        ewt = [carve(EXP_N) for _ in range(4)]
        eb2 = [carve(D) for _ in range(4)]
        ex = [carve(TH, ROW) for _ in range(4)]
        back_row = [carve(TH, dt=I32) for _ in range(4)]
        w1_hi, w1_lo = ([w[:, q * FF:(q + 1) * FF] for q in range(2)] for w in (w_hi, w_lo))
        exT_hi, exT_lo = ([w[:, 2 * FF + q * TT:2 * FF + (q + 1) * TT] for q in range(2)] for w in (w_hi, w_lo))
        ehT = [carve(FC, TT) for _ in range(2)]
        ey = [carve(TH, D) for _ in range(2)]
        yb = [[carve(TPS, D) for _ in range(2)] for _ in range(4)]
        gstat = carve(2, TPS, 6)
        gmv, gr = ([carve(*s) for _ in range(2)] for s in ((2, TPS, 2), (4, 2, TPS)))
        uz = [carve(N) for _ in range(2)]
        sg, ut, dtm, am, bm, hm, ym = (carve(N) for _ in range(7))

        psb = [ctx.enter_context(nc.psum_tensor(f"ps{i}", [P, 512], F32)) for i in range(8)]
        ps_t, ps_p, ps_s, ps_h, ps_u, ps_o = psb[0], psb[1:3], psb[3:5], psb[5], psb[6], psb[7]

        ps_in = [*ps_p, *ps_s]

        class Sems(dict):
            def __missing__(self, name):
                self[name] = sem(name)
                return self[name]

        s = Sems()

        def started(value):
            return not isinstance(value, int) or value > 0

        def apart(eng):
            eng.sem_inc(s["passed"], 1)

        def pairs_of(eng, body, items, first=2, link=None, per=0, shift=0):
            for k in range(first):
                body(Turn(k), Turn(k + shift))
            with eng.Fori(first // 2, items // 2) as n:
                if link:
                    link.enter(n, per, first // 2)
                for u in range(2):
                    body(Turn(u, n), Turn(u + shift, n))
            if link:
                link.leave(items // 2 - first // 2)

        def a_loop(eng, item, link=None, per=0):
            item(Turn(0), first=True)
            item(Turn(1), route=False)
            with eng.Fori(1, B // 2 - 1) as n:
                if link:
                    link.enter(n, per, 1)
                for u in range(2):
                    item(Turn(u, n))
            if link:
                link.leave(B // 2 - 2)
            item(Turn(B - 2))
            item(Turn(B - 1), last=True)

        def tile_loop(eng, body, layer, ahead=None, behind=None, peel=2):
            def step(k, n=None, first=False, last=False):
                j = Turn(k, n, AHEAD)
                js = j.at(layer * MAX_TILES)
                if body:
                    body(j, js)
                if ahead and not last:
                    ahead(j.at(1), js.at(1))
                if behind and not first:
                    behind(j.at(-1), js.at(-1))

            if ahead:
                ahead(Turn(0), Turn(layer * MAX_TILES))
            for k in range(peel):
                step(k, first=(k == 0))
            passes = (MAX_TILES - peel) // AHEAD
            with eng.Fori(0, passes) as n:
                for u in range(AHEAD):
                    step(peel + u, n)
            for k in range(peel + passes * AHEAD, MAX_TILES):
                step(k, last=(k == MAX_TILES - 1))
            if behind:
                behind(Turn(MAX_TILES - 1), Turn((layer + 1) * MAX_TILES - 1))

        def pay_of(ts):
            return ts.k % 4 if ts.n is None and ts.k >= B else ts.par

        def scattered_before(ts):
            each = TPS * 2 * 16
            if ts.n is None and ts.k >= B:
                return (SPARE + B // 2 * each if pay_of(ts) < 2 else 0) + (ts.k - B) // 4 * each
            return ts.half(each, SPARE)

        def scattered_in_all(layer, q):
            each = TPS * 2 * 16
            return (SPARE + B // 2 * each if q < 2 else 0) + (layer * B // 4 * each)

        def loads(j, layer, each):
            return j.part(AHEAD, each, each * (1 + layer * TILES_OF[j.quad]))

        block = ctx.enter_context(nc.Block())

        def tiles(t):
            return bass.ds(t.count(TPS), TPS)

        def tile_at(t, j):
            return bass.ds(t.count(TPS, j), 1)

        def t_order(ap):
            return ap.rearrange("d (p j) -> d j p", j=TPS)

        @block.sync
        def _(sp):
            for b in range(B):
                sp.dma_start(X[:, b * TPS:(b + 1) * TPS, :], x_in[b]).then_inc(s[f"x_loaded{b}"], 16)

            sp.wait_ge(s["pot_ready"], 1 + B)
            sp.dma_start(pot_d, potT[0:2, :]).then_inc(s["pot_stored"], 16)
            sp.wait_ge(s["pot_stored"], 16)
            sp.dma_start(cf[:, 0:2, :], pot_d.rearrange("k (p i) -> p k i", i=CH)).then_inc(s["pot_chunked"], 16)
            sp.wait_ge(s["gamma_ready"], 1)
            sp.dma_start(gamma_d.rearrange("(p i) -> p i", i=CH), cf[:, 5, :]).then_inc(s["gamma_stored"], 16)
            sp.wait_ge(s["gamma_stored"], 16)
            sp.dma_start(csr[0:NT, :], gamma_d.rearrange("(c i) -> c i", i=P)).then_inc(s["csr_loaded"], 16)
            sp.wait_ge(s["csum_ready"], 1)
            sp.dma_start(csum_d.rearrange("(c i) -> c i", i=P), csr2[0:NT, :]).then_inc(s["csum_stored"], 16)
            sp.wait_ge(s["csum_stored"], 16)
            sp.dma_start(decays[:, :], csum_d.rearrange("(a n) -> a n", a=1).to_broadcast([P, B * N]))\
                .then_inc(s["csum_spread"], 16)
            sp.wait_ge(s["maps_ready"], 1)
            sp.dma_start(maps_d.rearrange("r b k m -> (b k) r m"), cmap[:, :, :]).then_inc(s["maps_stored"], 16)
            sp.wait_ge(s["maps_stored"], 16)
            sp.dma_start(cmap16[0:B], maps_d[0]).then_inc(s["maps_loaded"], 16)
            sp.dma_start(cmap16[B:2 * B, ::-1, :], maps_d[1]).then_inc(s["maps_loaded"], 16)
            sp.wait_ge(s["states_ready"], 1)
            sp.dma_start(states_d[0], cst16[0:B, 0:NC, :]).then_inc(s["states_stored"], 16)
            sp.dma_start(states_d[1], cst16[B:2 * B, NC - 1::-1, :]).then_inc(s["states_stored"], 16)
            sp.wait_ge(s["states_stored"], 32)
            sp.dma_start(cstate[:, :, :], states_d.rearrange("r b k m -> (b k) r m")).then_inc(s["states_loaded"], 16)
            sp.wait_ge(s["green_ready"], 1)
            sp.dma_start(green_d.rearrange("k (p i) -> p k i", i=CH), green).then_inc(s["green_stored"], 16)
            sp.wait_ge(s["green_stored"], 16)
            def load_green(t):
                if started(v := t.count(1, -1)):
                    sp.wait_ge(s["bk_mm"], v)
                src = green_d[:, bass.ds(t.count(N), N)]
                sp.dma_start(gt[t.par][0:2, :], src).then_inc(s[f"gt_loaded{t.par}"], 16)

            sp.wait_ge(s["ones_set"], 2)
            load_green(Turn(0))
            load_green(Turn(1))
            with sp.Fori(0, (B - 2) // 2) as n:
                for u in range(2):
                    load_green(Turn(2 + u, n))
            def expert_tiles(layer):
                sp.wait_ge(s["tables_ready"], layer + 1)
                for e in range(E_N):
                    at = sp.value_load(tail_row[0:1, e:e + 1], min_val=e * CAP, max_val=e * CAP + B * N)
                    sp.dma_start(routed_d[bass.ds(at, TT), :].rearrange("(h p) r -> p h r", p=P),
                                 tail[:, :].bitcast(F32).unsqueeze(1).to_broadcast([P, TH, ROW]))\
                        .then_inc(s["tails_filled"], 16)
                def load_weights(j, js):
                    q = j.quad
                    e = sp.value_load(tile_e[0:1, bass.ds(j.count(), 1)], min_val=0, max_val=E_N - 1)
                    if started(v := js.count(1, -3)):
                        sp.wait_ge(s["y_mm"], v)
                    apart(sp)
                    sp.dma_start(ewt[q][:, :], experts_in[bass.ds(e, 1)].rearrange("a p c -> (a p) c")).then_inc(s[f"ewt_loaded{q}"], 16)
                    if started(v := 1 + js.count(1, -3)):
                        sp.wait_ge(s["ey_ready"], v)
                    apart(sp)
                    sp.dma_start(eb2[q][:, :], eb2_in[bass.ds(e, 1), :].to_broadcast([P, D])).then_inc(s[f"ewt_loaded{q}"], 16)

                def load(j, js):
                    q = j.quad
                    r = sp.value_load(tile_row[0:1, bass.ds(j.count(), 1)], min_val=0, max_val=ROWS_X - TT)
                    if started(v := js.count(1, -3)):
                        sp.wait_ge(s["et_mm"], v)
                    apart(sp)
                    if started(v := js.count(1, -3)):
                        sp.wait_ge(s["back_row_ready"], v)
                    apart(sp)
                    sp.dma_start(ex[q][:, :, :], routed_d[bass.ds(r, TT), :].rearrange("(h p) r -> p h r", p=P))\
                        .then_inc(s[f"ex_loaded{q}"], 16)
                    if j.n is not None or j.k >= 2:
                        load_weights(j, js)

                for k in range(2):
                    load_weights(Turn(k), Turn(layer * MAX_TILES + k))
                sp.wait_ge(s["tails_filled"], (layer + 1) * E_N * 16)
                for q in range(4 if layer else 2):
                    sp.wait_ge(s[f"scattered{q}"], scattered_in_all(layer, q))

                tile_loop(sp, load, layer, peel=4)
                for q in range(2):
                    sp.wait_ge(s[f"returned{q}"], (layer + 1) * RETURNS[q])

                for b in range(B):
                    q = b % 4
                    if started(v := layer * B + b - 3):
                        sp.wait_ge(s["combined"], v)
                    for k in range(2):
                        src = back_d[(k * B + b) * N:(k * B + b + 1) * N, :].rearrange("(p j) d -> p j d", j=TPS)
                        sp.dma_start(yb[q][k], src).then_inc(s[f"back_loaded{q}"], 16)

            expert_tiles(0)
            expert_tiles(1)

            for b in range(B):
                sp.wait_ge(s["combined"], B + b + 1)
                sp.dma_start(out[b], X[:, b * TPS:(b + 1) * TPS, :]).then_inc(s["stored"], 16)
            sp.wait_ge(s["stored"], 16 * B)

        @block.gpsimd
        def _(pool):
            for name in ("xres_ready",):
                pool.sem_inc(s[name], 1)
            pool.memset(powc[:, :], -0.5).then_inc(s["powc_set"], 1)
            for q in range(2):
                pool.memset(gt[q][:, :], 1.0).then_inc(s["ones_set"], 1)
            for q in range(2):
                pool.memset(pay[q][:, :, :, :], 0.0).then_inc(s["pay_set"], 1)
            pool.memset(crun[:, :, :], 1.0).then_inc(s["crun_set"], 1)
            pool.wait_ge(s["powc_set"], 1)
            pool.wait_ge(s["crun_set"], 1)
            pool.memset(cadd[:, :, :], 0.0).then_inc(s["crun_set"], 1)
            pool.memset(crun[:, :, 0], 0.0).then_inc(s["crun_set"], 1)
            link = Link(pool, s["pool_order"])
            for k in range(3):
                w = slice(k * H * HD, (k + 1) * H * HD)
                pool.wait_ge(s["w_hi_ready"], k + 1)
                pool.tensor_tensor(w_lo[:, w], wts[:, w], w_hi[:, w].bitcast(F32), ALU.subtract).then_inc(s["w_lo_ready"], 1)
            pool.wait_ge(s["csT_ready"], 1)
            pool.wait_ge(s["csum_spread"], 16)
            for c in range(NT):
                pool.tensor_scalar(dmat[:, c * P:(c + 1) * P], decays[:, c * P:(c + 1) * P], csT[:, c:c + 1], None,
                                   ALU.max).then_inc(s["dmax_ready"], 1)
            for m in range(TPS - 1):
                pool.memset(wst[m], 0.0)
            pool.wait_ge(s["dexp_ready"], NT)
            for b in range(B):
                seq = dmat[:, b * N:(b + 1) * N].rearrange("p (c t) -> p c t", t=P)
                pool.tensor_tensor(seq, seq, C("mask").unsqueeze(1).to_broadcast([P, TPS, P]), ALU.mult)\
                    .then_inc(s["dmat_ready"], 1)
            def rstd(var, tmp, dst, ready):
                apart(pool)
                link(pool.tensor_scalar(tmp, var, EPS, None, ALU.add))
                pool.tensor_tensor(dst, tmp, powc[:, 0:TPS], ALU.pow).then_inc(s[ready], 1)

            def prepare(t):
                pool.wait_ge(s["mv_ready"], t.count(1, 1))
                rstd(mv[:, :, 1], ve[:, :], rs[:, :], "rs_ready")
                pool.wait_ge(s["x2_ready"], t.count(1, 1))
                if started(v := t.count(1, -1)):
                    pool.wait_ge(s["x3_ready"], v)
                pool.tensor_tensor(x2b[t.par][:, :, :], x2[t.par][:, :, :],
                                   row("b_out").unsqueeze(1).to_broadcast([P, TPS, D]), ALU.add).then_inc(s["x2b_ready"], 1)

            def finish_norm(t):
                pool.wait_ge(s["mv3_ready"], t.count(1, 1))
                rstd(mv3[:, :, 1], ve3[:, :], rs3[:, :], "rs3_ready")

            def finish_residual(t):
                if started(v := 1 + t.count()):
                    pool.wait_ge(s["x1_ready"], v)
                apart(pool)
                link(pool.tensor_tensor(xres[:, :, :], x3[:, :, :], X[:, tiles(t), :], ALU.add))
                pool.tensor_tensor(xres[:, :, :], xres[:, :, :], row("b_ff2").unsqueeze(1).to_broadcast([P, TPS, D]),
                                   ALU.add).then_inc(s["xres_ready"], 1)

            def scale_heads(t):
                for p in range(PAIRS):
                    pool.wait_ge(s["qk_ready"], t.count(2 * PAIRS, 2 * p + 1))
                    apart(pool)
                    pool.tensor_tensor(qd[:, p, :], qT[:, p, :], decays[:, bass.ds(t.count(N), N)], ALU.mult)\
                        .then_inc(s["qd_ready"], 1)
                for m in range(TPS):
                    pool.wait_ge(s["tok_ready"], t.count(2 * TPS, 2 * m + 2))
                    apart(pool)
                    pool.tensor_tensor(vdec[:, m, :], vtok[:, m, :], decC[:, tile_at(t, m)].to_broadcast([P, H * HD]), ALU.mult)\
                        .then_inc(s["vdec_ready"], 1)

            def route_norm(ts):
                pool.wait_ge(s["rmv_ready"], ts.count(1, 1))
                q = ts.par
                rstd(rmv[:, q, :, 1], rve[:, q, :], rrs[:, q, :], "rrs_ready")

            def route_rows(ts):
                q = pay_of(ts)
                pool.wait_ge(s["slots_ready"], 1 + ts.count(1, 1))
                apart(pool)
                pool.wait_ge(s["pay2_ready"], ts.count(1, 1))
                apart(pool)
                for j in range(TPS):
                    for k in range(2):
                        pool.indirect_dma_start(routed_d, bass.IndirectOffsetOnAxis(ap=slots[:, q, k, j:j + 1], axis=0),
                                                pay[q][:, j, k, :], None).then_inc(s[f"scattered{q}"], 16)

            def a_item(t, first=False, last=False, route=True):
                if not last:
                    prepare(t.at(1))
                if not first:
                    finish_norm(t.at(-1))
                if not first and route:
                    route_norm(t.at(-2))
                if not first:
                    finish_residual(t.at(-1))
                scale_heads(t)
                if not first and route:
                    route_rows(t.at(-2))

            pool.wait_ge(s["params_loaded"], 16 * PARAM_LOADS)
            half = (MAX_TILES - MIN_TILES + 1) // 2
            for q, (lo, hi) in enumerate(((0, half), (half, MAX_TILES - MIN_TILES))):
                dst = routed_d[E_N * CAP + lo * TT:E_N * CAP + hi * TT, :].rearrange("(g p) r -> p g r", p=P)
                src = tail[:, :].bitcast(F32).unsqueeze(1).to_broadcast([P, (hi - lo) * TH, ROW])
                pool.dma_start(dst, src).then_inc(s[f"scattered{q}"], SPARE)
            pool.wait_ge(s["decC_ready"], 1)
            prepare(Turn(0))
            a_loop(pool, a_item, link, 8)
            t = Turn(B - 1)
            finish_norm(t)
            route_norm(t.at(-1))
            finish_residual(t)
            route_norm(t)
            route_rows(t.at(-1))
            route_rows(t)
            def experts(layer):
                def give_back(j, js):
                    q = j.par
                    pool.wait_ge(s["ey_ready"], 1 + js.count(1, 1))
                    apart(pool)
                    for h in range(TH):
                        pool.indirect_dma_start(back_d, bass.IndirectOffsetOnAxis(ap=back_row[j.quad][:, h:h + 1], axis=0),
                                                ey[q][:, h, :], None, bounds_check=2 * B * N - 1, oob_is_err=False)\
                            .then_inc(s[f"returned{j.par}"], 16)

                tile_loop(pool, give_back, layer)

            experts(0)

            def scan_norm(t):
                pool.wait_ge(s["gmv_ready"], t.half(1, 1))
                if started(v := t.count(TPS, -2 * TPS)):
                    pool.wait_ge(s["gres_ready"], v)
                gm, g = gmv[t.k // 2 % 2], gr[t.k // 2 % 2]
                v, a, r = gm[:, :, :, 1], g[:, 0], g[:, 1]
                power = powc[:, 0:2 * TPS].rearrange("p (q j) -> p q j", q=2)
                link(pool.tensor_scalar(a, v, EPS, None, ALU.add))
                link(pool.tensor_tensor(r, a, power, ALU.pow))
                link(pool.tensor_tensor(a, r, r, ALU.mult))
                link(pool.tensor_tensor(a, a, v, ALU.mult))
                link(pool.tensor_scalar(a, a, RMS_EPS, None, ALU.add))
                link(pool.tensor_tensor(a, a, power, ALU.pow))
                pool.tensor_tensor(g[:, 2], a, r, ALU.mult).then_inc(s["grs_ready"], 1)
                link(pool.tensor_tensor(g[:, 3], gm[:, :, :, 0], r, ALU.mult))
                link(pool.tensor_scalar(g[:, 3], g[:, 3], -1.0, None, ALU.mult))
                pool.tensor_scalar(g[:, 0], r, 1.0, None, ALU.add).then_inc(s["gc_ready"], 1)

            def scan_bias(t):
                pool.wait_ge(s["gres_ready"], t.count(TPS, TPS))
                at = X[:, tiles(t), :]
                pool.tensor_tensor(at, at, row("b_outb").unsqueeze(1).to_broadcast([P, TPS, D]), ALU.add).then_inc(s["gbias_ready"], 1)

            for q in (2, 3):
                pool.memset(pay[q], 0.0).then_inc(s["pay_set"], 1)
            scan_norm(Turn(0))
            for p in range(B // 2 + 1):
                if p < B // 2 - 1:
                    scan_norm(Turn(2 * p + 2))
                if p < B // 2:
                    scan_bias(Turn(2 * p))
                    scan_bias(Turn(2 * p + 1))
                if p:
                    route_rows(Turn(B + 2 * p - 2))
                if p < B // 2:
                    for r in (2 * p, 2 * p + 1):
                        route_norm(Turn(B + r))
                if p:
                    route_rows(Turn(B + 2 * p - 1))
            experts(1)
            for b in range(B):
                at = X[:, b * TPS:(b + 1) * TPS, :]
                pool.wait_ge(s["first_weighted"], (b + 1) * TPS)
                pool.tensor_tensor(at, at, yb[b % 4][0], ALU.add).then_inc(s["first_added"], 1)

        @block.scalar
        def _(act):
            for name in ("ff_ready", "x3T_ready", "rxT_ready", "pot_ready",):
                act.sem_inc(s[name], 1)
            for dst, src in ((cols, cols_in), (cst, consts), (rows, rows_in.to_broadcast([P, ROWS_N])), (wbk, wbk_in),
                             (ids, ids_in), (tail, tail_in)):
                full = tuple(slice(None) for _ in dst.shape)
                act.dma_start(dst[full], src).then_inc(s["params_loaded"], 16)
            act.dma_start(wts[:, :], wts_in).then_inc(s["wts_loaded"], 16)
            link = Link(act, s["act_order"])
            for k in range(2):
                act.wait_ge(s["var_ready"], k + 1)
                act.activation(sm[:, 7, :], sm[:, 3, :], ACT.Sqrt).then_inc(s["root_ready"], 1)
            act.wait_ge(s["params_loaded"], 16 * PARAM_LOADS)

            act.wait_ge(s["wts_loaded"], 16)
            for k in range(3):
                w = slice(k * H * HD, (k + 1) * H * HD)
                act.activation(w_hi[:, w], wts[:, w], ACT.Copy).then_inc(s["w_hi_ready"], 1)

            def first_pass(t, _):
                act.wait_ge(s["t1_mm"], t.count(1, 1))
                if started(v := t.count(1, -1)):
                    act.wait_ge(s["pot_mm"], v)
                act.activation(t_order(xnT[t.par][:, :]), (ps_t, ps_o)[t.par][:, :].rearrange("d (j p) -> d j p", j=TPS), ACT.Copy)\
                    .then_inc(s["xn1T_ready"], 1)
                if t.n is not None or t.k:
                    potential(t.at(-1))

            def potential(t):
                act.wait_ge(s["pot_mm"], t.count(1, 1))
                act.activation(potT[0:2, bass.ds(t.count(N), N)], ps_p[t.par][0:2, :], ACT.Identity, bias=potb[0:2, :])\
                    .then_inc(s["pot_ready"], 1)

            act.wait_ge(s["potb_ready"], 1)
            pairs_of(act, first_pass, B)
            potential(Turn(B - 1))
            act.wait_ge(s["vabs_ready"], 1)
            link(act.activation(cf[:, 3, :], cf[:, 2, :], ACT.Exp, scale=-1.0))
            act.activation(cf[:, 4, :], cf[:, 3, :], ACT.Ln, bias=1.0).then_inc(s["log_ready"], 1)
            for c in range(NT):
                act.wait_ge(s["dmax_ready"], c + 1)
                act.activation(dmat[:, c * P:(c + 1) * P], dmat[:, c * P:(c + 1) * P], ACT.Exp, scale=-DT,
                               bias=csr[:, c:c + 1]).then_inc(s["dexp_ready"], 1)
            act.wait_ge(s["decC_arg_ready"], 1)
            link(act.activation(decays[:, :], decays[:, :], ACT.Exp, scale=-DT))
            act.activation(sm[:, 8, :], sm[:, 7, :], ACT.Exp, scale=-DT).then_inc(s["decC_exp_ready"], 1)
            def heads_evac(t):
                for n in range(2 * PAIRS):
                    p, key = n // 2, n % 2
                    act.wait_ge(s["qk_mm"], t.count(2 * PAIRS, n + 1))
                    if n == 0:
                        if started(v := t.count(PAIRS)):
                            act.wait_ge(s["qd_ready"], v)
                    act.activation((kT if key else qT)[:, p, :], ps_in[n % 4][:, :], ACT.Identity,
                                   bias=col("bk" if key else "bq", p)).then_inc(s["qk_ready"], 1)

            def prepare(t):
                act.wait_ge(s["t2_mm"], t.count(1, 1))
                act.activation(t_order(xnT[0][:, :]), ps_t[:, :].rearrange("d (j p) -> d j p", j=TPS), ACT.Identity,
                               scale=col("g2"), bias=col("b2")).then_inc(s["xnT_ready"], 1)

            def finish_norm(t):
                act.wait_ge(s["t3_mm"], t.count(1, 1))
                act.activation(x3T[:, :], ps_u[:, :], ACT.Identity, scale=col("g3"), bias=col("b3"))\
                    .then_inc(s["x3T_ready"], 1)

            def finish(t):
                for c in range(FC):
                    act.wait_ge(s["ff1_mm"], t.count(FC, c + 1))
                    act.activation(hff[:, c, :], ps_p[c % 2][:, :], ACT.Gelu_apprx_tanh, bias=col("bff1", c))\
                        .then_inc(s["ff_ready"], 1)

            def heb_evac(t):
                for m in range(TPS):
                    act.wait_ge(s["pv_mm"], t.count(TPS, m + 1))
                    act.activation(hebT[:, :, m * P:(m + 1) * P], ps_h[:, :].rearrange("e (p t) -> e p t", p=PAIRS), ACT.Copy)\
                        .then_inc(s["heb_ready"], 1)

            def route_xT(ts):
                act.wait_ge(s["rt_mm"], ts.count(1, 1))
                act.activation(rxT[ts.par][:, :], ps_t[:, :], ACT.Copy).then_inc(s["rxT_ready"], 1)

            def route_pay(ts):
                q = pay_of(ts)
                act.wait_ge(s["pay_ready"], ts.count(1, 1))
                if started(v := scattered_before(ts)):
                    act.wait_ge(s[f"scattered{q}"], v)
                act.activation(pay[q][:, :, 1, 0:D], pay[q][:, :, 0, 0:D], ACT.Copy).then_inc(s["pay2_ready"], 1)

            def a_item(t, first=False, last=False, route=True):
                heads_evac(t)
                if not first:
                    finish_norm(t.at(-1))
                if not last:
                    prepare(t.at(1))
                if not first:
                    finish(t.at(-1))
                if not first and route:
                    route_pay(t.at(-2))
                    route_xT(t.at(-2))
                heb_evac(t)

            prepare(Turn(0))
            a_loop(act, a_item)
            t = Turn(B - 1)
            finish_norm(t)
            finish(t)
            for r in (t.at(-1), t):
                route_pay(r)
                route_xT(r)
            def experts(layer):
                act.wait_ge(s["slots_ready"], 1 + (layer + 1) * B)
                act.activation(etok[:, :], dtok[:, :], ACT.Exp).then_inc(s["etok_ready"], 1)

                def w1_part(j, js):
                    if started(v := js.count(FC, -FC)):
                        act.wait_ge(s["h_mm"], v)
                    act.wait_ge(s[f"ewt_loaded{j.quad}"], loads(j, layer, 32))
                    act.activation(w1_hi[j.par], ewt[j.quad][:, EXP_AT["w1"][0]:EXP_AT["w1"][1]], ACT.Copy).then_inc(s["w1_hi_ready"], 1)

                def x_part(j, js):
                    act.wait_ge(s["et_mm"], js.count(1, 1))
                    act.activation(exT_hi[j.par], (ps_t, ps_u)[j.par][:, 0:TT], ACT.Copy).then_inc(s["exT_hi_ready"], 1)

                def hidden_evac(j, js):
                    q = j.par
                    if j.n is not None or j.k < MAX_TILES - 1:
                        w1_part(j.at(1), js.at(1))
                    if started(v := js.count(1, -1)):
                        act.wait_ge(s["y_mm"], v)
                    for c in range(FC):
                        act.wait_ge(s["h_mm"], js.count(FC, c // 2 * 2 + 2))
                        src = (ps_s, ps_p)[q][c // 2][:, (c % 2) * TT:(c % 2 + 1) * TT]
                        b1 = EXP_AT["b1"][0] + c
                        act.activation(ehT[q][:, c, :], src, ACT.Gelu_apprx_tanh, bias=ewt[j.quad][:, b1:b1 + 1])\
                            .then_inc(s["ehT_ready"], 1)

                w1_part(Turn(0), Turn(layer * MAX_TILES))
                tile_loop(act, hidden_evac, layer, ahead=x_part)

            experts(0)

            def scan_xT(t):
                act.wait_ge(s["gt_mm"], t.count(1, 1))
                act.activation(t_order(xnT[t.par][:, :]), ps_p[t.par][:, :].rearrange("d (j p) -> d j p", j=TPS), ACT.Identity,
                               scale=col("norm_w")).then_inc(s["gxT_ready"], 1)

            def scan_uz(t):
                act.wait_ge(s["guz_mm"], t.count(1, 1))
                if started(v := t.count(1, -1)):
                    act.wait_ge(s["gx_mm"], v)
                act.activation(uz[t.par], ps_p[t.par][:, :], ACT.Identity, bias=col("b_uz")).then_inc(s["guz_ready"], 1)

            def scan_residual(t):
                q, g = t.par, gr[t.k // 2 % 2]
                act.wait_ge(s["gc_ready"], t.half(1, 1))
                act.wait_ge(s["gxh_ready"], t.count(1, 1))
                for j in range(TPS):
                    at = X[:, t.k * TPS + j, :]
                    act.activation(at, at, ACT.Identity, scale=g[:, 0, q, j:j + 1], bias=g[:, 3, q, j:j + 1])\
                        .then_inc(s["gres_ready"], 1)

            def scan_act(t):
                act.wait_ge(s["g_mm"], t.count(1, 2))
                if started(v := t.half()):
                    act.wait_ge(s["gy_ready"], v)
                act.activation(sg, ps_u[:, :], ACT.Sigmoid, bias=col("b_g")).then_inc(s["gsg_ready"], 1)
                act.wait_ge(s["gx_mm"], t.count(1, 2))
                act.activation(dtm, ps_s[1][:, :], ACT.Sigmoid, bias=col("b_dt")).then_inc(s["gdt_ready"], 1)
                act.activation(ut, ps_s[0][:, :], ACT.Tanh, bias=col("b_x")).then_inc(s["gut_ready"], 1)

            for p in range(B // 2 + 1):
                if p:
                    for r in (2 * p - 2, 2 * p - 1):
                        route_pay(Turn(B + r))
                        route_xT(Turn(B + r))
                if p < B // 2:
                    for q in range(2):
                        scan_xT(Turn(2 * p + q))
                    for q in range(2):
                        scan_uz(Turn(2 * p + q))
                    scan_act(Turn(2 * p))
                    for q in range(2):
                        scan_residual(Turn(2 * p + q))
            experts(1)
            act.wait_ge(s["wtok_ready"], 2)
            for b in range(B):
                q = b % 4
                act.wait_ge(s[f"back_loaded{q}"], 32 * (B // 4 + b // 4 + 1))
                for j in range(TPS):
                    y = yb[q][0][:, j, :]
                    act.activation(y, y, ACT.Identity, scale=wtok[:, 0, b * TPS + j:b * TPS + j + 1]).then_inc(s["first_weighted"], 1)

        @block.tensor
        def _(pe):
            for name in ("rank_mm",):
                pe.sem_inc(s[name], 1)
            pe.wait_ge(s["params_loaded"], 16 * PARAM_LOADS)
            pe.matmul(ps_o[0:2, 0:1], cols[:, COLS_AT["w_pot"][0]:COLS_AT["w_pot"][1]], col("b1"), start=True, stop=True)\
                .then_inc(s["potb_mm"], 1)
            pe.wait_ge(s["gw_ready"], 1)

            def first_pass(t, _):
                pe.wait_ge(s["xh1_ready"], t.count(1, 1))
                if started(v := t.count(1, -1)):
                    pe.wait_ge(s["xn1T_ready"], v)
                for j in range(TPS):
                    mm = pe.transpose((ps_t, ps_o)[t.par][:, j * P:(j + 1) * P], xh[t.par][:, j, :], ident)
                mm.then_inc(s["t1_mm"], 1)
                if t.n is not None or t.k:
                    potential(t.at(-1))

            def potential(t):
                pe.wait_ge(s["xn1T_ready"], t.count(1, 1))
                if started(v := 1 + t.count(1, -1)):
                    pe.wait_ge(s["pot_ready"], v)
                pe.matmul(ps_p[t.par][0:2, :], gw, xnT[t.par][:, :], start=True, stop=True).then_inc(s["pot_mm"], 1)

            pe.wait_ge(s["potb_ready"], 1)
            pairs_of(pe, first_pass, B)
            potential(Turn(B - 1))
            pe.wait_ge(s["xn1T_ready"], B)
            pe.wait_ge(s["csum_ready"], 1)
            pe.transpose(ps_o[:, 0:NT], csr2[0:NT, :], ident[0:NT, 0:NT]).then_inc(s["csT_mm"], 1)
            pe.wait_ge(s["wts_loaded"], 16)
            pe.wait_ge(s["w_lo_ready"], 3)
            def add_bk(t):
                pe.wait_ge(s[f"gt_loaded{t.par}"], t.half(16, 16))
                if started(v := t.count()):
                    pe.wait_ge(s["xnT_ready"], v)
                if started(v := 1 + t.count(1, -3)):
                    pe.wait_ge(s["rxT_ready"], v)
                for j in range(TPS):
                    mm = pe.matmul(ps_t[:, j * P:(j + 1) * P], gt[t.par][0:3, j::TPS], wbk[:, :], start=True, stop=True)
                mm.then_inc(s["bk_mm"], 1)

            def transpose2(t):
                pe.wait_ge(s["xh_ready"], t.count(1, 1))
                for j in range(TPS):
                    mm = pe.transpose(ps_t[:, j * P:(j + 1) * P], xh[t.par][:, j, :], ident)
                mm.then_inc(s["t2_mm"], 1)

            def heb_out(t):
                pe.wait_ge(s["heb_ready"], t.count(TPS, TPS))
                if started(v := 1 + t.count()):
                    pe.wait_ge(s["x1_ready"], v)
                for j in range(TPS):
                    for p in range(PAIRS):
                        mm = pe.matmul(ps_o[:, j * P:(j + 1) * P], hebT[:, p, j::TPS], W("w_out", p * D, (p + 1) * D),
                                       start=(p == 0), stop=(p == PAIRS - 1))
                mm.then_inc(s["wo_mm"], 1)

            def heads_in(t):
                def part(m=0, n=TPS):
                    return tuple(x[:, m * P:(m + n) * P] for x in (xnT_hi, xnT_lo))

                pe.wait_ge(s["xn_split"], t.count(1, 1))
                for n in range(2 * PAIRS):
                    p, key = n // 2, n % 2
                    if n < 2:
                        if started(v := 1 + t.count(FC, -FC)):
                            pe.wait_ge(s["ff_ready"], v)
                    elif n < 4:
                        if started(v := t.count(TPS)):
                            pe.wait_ge(s["pT_ready"], v)
                    else:
                        pe.wait_ge(s["qk_ready"], t.count(2 * PAIRS, n - 3))
                    passes(pe, ps_in[n % 4][:, :], W_parts("k" if key else "q", p * P, (p + 1) * P), part()).then_inc(s["qk_mm"], 1)
                for n in range(2 * TPS):
                    m, val = n // 2, n % 2
                    if n < 4:
                        pe.wait_ge(s["qk_ready"], t.count(2 * PAIRS, 2 * PAIRS - 3 + n))
                    else:
                        pe.wait_ge(s["tok_ready"], t.count(2 * TPS, n - 3))
                    passes(pe, ps_in[n % 4][:, :], part(m, 1), W_parts("v" if val else "k")).then_inc(s["tok_mm"], 1)

            def mlp_in(t):
                pe.wait_ge(s["xh3_ready"], t.count(1, 1))
                pe.wait_ge(s["w_ready"], t.count(TPS - 1, TPS - 1))
                for j in range(TPS):
                    mm = pe.transpose(ps_u[:, j * P:(j + 1) * P], x3h[:, j, :], ident)
                mm.then_inc(s["t3_mm"], 1)

            def mlp_hidden(t, tail=False):
                pe.wait_ge(s["x3T_ready"], 1 + t.count(1, 1))
                for c in range(FC):
                    if c < 2 and tail:
                        pe.wait_ge(s["ff_ready"], 1 + t.count(FC))
                    elif c < 2:
                        pe.wait_ge(s["tok_ready"], t.count(2 * TPS, 4 * TPS - 3 + c))
                    else:
                        pe.wait_ge(s["ff_ready"], 1 + t.count(FC, c - 1))
                    pe.matmul(ps_p[c % 2][:, :], W("ff1", c * P, (c + 1) * P), x3T[:, :], start=True, stop=True)\
                        .then_inc(s["ff1_mm"], 1)

            def mlp_out(t):
                pe.wait_ge(s["ff_ready"], 1 + t.count(FC, FC))
                pe.wait_ge(s["x3_ready"], t.count(1, 1))
                if started(v := 1 + t.count()):
                    pe.wait_ge(s["slots_ready"], v)
                for j in range(TPS):
                    for c in range(FC):
                        mm = pe.matmul(ps_o[:, j * P:(j + 1) * P], hff[:, c, j * P:(j + 1) * P], W("ff2", c * D, (c + 1) * D),
                                       start=(c == 0), stop=(c == FC - 1))
                mm.then_inc(s["ff2_mm"], 1)

            def scores(t, m):
                pe.wait_ge(s["qk_ready"], t.count(2 * PAIRS, 2 * PAIRS))
                if started(v := t.count(TPS, m)):
                    pe.wait_ge(s["pT_ready"], v)
                if m == 0:
                    pe.wait_ge(s["tok_ready"], t.count(2 * TPS, 2 * TPS))
                ch = slice(m * P, (m + 1) * P)
                for p in range(PAIRS):
                    for o in range(2):
                        h = slice(o * HD, (o + 1) * HD)
                        mm = pe.matmul(ps_s[o][:, p * P:(p + 1) * P], kT[h, p, ch], qT[h, p, ch], start=True, stop=True)
                mm.then_inc(s["sc_mm"], 1)

            def update(t, m):
                pe.wait_ge(s["vdec_ready"], t.count(TPS, m + 1))
                if started(v := t.count(TPS - 1, m)):
                    pe.wait_ge(s["w_ready"], v)
                if m == 0:
                    if started(v := 1 + t.count()):
                        pe.wait_ge(s["x3T_ready"], v)
                for p in range(PAIRS):
                    c = slice(p * P, (p + 1) * P)
                    mm = pe.matmul(ps_u[:, c], ktok[:, m, c], vdec[:, m, c], start=True, stop=True)
                mm.then_inc(s["u_mm"], 1)

            def outputs(t, m):
                pe.wait_ge(s["pT_ready"], t.count(TPS, m + 1))
                if started(v := t.count(TPS, m)):
                    pe.wait_ge(s["heb_ready"], v)
                if m:
                    pe.wait_ge(s["w_ready"], t.count(TPS - 1, m))
                    pe.wait_ge(s["qd_ready"], t.count(PAIRS, PAIRS))
                for p in range(PAIRS):
                    c = slice(p * P, (p + 1) * P)
                    if m:
                        pe.matmul(ps_h[:, c], wst[m - 1][:, p, :], qd[:, p, m * P:(m + 1) * P], start=True, stop=False,
                                  skip_group_check=True)
                    for o in range(2):
                        hd = (2 * p + o) * HD
                        mm = pe.matmul(ps_h[o * HD:(o + 1) * HD, c], vtok[:, m, hd:hd + HD], pT[m % 2][o][:, p, :],
                                       start=(m == 0), stop=True, skip_group_check=True)
                mm.then_inc(s["pv_mm"], 1)

            def heb(t, route):
                for m in range(TPS):
                    scores(t, m)
                    if m:
                        outputs(t, m - 1)
                    if m < TPS - 1:
                        update(t, m)
                    if route and m == 0:
                        route_scores(t.at(-2), after=t.at(-1))
                    if route and m == 2:
                        route_ranks(t.at(-2))
                outputs(t, TPS - 1)

            def route_t(ts):
                pe.wait_ge(s["pay_ready"], ts.count(1, 1))
                for j in range(TPS):
                    mm = pe.transpose(ps_t[:, j * P:(j + 1) * P], pay[pay_of(ts)][:, j, 0, 0:D], ident)
                mm.then_inc(s["rt_mm"], 1)

            def route_scores(ts, w=1, after=None):
                pe.wait_ge(s["rxT_ready"], 1 + ts.count(1, w))
                if after:
                    pe.wait_ge(s["x3_ready"], after.count(1, 1))
                for i in range(w):
                    for j in range(TPS):
                        at = (i * TPS + j) * E_N
                        mm = pe.matmul(ps_o[:, at:at + E_N], rxT[ts.at(i).par][:, j * P:(j + 1) * P], W("wr"), start=True, stop=True)
                mm.then_inc(s["score_mm"], w)

            def route_ranks(ts, w=1):
                n = w * TPS * E_N
                pe.wait_ge(s["m_ready"], ts.count(1, w))
                flat = rt[:, 8, 0:w * TPS, :].rearrange("p j e -> p (j e)")
                pe.matmul(ps_o[:, 128:128 + n], C("before"), flat, start=True, stop=True)
                pe.matmul(ps_o[:, 256:256 + n], C("ones"), flat, start=True, stop=True).then_inc(s["rank_mm"], w)

            def a_item(t, first=False, last=False, route=True):
                route = route and not first
                if not last:
                    add_bk(t.at(1))
                if not first:
                    heb_out(t.at(-1))
                heads_in(t)
                if not first:
                    mlp_in(t.at(-1))
                if not last:
                    transpose2(t.at(1))
                if not first:
                    mlp_hidden(t.at(-1))
                if route:
                    pe.wait_ge(s["xnT_ready"], t.count(1, 1 if last else 2))
                    route_t(t.at(-2))
                heb(t, route)
                if not first:
                    mlp_out(t.at(-1))

            add_bk(Turn(0))
            transpose2(Turn(0))
            a_loop(pe, a_item)
            t = Turn(B - 1)
            heb_out(t)
            mlp_in(t)
            mlp_hidden(t, True)
            pe.wait_ge(s["rxT_ready"], 1 + B - 2)
            route_t(t.at(-1))
            route_scores(t.at(-1), after=t)
            route_ranks(t.at(-1))
            mlp_out(t)
            pe.wait_ge(s["x1_ready"], 1 + B)
            pe.wait_ge(s["rxT_ready"], 1 + B - 1)
            route_t(t)
            route_scores(t)
            route_ranks(t)
            def experts(layer):
                def x_t(j, js):
                    pe.wait_ge(s[f"ex_loaded{j.quad}"], loads(j, layer, 16))
                    if started(v := js.count(1, -1)):
                        pe.wait_ge(s["exT_ready"], v)
                    for h in range(TH):
                        mm = pe.transpose((ps_t, ps_u)[j.par][:, h * P:(h + 1) * P], ex[j.quad][:, h, 0:D], ident)
                    mm.then_inc(s["et_mm"], 1)

                def hidden(j, js):
                    pe.wait_ge(s["exT_ready"], js.count(1, 1))
                    pe.wait_ge(s["w1_lo_ready"], js.count(1, 1))
                    if started(v := js.count(FC, -FC)):
                        pe.wait_ge(s["ehT_ready"], v)
                    for c in range(FC):
                        w1 = tuple(w[j.par][:, c * P:(c + 1) * P] for w in (w1_hi, w1_lo))
                        passes(pe, (ps_s, ps_p)[j.par][c // 2][:, (c % 2) * TT:(c % 2 + 1) * TT], w1,
                               (exT_hi[j.par], exT_lo[j.par])).then_inc(s["h_mm"], 1)

                def result(j, js):
                    pe.wait_ge(s["ehT_ready"], js.count(FC, FC))
                    if started(v := 1 + js.count(1, -1)):
                        pe.wait_ge(s["ey_ready"], v)
                    for h in range(TH):
                        for c in range(FC):
                            w2 = EXP_AT["w2"][0] + c * D
                            mm = pe.matmul((ps_o, ps_h)[j.par][:, h * D:(h + 1) * D], ehT[j.par][:, c, h * P:(h + 1) * P],
                                           ewt[j.quad][:, w2:w2 + D], start=(c == 0), stop=(c == FC - 1))
                    mm.then_inc(s["y_mm"], 1)

                tile_loop(pe, hidden, layer, ahead=x_t, behind=result)

            experts(0)

            def scan_t(t):
                pe.wait_ge(s["gxh_ready"], t.count(1, 1))
                if started(v := t.count(1, -1)):
                    pe.wait_ge(s["guz_ready"], v)
                for j in range(TPS):
                    mm = pe.transpose(ps_p[t.par][:, j * P:(j + 1) * P], xh[t.par][:, j, :], ident)
                mm.then_inc(s["gt_mm"], 1)

            def scan_in(t):
                q = t.par
                pe.wait_ge(s["gxT_ready"], t.count(1, 1))
                if q == 0:
                    if started(v := t.half()):
                        pe.wait_ge(s["gsg_ready"], v)
                pe.matmul(ps_p[q][:, :], W("w_in", 0, 2 * S), xnT[q][:, :], start=True, stop=True).then_inc(s["guz_mm"], 1)
                pe.matmul(ps_u[q * S:(q + 1) * S, :], W("w_in", 2 * S, 3 * S), xnT[q][:, :], start=True, stop=True)\
                    .then_inc(s["g_mm"], 1)

            def scan_gates(t):
                q = t.par
                pe.wait_ge(s["guz_ready"], t.count(1, 1))
                if q == 0:
                    if started(v := t.half()):
                        pe.wait_ge(s["gut_ready"], v)
                    if started(v := t.half()):
                        pe.wait_ge(s["gdt_ready"], v)
                apart(pe)
                for k in range(2):
                    h = slice(k * S, (k + 1) * S)
                    mm = pe.matmul(ps_s[k][q * S:(q + 1) * S, :], W("w_xdt")[h, :], uz[q][h, :], start=True, stop=True)
                mm.then_inc(s["gx_mm"], 1)

            def scan_out(t):
                q = t.par
                pe.wait_ge(s["gy_ready"], t.half(1, 1))
                if started(v := t.count(1, -1)):
                    pe.wait_ge(s["scanned"], v)
                pe.wait_ge(s["slots_ready"], 1 + B + t.k // 2 * 2)
                for j in range(TPS):
                    h, at = slice(q * S, (q + 1) * S), (ps_o, ps_h)[q][:, j * D:(j + 1) * D]
                    mm = pe.matmul(at, ym[h, j::TPS], W("w_outb")[h, :], start=True, stop=True)
                mm.then_inc(s["gout_mm"], 1)

            for p in range(B // 2 + 1):
                t0, t1, r = Turn(2 * p), Turn(2 * p + 1), Turn(B + 2 * p - 2)
                if p:
                    for x in (r, r.at(1)):
                        pe.wait_ge(s["rxT_ready"], 1 + x.k)
                        route_t(x)
                if p < B // 2:
                    scan_t(t0)
                    scan_t(t1)
                if p:
                    pe.wait_ge(s["scanned"], 2 * p)
                    pe.wait_ge(s["slots_ready"], 1 + r.k)
                    route_scores(r, 2)
                if p < B // 2:
                    scan_in(t0)
                    scan_in(t1)
                    scan_gates(t0)
                    scan_gates(t1)
                if p:
                    route_ranks(r, 2)
                if p < B // 2:
                    scan_out(t0)
                    scan_out(t1)
            experts(1)

        @block.vector
        def _(dve):
            for name in ("x1_ready", "ey_ready", "slots_ready",):
                dve.sem_inc(s[name], 1)
            link = Link(dve, s["dve_order"])
            dve.wait_ge(s["params_loaded"], 16 * PARAM_LOADS)
            link(dve.tensor_scalar(gw, cols[:, COLS_AT["w_pot"][0]:COLS_AT["w_pot"][1]], col("g1"), None, ALU.mult))
            dve.wait_ge(s["potb_mm"], 1)
            dve.tensor_tensor(potb[0:2, :], ps_o[0:2, 0:1], col("b_pot")[0:2, :], ALU.add).then_inc(s["potb_ready"], 1)
            dve.memset(cstep[:, :, :], 0.0).then_inc(s["gw_ready"], 1)

            for b in range(B):
                dve.wait_ge(s[f"x_loaded{b}"], 16)
                for j in range(b * TPS, (b + 1) * TPS):
                    link.mark(dve.bn_stats(st1[:, j, :], X[:, j, :]))
            link.sync()
            m, dm, v, t = sm[:, 0, :], sm[:, 1, :], sm[:, 2, :], sm[:, 3, :]
            ra, rb, rab = sm[:, 4, :], sm[:, 5, :], sm[:, 6, :]
            link.mark(dve.tensor_tensor(m, st1[:, :, 1], st1[:, :, 4], ALU.add))
            link.mark(dve.tensor_tensor(dm, st1[:, :, 1], st1[:, :, 4], ALU.subtract))
            link(dve.tensor_tensor(v, st1[:, :, 2], st1[:, :, 5], ALU.add))
            link.mark(dve.tensor_scalar(m, m, 0.5, None, ALU.mult))
            link.mark(dve.tensor_tensor(dm, dm, dm, ALU.mult))
            link(dve.tensor_scalar(v, v, 1.0 / D, None, ALU.mult))
            link(dve.scalar_tensor_tensor(out=v, in0=dm, scalar=0.25, in1=v, op0=ALU.mult, op1=ALU.add))

            def rsqrt(k, r):
                y, z = sm[:, 8, :], sm[:, 9, :]
                dve.sem_inc(s["var_ready"], 1)
                dve.wait_ge(s["root_ready"], k)
                link(dve.reciprocal(y, sm[:, 7, :]))
                link(dve.tensor_tensor(z, y, y, ALU.mult))
                link(dve.tensor_tensor(z, z, t, ALU.mult))
                link(dve.tensor_scalar(z, z, -0.5, 0.5, ALU.mult, ALU.add))
                link(dve.tensor_tensor(z, y, z, ALU.mult))
                link(dve.tensor_tensor(r, y, z, ALU.add))

            link(dve.tensor_scalar(t, v, EPS, None, ALU.add))
            rsqrt(1, ra)
            link(dve.tensor_tensor(t, ra, ra, ALU.mult))
            link(dve.tensor_tensor(t, t, v, ALU.mult))
            link(dve.tensor_scalar(t, t, EPS, None, ALU.add))
            rsqrt(2, rb)
            link(dve.tensor_tensor(rab, ra, rb, ALU.mult))

            def first_pass(t, _):
                if started(v := t.count(1, -1)):
                    dve.wait_ge(s["t1_mm"], v)
                for j in range(TPS):
                    at = tile_at(t, j)
                    ins = dve.tensor_scalar(xh[t.par][:, j, :], X[:, at, :], sm[:, 0, at], sm[:, 6, at],
                                            ALU.subtract, ALU.mult)
                    if j < TPS - 1:
                        link.mark(ins)
                ins.then_inc(s["xh1_ready"], 1)

            pairs_of(dve, first_pass, B, link=link, per=2 * (TPS - 1))

            dve.wait_ge(s["pot_chunked"], 16)
            u, v, va, gm = cf[:, 0, :], cf[:, 1, :], cf[:, 2, :], cf[:, 5, :]
            link(dve.tensor_scalar(va, v, -1.0, None, ALU.mult))
            dve.tensor_tensor(va, v, va, ALU.max).then_inc(s["vabs_ready"], 1)
            link.mark(dve.tensor_scalar(u, u, 2.0, None, ALU.add))
            dve.wait_ge(s["log_ready"], 1)
            link(dve.scalar_tensor_tensor(out=gm, in0=v, scalar=0.0, in1=cf[:, 4, :], op0=ALU.max, op1=ALU.add))
            link.mark(dve.tensor_scalar(gm, gm, GAMMA_FLOOR, None, ALU.add))
            dve.memset(pseq[:, :, :, :], 0.0).then_inc(s["gamma_ready"], 1)
            link.sync()
            link.mark(dve.tensor_copy(dre[:, :, 0], u))
            link.mark(dve.tensor_copy(dre[:, :, 1], u[:, ::-1]))
            link.mark(dve.tensor_copy(dim2[:, :, 0, 0], gm))
            link.mark(dve.tensor_copy(dim2[:, :, 1, 0], gm[:, ::-1]))
            link.mark(dve.tensor_scalar(dim2[:, :, 0, 1], gm, -1.0, None, ALU.mult))
            link.mark(dve.tensor_scalar(dim2[:, :, 1, 1], gm[:, ::-1], -1.0, None, ALU.mult))
            dve.wait_ge(s["csr_loaded"], 16)
            dve.wait_ge(s["gamma_ready"], 1)
            dve.tensor_tensor_scan(csr2[0:NT, :], C("ones")[0:NT, :], csr[0:NT, :], 0.0, ALU.mult, ALU.add)\
                .then_inc(s["csum_ready"], 1)

            def slot(g, i):
                return pseq[:, g, i, :]

            link.mark(dve.memset(slot(0, 1).rearrange("p (r a c) -> p r a c", r=2, a=2)[:, :, 0, 0], 1.0))
            link(dve.memset(slot(0, 0).rearrange("p (r a c) -> p r a c", r=2, a=2)[:, :, 1, 0], 1.0))

            def norm(g, out):
                both = pseq[:, g, SEG:SEG + 2, :]
                link(dve.tensor_reduce(cnrm[:, 0, :], both.rearrange("p i (r m) -> p r i m", r=2), mybir.AxisListType.XY,
                                       ALU.add, apply_absolute_value=True))
                link(dve.reciprocal(cnrm[:, 1, :], cnrm[:, 0, :]))
                for r in range(2):
                    link.mark(dve.tensor_scalar(out[:, :, 4 * r:4 * r + 4], both[:, :, 4 * r:4 * r + 4], cnrm[:, 1, r:r + 1],
                                                None, ALU.mult))
                link.sync()

            for g in range(2):
                if g:
                    dve.wait_ge(s["csT_mm"], 1)
                    link(dve.tensor_copy(csT, ps_o[:, 0:NT]))
                    dve.tensor_scalar(csr[:, 0:NT], csT, DT, None, ALU.mult).then_inc(s["csT_ready"], 1)
                    norm(0, pseq[:, 1, 0:2, :])
                for i in range(SEG):
                    k = g * SEG + i
                    cur, last, new = slot(g, i + 1), slot(g, i), slot(g, i + 2)
                    swapped = cur.rearrange("p (r a c) -> p r a c", r=2, a=2)[:, :, :, ::-1]
                    link.mark(dve.tensor_tensor(cstep[:, 0, :].rearrange("p (r a c) -> p r a c", r=2, a=2), swapped,
                                                dim2[:, k, :, :].unsqueeze(2).to_broadcast([P, 2, 2, 2]), ALU.mult))
                    for r in range(2):
                        at = slice(4 * r, 4 * r + 4)
                        link.mark(dve.scalar_tensor_tensor(out=cstep[:, 1, at], in0=cur[:, at], scalar=dre[:, k, r:r + 1],
                                                           in1=last[:, at], op0=ALU.mult, op1=ALU.subtract))
                    link.sync()
                    link(dve.tensor_tensor(new, cstep[:, 0, :], cstep[:, 1, :], ALU.add))

            fin = pval[:, 0, 0:16].rearrange("p (i m) -> p i m", i=2)
            norm(1, fin)
            for w in range(2):
                pw = fin[:, 1 - w, :].rearrange("p (r a c) -> p r a c", r=2, a=2)
                mw = cmap[:, :, 8 * w:8 * w + 8].rearrange("p r (o a c) -> p r o a c", o=2, a=2)
                link.mark(dve.tensor_copy(mw[:, :, 0, :, 0], pw[:, :, :, 0]))
                link.mark(dve.tensor_scalar(mw[:, :, 0, :, 1], pw[:, :, :, 1], -1.0, None, ALU.mult))
                link.mark(dve.tensor_copy(mw[:, :, 1, :, 0], pw[:, :, :, 1]))
                link.mark(dve.tensor_copy(mw[:, :, 1, :, 1], pw[:, :, :, 0]))
            link.sync()
            R = 2 * B
            dve.memset(cst16[0:R, :, :], 0.0).then_inc(s["maps_ready"], 1)
            dve.wait_ge(s["csum_spread"], 16)
            ends = decays[:, :].rearrange("p (c i) -> p c i", i=P)[:, :, P - 1]
            dve.tensor_tensor(sm[:, 7, :], ends, csT, ALU.subtract).then_inc(s["decC_arg_ready"], 1)
            dve.wait_ge(s["maps_ready"], 1)
            link(dve.memset(cst16[0:R, 0, 0:1], 1.0))
            dve.wait_ge(s["maps_loaded"], 32)
            for k in range(NC - 1):
                link(dve.tensor_tensor(cprod16[0:R, :].rearrange("p (o i) -> p o i", o=4),
                                       cmap16[0:R, k, :].rearrange("p (o i) -> p o i", o=4),
                                       cst16[0:R, k, :].unsqueeze(1).to_broadcast([R, 4, 4]), ALU.mult))
                link(dve.tensor_reduce(cst16[0:R, k + 1, :], cprod16[0:R, :].rearrange("p (o i) -> p o i", o=4), X_AXIS, ALU.add))
            link(dve.tensor_reduce(cnrm16[0:R, 0, :], cst16[0:R, 0:NC, :], X_AXIS, ALU.add, apply_absolute_value=True))
            link(dve.reciprocal(cnrm16[0:R, 1, :], cnrm16[0:R, 0, :]))
            dve.tensor_tensor(cst16[0:R, 0:NC, :], cst16[0:R, 0:NC, :],
                              cnrm16[0:R, 1, :].unsqueeze(2).to_broadcast([R, NC, 4]), ALU.mult).then_inc(s["states_ready"], 1)
            dve.wait_ge(s["states_loaded"], 16)
            link(dve.tensor_scalar(cneg, cstate, -1.0, None, ALU.mult))
            flat = pseq.rearrange("p g i m -> p (g i) m")
            for term in range(4):
                for r in range(2):
                    for c in range(2):
                        a, im = term // 2, term % 2
                        src = flat[:, :, 4 * r + 2 * a + (c ^ im)]
                        sc = (cneg if im and not c else cstate)[:, r, term:term + 1]
                        dst = pval[:, 2 * r + c, :]
                        if term == 0:
                            link.mark(dve.tensor_scalar(dst, src, sc, None, ALU.mult))
                        else:
                            link.mark(dve.scalar_tensor_tensor(out=dst, in0=src, scalar=sc, in1=dst, op0=ALU.mult, op1=ALU.add))
                link.sync()
            pv = pval.rearrange("p (r c) (g i) -> p r c g i", r=2, g=2)

            def val(r, c, back):
                return pv[:, r, c, :, 2 - back:2 - back + SEG]

            def half(x, r):
                return cw[:, x, r, :].rearrange("p (g i) -> p g i", g=2)

            def both(f):
                for r in range(2):
                    link.mark(f(r))
                link.sync()

            both(lambda r: dve.scalar_tensor_tensor(out=half(0, r), in0=val(r, 0, 1), scalar=-1.0, in1=val(r, 0, 1), op0=ALU.mult, op1=ALU.max))
            both(lambda r: dve.scalar_tensor_tensor(out=half(1, r), in0=val(r, 1, 1), scalar=-1.0, in1=val(r, 1, 1), op0=ALU.mult, op1=ALU.max))
            link(dve.tensor_tensor(cw[:, 0], cw[:, 0], cw[:, 1], ALU.add))
            link(dve.reciprocal(cw[:, 1], cw[:, 0]))
            for c in range(2):
                both(lambda r: dve.tensor_tensor(half(2 + c, r), val(r, c, 1), half(1, r), ALU.mult))
                both(lambda r: dve.tensor_tensor(half(4 + c, r), val(r, c, 0), half(1, r), ALU.mult))
            qr, qi, pr, pi = cw[:, 2], cw[:, 3], cw[:, 4], cw[:, 5]
            link.mark(dve.tensor_tensor(cw[:, 6], qr, qr, ALU.mult))
            link.mark(dve.tensor_tensor(cw[:, 7], qi, qi, ALU.mult))
            link.mark(dve.tensor_tensor(cw[:, 8], pr, qr, ALU.mult))
            link.mark(dve.tensor_tensor(cw[:, 9], pi, qi, ALU.mult))
            link.sync()
            link.mark(dve.tensor_tensor(cw[:, 6], cw[:, 6], cw[:, 7], ALU.add))
            link.mark(dve.tensor_tensor(cw[:, 8], cw[:, 8], cw[:, 9], ALU.add))
            link.sync()
            link.mark(dve.tensor_tensor(cw[:, 7], pi, qr, ALU.mult))
            link.mark(dve.tensor_tensor(cw[:, 9], pr, qi, ALU.mult))
            link.mark(dve.reciprocal(cw[:, 0], cw[:, 6]))
            link.sync()
            link.mark(dve.tensor_tensor(cw[:, 7], cw[:, 7], cw[:, 9], ALU.subtract))
            link.mark(dve.tensor_tensor(cw[:, 1], cw[:, 8], cw[:, 0], ALU.mult))
            link.sync()
            link(dve.tensor_tensor(cw[:, 2], cw[:, 7], cw[:, 0], ALU.mult))
            for x, dst in ((1, 3), (2, 4)):
                link.mark(dve.tensor_tensor(cw[:, dst, 0, :], cw[:, x, 0, :], cw[:, x, 1, ::-1], ALU.add))
            link.sync()
            link.mark(dve.tensor_tensor(cw[:, 3, 0, :], cw[:, 3, 0, :], u, ALU.subtract))
            link.mark(dve.tensor_tensor(cw[:, 4, 0, :], cw[:, 4, 0, :], gm, ALU.add))
            link.sync()
            sr, si = cw[:, 3, 0, :], cw[:, 4, 0, :]
            link.mark(dve.tensor_tensor(cw[:, 5, 0, :], sr, sr, ALU.mult))
            link.mark(dve.tensor_tensor(cw[:, 6, 0, :], si, si, ALU.mult))
            link.sync()
            link(dve.tensor_tensor(cw[:, 5, 0, :], cw[:, 5, 0, :], cw[:, 6, 0, :], ALU.add))
            link(dve.reciprocal(cw[:, 6, 0, :], cw[:, 5, 0, :]))
            link(dve.tensor_tensor(green[:, 0, :], sr, cw[:, 6, 0, :], ALU.mult))
            dve.scalar_tensor_tensor(out=green[:, 1, :], in0=si, scalar=-1.0, in1=cw[:, 6, 0, :], op0=ALU.mult,
                                     op1=ALU.mult).then_inc(s["green_ready"], 1)
            dve.wait_ge(s["decC_exp_ready"], 1)
            link(dve.tensor_scalar(decC[:, :], sm[:, 8, :], ETA, None, ALU.mult))
            dve.memset(cneg[:, 0, 0:1], 0.0).then_inc(s["decC_ready"], 1)

            def norm_stats(x, stat, mv, ready):
                for j in range(TPS):
                    link.mark(dve.bn_stats(stat[:, j, :], x[:, j, :]))
                link.sync()
                apart(dve)
                for j in range(TPS):
                    ins = dve.bn_aggr(mv[:, j, :], stat[:, j, :])
                    if j < TPS - 1:
                        link.mark(ins)
                ins.then_inc(s[ready], 1)

            def normalise(dst, x, mv, rs, ready):
                for j in range(TPS):
                    ins = dve.tensor_scalar(dst[:, j, :], x[:, j, :], mv[:, j, 0:1], rs[:, j:j + 1], ALU.subtract, ALU.mult)
                    if j < TPS - 1:
                        link.mark(ins)
                ins.then_inc(s[ready], 1)

            def prepare(t):
                q = t.par
                if started(v := t.count(1, -1)):
                    dve.wait_ge(s["x2b_ready"], v)
                for j in range(TPS):
                    at = tile_at(t, j)
                    link.mark(dve.tensor_scalar(x2[q][:, j, :], X[:, at, :], sm[:, 0, at], sm[:, 4, at], ALU.subtract, ALU.mult))
                link.sync()
                dve.wait_ge(s["bk_mm"], t.count(1, 1))
                flat = x2[q][:, :, :].rearrange("p j d -> p (j d)")
                dve.tensor_tensor(flat, ps_t[:, :], flat, ALU.add).then_inc(s["x2_ready"], 1)
                dve.wait_ge(s["x2_ready"], t.count(1, 1))
                norm_stats(x2[q], stat, mv, "mv_ready")

            def prepare_norm(t):
                dve.wait_ge(s["rs_ready"], t.count(1, 1))
                normalise(xh[t.par], x2[t.par], mv, rs, "xh_ready")

            def finish(t):
                dve.wait_ge(s["wo_mm"], t.count(1, 1))
                if started(v := 1 + t.count()):
                    dve.wait_ge(s["xres_ready"], v)
                dve.tensor_tensor(x3[:, :, :].rearrange("p j d -> p (j d)"), ps_o[:, :],
                                  x2b[t.par][:, :, :].rearrange("p j d -> p (j d)"), ALU.add).then_inc(s["x3_ready"], 1)
                dve.wait_ge(s["x3_ready"], t.count(1, 1))
                norm_stats(x3, stat3, mv3, "mv3_ready")

            def finish_norm(t):
                dve.wait_ge(s["rs3_ready"], t.count(1, 1))
                normalise(x3h, x3, mv3, rs3, "xh3_ready")

            def finish_out(t):
                dve.wait_ge(s["ff2_mm"], t.count(1, 1))
                dve.wait_ge(s["xres_ready"], 1 + t.count(1, 1))
                dve.tensor_tensor(X[:, tiles(t), :], ps_o[:, :].rearrange("p (j d) -> p j d", j=TPS), xres[:, :, :], ALU.add)\
                    .then_inc(s["x1_ready"], 1)

            def tokens_evac(t):
                if started(v := t.count(TPS)):
                    dve.wait_ge(s["vdec_ready"], v)
                for n in range(2 * TPS):
                    m, val = n // 2, n % 2
                    dve.wait_ge(s["tok_mm"], t.count(2 * TPS, n + 1))
                    dve.tensor_tensor((vtok if val else ktok)[:, m, :], ps_in[n % 4][:, :], row("bv" if val else "bk"), ALU.add)\
                        .then_inc(s["tok_ready"], 1)

            def split(t):
                dve.wait_ge(s["xnT_ready"], t.count(1, 1))
                link(dve.tensor_copy(xnT_hi[:, :], xnT[0][:, :]))
                dve.tensor_tensor(xnT_lo[:, :], xnT[0][:, :], xnT_hi[:, :].bitcast(F32), ALU.subtract).then_inc(s["xn_split"], 1)

            def heb(t, route, last):
                def weigh(m):
                    dve.wait_ge(s["sc_mm"], t.count(TPS, m + 1))
                    dm = dmat[:, bass.ds(t.count(N, m * P), P)].unsqueeze(1).to_broadcast([P, PAIRS, P])
                    for o in range(2):
                        ins = dve.tensor_tensor(pT[m % 2][o], ps_s[o][:, :].rearrange("s (p t) -> s p t", p=PAIRS), dm, ALU.mult)
                        if o == 0:
                            link.mark(ins)
                    ins.then_inc(s["pT_ready"], 1)

                def store(m):
                    dve.wait_ge(s["u_mm"], t.count(TPS - 1, m + 1))
                    if m:
                        dve.wait_ge(s["w_ready"], t.count(TPS - 1, m))
                    for o in range(2):
                        h = slice(o * HD, (o + 1) * HD)
                        add = ps_u[h, :].rearrange("d (p e) -> d p e", p=PAIRS)[:, :, h]
                        if m == 0:
                            ins = dve.tensor_copy(wst[m][h, :, h], add)
                        else:
                            ins = dve.scalar_tensor_tensor(out=wst[m][h, :, h], in0=wst[m - 1][h, :, h],
                                                           scalar=decays[h, bass.ds(t.count(N, m * P + P - 1), 1)], in1=add,
                                                           op0=ALU.mult, op1=ALU.add)
                        if o == 0:
                            link.mark(ins)
                    ins.then_inc(s["w_ready"], 1)

                for m in range(TPS):
                    weigh(m)
                    if m < TPS - 1:
                        store(m)
                    if m == 0 and not last:
                        split(t.at(1))
                    if route and m == 1:
                        route_choose(t.at(-2), t.at(-2))
                    if route and m == 3:
                        route_slots(t.at(-2), t.at(-2))

            def route_stats(t, ts):
                for j in range(TPS):
                    link.mark(dve.bn_stats(rstat[:, ts.par, j, :], X[:, tile_at(t, j), :]))
                link.sync()
                apart(dve)
                for j in range(TPS):
                    ins = dve.bn_aggr(rmv[:, ts.par, j, :], rstat[:, ts.par, j, :])
                    if j < TPS - 1:
                        link.mark(ins)
                ins.then_inc(s["rmv_ready"], 1)

            def route_norm(t, ts):
                q, w = ts.par, pay_of(ts)
                dve.wait_ge(s["rrs_ready"], ts.count(1, 1))
                if started(v := scattered_before(ts)):
                    dve.wait_ge(s[f"scattered{w}"], v)
                apart(dve)
                link.mark(dve.tensor_copy(pay[w][:, :, :, D].bitcast(I32), ids[:, tiles(t), :]))
                for j in range(TPS):
                    link.mark(dve.tensor_scalar(pay[w][:, j, 0, 0:D], X[:, tile_at(t, j), :], rmv[:, q, j, 0:1], rrs[:, q, j:j + 1],
                                                ALU.subtract, ALU.mult))
                link.sync()
                dve.sem_inc(s["pay_ready"], 1)

            def route_choose(t, ts, w=1):
                G = w * TPS

                def wide(v):
                    return v.unsqueeze(2).to_broadcast([P, G, E_N])

                dve.wait_ge(s["score_mm"], ts.count(1, w))
                link(dve.tensor_tensor(rt[:, 0, 0:G], ps_o[:, 0:G * E_N].rearrange("p (j e) -> p j e", j=G),
                                       row("br").unsqueeze(1).to_broadcast([P, G, E_N]), ALU.add))
                for k in range(2):
                    sc, eq, pri, oh = (rt[:, 4 * k + i, 0:G] for i in range(4))
                    link(dve.tensor_reduce(rv[:, k, 0:G], sc, X_AXIS, ALU.max))
                    link(dve.tensor_tensor(eq, sc, wide(rv[:, k, 0:G]), ALU.is_equal))
                    link(dve.tensor_tensor(pri, eq, C("rev").unsqueeze(1).to_broadcast([P, G, E_N]), ALU.mult))
                    link(dve.tensor_reduce(rv[:, 2, 0:G], pri, X_AXIS, ALU.max))
                    link(dve.tensor_tensor(oh, pri, wide(rv[:, 2, 0:G]), ALU.is_equal))
                    if k == 0:
                        link(dve.scalar_tensor_tensor(out=rt[:, 4, 0:G], in0=oh, scalar=NEG_BIG, in1=sc, op0=ALU.mult, op1=ALU.add))
                dve.wait_ge(s["rank_mm"], 1 + ts.count())
                dve.tensor_tensor(rt[:, 8, 0:G], rt[:, 3, 0:G], rt[:, 7, 0:G], ALU.add).then_inc(s["m_ready"], w)
                link.mark(dve.tensor_tensor(dtok[:, bass.ds(t.count(TPS), G)], rv[:, 1, 0:G], rv[:, 0, 0:G], ALU.subtract))

            def route_slots(t, ts, w=1):
                q, G = pay_of(ts), w * TPS
                dve.wait_ge(s["rank_mm"], 1 + ts.count(1, w))
                link(dve.tensor_copy(cadd[:, :, 1:G + 1], ps_o[:, 256:256 + G * E_N].rearrange("p (j e) -> p e j", j=G)))
                link(dve.tensor_tensor_scan(*(x[:, :, :].rearrange("p e j -> p (e j)") for x in (csum, crun, cadd)), 0.0,
                                            ALU.mult, ALU.add))
                link.mark(dve.tensor_copy(cadd[:, :, 0], csum[:, :, G]))
                link(dve.tensor_tensor(rt[:, 9, 0:G], ps_o[:, 128:128 + G * E_N].rearrange("p (j e) -> p j e", j=G),
                                       csum[:, :, 0:G].rearrange("p e j -> p j e"), ALU.add))
                for k in range(2):
                    link.mark(dve.tensor_tensor(rt[:, 10 + k, 0:G], rt[:, 3 + 4 * k, 0:G], rt[:, 9, 0:G], ALU.mult))
                link.sync()
                link(dve.tensor_reduce(rsl[:, :, 0:G], rt[:, 10:12, 0:G], X_AXIS, ALU.add))
                for i in range(w):
                    if started(v := scattered_before(ts.at(i))):
                        dve.wait_ge(s[f"scattered{q + i}"], v)
                apart(dve)
                dve.tensor_copy(slots[:, q:q + w].rearrange("p w k j -> p k w j"),
                                rsl[:, :, 0:G].rearrange("p k (w j) -> p k w j", w=w)).then_inc(s["slots_ready"], w)

            def a_item(t, first=False, last=False, route=True):
                route = route and not first
                if not last:
                    prepare(t.at(1))
                if not first:
                    finish(t.at(-1))
                if route:
                    dve.wait_ge(s["x1_ready"], 1 + t.count(1, -1))
                    apart(dve)
                    route_stats(t.at(-2), t.at(-2))
                if not last:
                    prepare_norm(t.at(1))
                if not first:
                    finish_norm(t.at(-1))
                if route:
                    route_norm(t.at(-2), t.at(-2))
                tokens_evac(t)
                heb(t, route, last)
                if not first:
                    finish_out(t.at(-1))

            dve.wait_ge(s["crun_set"], 3)
            link(dve.tensor_copy(cadd[:, :, 0], C("ebase")))
            dve.wait_ge(s["pay_set"], 2)
            prepare(Turn(0))
            prepare_norm(Turn(0))
            split(Turn(0))
            dve.wait_ge(s["dmat_ready"], B)
            a_loop(dve, a_item, link, PER_A)
            t = Turn(B - 1)
            finish(t)
            dve.wait_ge(s["x1_ready"], 1 + B - 1)
            route_stats(t.at(-1), t.at(-1))
            finish_norm(t)
            route_norm(t.at(-1), t.at(-1))
            route_choose(t.at(-1), t.at(-1))
            route_slots(t.at(-1), t.at(-1))
            finish_out(t)
            dve.wait_ge(s["x1_ready"], 1 + B)
            route_stats(t, t)
            route_norm(t, t)
            route_choose(t, t)
            route_slots(t, t)
            def tile_tables(layer):
                o = slice(0, 1)
                link(dve.tensor_copy(tail_row[o, :], cadd[o, :, 0]))
                link(dve.tensor_tensor(tl[o, 0, :], cadd[o, :, 0], C("ebase")[o, :], ALU.subtract))
                link(dve.tensor_tensor(tlk[o], tl[o, 0, :].unsqueeze(2).to_broadcast([1, E_N, 16]),
                                       C("kthr")[o, :].unsqueeze(1).to_broadcast([1, E_N, 16]), ALU.is_gt))
                link(dve.tensor_reduce(tl[o, 1, :], tlk[o], X_AXIS, ALU.add))
                link(dve.tensor_tensor_scan(tl[o, 2, :], C("ones")[o, 0:E_N], tl[o, 1, :], 0.0, ALU.mult, ALU.add))
                wide = [1, MAX_TILES, E_N]
                link(dve.tensor_tensor(tlj[o], C("jj")[o, :].unsqueeze(2).to_broadcast(wide),
                                       tl[o, 2, :].unsqueeze(1).to_broadcast(wide), ALU.is_ge))
                link(dve.tensor_reduce(tlr[o, 0, :], tlj[o], X_AXIS, ALU.add))
                link(dve.tensor_tensor(tlj[o], tlj[o], tl[o, 1, :].unsqueeze(1).to_broadcast(wide), ALU.mult))
                link(dve.tensor_reduce(tlr[o, 1, :], tlj[o], X_AXIS, ALU.add))
                link(dve.tensor_tensor(tlr[o, 1, :], C("jj")[o, :], tlr[o, 1, :], ALU.subtract))
                link(dve.tensor_scalar(tlr[o, 1, :], tlr[o, 1, :], float(TT), None, ALU.mult))
                link(dve.scalar_tensor_tensor(out=tlr[o, 2, :], in0=tlr[o, 0, :], scalar=float(CAP), in1=tlr[o, 1, :],
                                              op0=ALU.mult, op1=ALU.add))
                link(dve.tensor_scalar(tlr[o, 3, :], tlr[o, 0, :], float(E_N - 1), None, ALU.min))
                link(dve.tensor_copy(tile_row[o, :], tlr[o, 2, :]))
                dve.tensor_copy(tile_e[o, :], tlr[o, 3, :]).then_inc(s["tables_ready"], 1)

            def experts(layer):
                link.sync()
                tile_tables(layer)
                dve.wait_ge(s["etok_ready"], layer + 1)
                link(dve.tensor_scalar(wtok[:, 0, :], etok[:, :], 1.0, None, ALU.add))
                link(dve.reciprocal(wtok[:, 0, :], wtok[:, 0, :]))
                dve.tensor_tensor(wtok[:, 1, :], wtok[:, 0, :], etok[:, :], ALU.mult).then_inc(s["wtok_ready"], 1)

                def result(j, js):
                    q = j.par
                    dve.wait_ge(s["y_mm"], js.count(1, 1))
                    dve.wait_ge(s[f"ewt_loaded{j.quad}"], loads(j, layer, 32))
                    if started(v := j.half(32, layer * RETURNS[q])):
                        dve.wait_ge(s[f"returned{q}"], v)
                    dve.tensor_tensor(ey[q], (ps_o, ps_h)[q][:, 0:TH * D].rearrange("p (h d) -> p h d", h=TH),
                                      eb2[j.quad].unsqueeze(1).to_broadcast([P, TH, D]), ALU.add).then_inc(s["ey_ready"], 1)

                def second_parts(j, js):
                    q = j.par
                    dve.wait_ge(s[f"ex_loaded{j.quad}"], loads(j, layer, 16))
                    if started(v := j.half(32, layer * RETURNS[q] - 32)):
                        dve.wait_ge(s[f"returned{q}"], v)
                    dve.tensor_copy(back_row[j.quad], ex[j.quad][:, :, D].bitcast(I32)).then_inc(s["back_row_ready"], 1)
                    dve.wait_ge(s["w1_hi_ready"], js.count(1, 1))
                    dve.tensor_tensor(w1_lo[q], ewt[j.quad][:, EXP_AT["w1"][0]:EXP_AT["w1"][1]], w1_hi[q].bitcast(F32), ALU.subtract)\
                        .then_inc(s["w1_lo_ready"], 1)
                    dve.wait_ge(s["exT_hi_ready"], js.count(1, 1))
                    dve.tensor_tensor(exT_lo[q], (ps_t, ps_u)[q][:, 0:TT], exT_hi[q].bitcast(F32), ALU.subtract)\
                        .then_inc(s["exT_ready"], 1)

                tile_loop(dve, None, layer, ahead=second_parts, behind=result, peel=4)

            def combine(b, layer):
                q = b % 4
                dve.wait_ge(s["wtok_ready"], layer + 1)
                dve.wait_ge(s[f"back_loaded{q}"], 32 * (layer * B // 4 + b // 4 + 1))
                for k in range(2):
                    for j in range(TPS):
                        at = b * TPS + j
                        link.mark(dve.scalar_tensor_tensor(out=X[:, at, :], in0=yb[q][k][:, j, :], scalar=wtok[:, k, at:at + 1],
                                                           in1=X[:, at, :], op0=ALU.mult, op1=ALU.add))
                    link.sync()
                dve.sem_inc(s["combined"], 1)

            experts(0)

            def scan_stats(n):
                for q in range(2):
                    for j in range(TPS):
                        link.mark(dve.bn_stats(gstat[:, q, j, :], X[:, tile_at(Turn(q, n), j), :]))
                link.sync()
                apart(dve)
                for q in range(2):
                    for j in range(TPS):
                        link.mark(dve.bn_aggr(gmv[n % 2][:, q, j, :], gstat[:, q, j, :]))
                link.sync()
                dve.sem_inc(s["gmv_ready"], 1)

            def scan_norm(t):
                q, gm, g = t.par, gmv[t.k // 2 % 2], gr[t.k // 2 % 2]
                dve.wait_ge(s["grs_ready"], t.half(1, 1))
                if started(v := t.count(1, -1)):
                    dve.wait_ge(s["gt_mm"], v)
                for j in range(TPS):
                    link.mark(dve.tensor_scalar(xh[q][:, j, :], X[:, tile_at(t, j), :], gm[:, q, j, 0:1], g[:, 2, q, j:j + 1],
                                                ALU.subtract, ALU.mult))
                link.sync()
                dve.sem_inc(s["gxh_ready"], 1)

            def scan_scan(t):
                dve.wait_ge(s["gdt_ready"], t.half(1, 1))
                link(dve.tensor_scalar(am, dtm, -1.0, 1.0, ALU.mult, ALU.add))
                dve.wait_ge(s["gut_ready"], t.half(1, 1))
                link(dve.tensor_tensor(bm, dtm, ut, ALU.mult))
                link(dve.tensor_tensor_scan(hm, am, bm, 0.0, ALU.mult, ALU.add))
                dve.wait_ge(s["gsg_ready"], t.half(1, 1))
                if started(v := t.count()):
                    dve.wait_ge(s["gout_mm"], v)
                dve.tensor_tensor(ym, hm, sg, ALU.mult).then_inc(s["gy_ready"], 1)

            def scan_out(t):
                dve.wait_ge(s["gout_mm"], t.count(1, 1))
                dve.wait_ge(s["gbias_ready"], t.count(1, 1))
                dve.tensor_tensor(X[:, tiles(t), :], (ps_o, ps_h)[t.par][:, :].rearrange("p (j d) -> p j d", j=TPS),
                                  X[:, tiles(t), :], ALU.add).then_inc(s["scanned"], 1)

            link(dve.tensor_copy(cadd[:, :, 0], C("ebase")))
            for b in range(2):
                combine(b, 0)
            dve.wait_ge(s["pay_set"], 4)
            scan_stats(0)
            for p in range(B // 2 + 1):
                t0, t1, r = Turn(2 * p), Turn(2 * p + 1), Turn(2 * p - 2)
                if p:
                    for x in (r, r.at(1)):
                        route_norm(x, x.at(B))
                if p < B // 2:
                    scan_norm(t0)
                    scan_norm(t1)
                if p < B // 2 - 1:
                    combine(2 * p + 2, 0)
                    combine(2 * p + 3, 0)
                    if started(v := p):
                        dve.wait_ge(s["gc_ready"], v)
                    scan_stats(p + 1)
                if p:
                    route_choose(r, r.at(B), 2)
                if p < B // 2:
                    scan_scan(t0)
                if p:
                    route_slots(r, r.at(B), 2)
                if p < B // 2:
                    scan_out(t0)
                    scan_out(t1)
                    dve.wait_ge(s["scanned"], 2 * p + 2)
                    for t in (t0, t1):
                        route_stats(t, t.at(B))
            experts(1)
            for b in range(B):
                q = b % 4
                dve.wait_ge(s["first_added"], b + 1)
                dve.wait_ge(s[f"back_loaded{q}"], 32 * (B // 4 + b // 4 + 1))
                for j in range(TPS):
                    at = b * TPS + j
                    link.mark(dve.scalar_tensor_tensor(out=X[:, at, :], in0=yb[q][1][:, j, :], scalar=wtok[:, 1, at:at + 1],
                                                       in1=X[:, at, :], op0=ALU.mult, op1=ALU.add))
                link.sync()
                dve.sem_inc(s["combined"], 1)


def kernel(**inputs):
    import numpy as np
    import concourse.bacc as _bacc
    from concourse import mybir as _mybir
    from concourse.bass_utils import run_bass_kernel_spmd as _run

    a = {k: np.asarray(v) for k, v in inputs.items()}
    A, G, M = "L0_attn_a_", "L0_attn_b_", "L0_ffn_"

    def chunks(w, n):
        return w.reshape(n, P, -1).transpose(1, 0, 2).reshape(P, -1)

    def pack(parts, widths, height):
        assert [p.shape for p in parts.values()] == [(height, w) for w in widths.values()] and list(parts) == list(widths)
        return np.ascontiguousarray(np.concatenate(list(parts.values()), axis=1))

    hh = H * HD
    wqkv, bqkv = a[A + "w_qkv"], a[A + "b_qkv"]
    b_pot = np.zeros((P, 1), np.float32)
    b_pot[0:2, 0] = a[A + "b_pot"]
    one = lambda v: v.reshape(P, 1)
    col = lambda v: v.reshape(-1, P).T
    cols = pack(dict(
        w_pot=a[A + "w_pot"], g1=one(a[A + "ln1_g"]), b1=one(a[A + "ln1_b"]), g2=one(a[A + "ln2_g"]), b2=one(a[A + "ln2_b"]),
        g3=one(a[A + "ln3_g"]), b3=one(a[A + "ln3_b"]), bq=col(bqkv[0:hh]), bk=col(bqkv[hh:2 * hh]), bff1=col(a[A + "b_ff1"]),
        norm_w=one(a[G + "norm_w"]), b_uz=one(a[G + "b_in"][0:2 * S]), b_g=one(np.tile(a[G + "b_in"][2 * S:], 2)),
        b_x=one(np.tile(a[G + "b_x"], 2)), b_dt=one(np.tile(a[G + "b_dt"], 2)), b_pot=b_pot), COLS_W, P)
    rows = pack(dict(bk=bqkv[None, hh:2 * hh], bv=bqkv[None, 2 * hh:], b_out=a[A + "b_out"][None], b_ff2=a[A + "b_ff2"][None],
                     b_outb=a[G + "b_out"][None], br=a[M + "br"][None]), ROWS_W, 1)
    wts = pack(dict(q=wqkv[:, 0:hh], k=wqkv[:, hh:2 * hh], v=wqkv[:, 2 * hh:], w_out=chunks(a[A + "w_out"], PAIRS), ff1=a[A + "w_ff1"],
                    ff2=chunks(a[A + "w_ff2"], FC), w_in=a[G + "W_in"], w_xdt=np.concatenate([a[G + "W_x"], a[G + "W_dt"]]),
                    w_outb=np.tile(a[G + "W_out"], (2, 1)), wr=a[M + "Wr"]), WTS_W, P)
    wbk = np.concatenate([a[A + "w_bk"], a[A + "b_bk"][None]])
    experts = np.stack([pack(dict(w1=a[M + "W1"][e], w2=chunks(a[M + "W2"][e], FC), b1=col(a[M + "b1"][e])), EXP_W, P)
                        for e in range(E_N)])
    f32 = np.float32
    k, e = np.arange(P), np.arange(E_N)
    every = lambda v: np.broadcast_to(np.asarray(v, f32), (P, len(v)))
    consts = pack(dict(ident=np.eye(P, dtype=f32), ones=np.ones((P, P), f32), before=(k[:, None] < k).astype(f32),
                       mask=np.where(k[:, None] <= k, f32(ETA), f32(0)), rev=every(E_N - e), ebase=every(e * CAP),
                       kthr=every(np.arange(16) * TT), jj=every(np.arange(MAX_TILES))), CONST_W, P)
    token = (np.arange(B)[None, :, None] * N + k[:, None, None] * TPS + np.arange(TPS)[None, None, :]).reshape(P, NT)
    ids = np.stack([token, token + B * N], axis=-1).astype(np.int32)
    tail = np.zeros((P, ROW), np.int32)
    tail[:, D] = NOWHERE
    arrays = dict(x_in=np.ascontiguousarray(a[A + "x"].reshape(B, P, TPS, D)), consts=consts, ids_in=ids, tail_in=tail, cols_in=cols,
                  rows_in=rows, wts_in=wts, wbk_in=wbk, experts_in=experts, eb2_in=a[M + "b2"])
    nc = _bacc.Bacc("TRN2", target_bir_lowering=False, num_devices=1)
    args = {n: nc.dram_tensor(n, v.shape, _mybir.dt.from_np(v.dtype), kind="ExternalInput").ap() for n, v in arrays.items()}
    out = nc.dram_tensor("out", (B, P, TPS, D), F32, kind="ExternalOutput").ap()
    hybrid_kernel(nc, **args, out=out)
    r = _run(nc, [arrays], core_ids=[0])
    return r.results[0]["out"].reshape(B, N, D)
```
